# Optimizing a Trainium2 kernel written in Bass

```python
import numpy as np
import jax
import jax.numpy as jnp

def _softmax(x, axis=-1):
    return jax.nn.softmax(x, axis=axis)

def _gelu(x):
    return jax.nn.gelu(x, approximate=True)

def _silu(x):
    return jax.nn.silu(x)

def _sigmoid(x):
    return jax.nn.sigmoid(x)

def _layernorm(x, axis=-1, eps=1e-05):
    m = jnp.mean(x, axis=axis, keepdims=True)
    v = jnp.var(x, axis=axis, keepdims=True)
    return (x - m) / jnp.sqrt(v + eps)

def _scatter_add(tgt, idx, src, axis=0):
    return tgt.at[idx].add(src)

def _segment_sum(src, seg, n):
    return jax.ops.segment_sum(src, seg, n)
kernel_name = 'mk_seq_postln_d2_jaxref_r8_a3673e'

def setup_inputs(seed: int=0):
    np.random.seed(seed)
    _w = jnp.asarray

    def _L0_attn_setup():
        import jax, jax.numpy as jnp
        import numpy as np
        NUM_HEADS = 32
        NUM_KV_HEADS = 8
        HEAD_DIM = 128
        key = jax.random.key(seed)
        ks = jax.random.split(key, 5)
        B, S, H = (2, 256, 512)
        Dq = NUM_HEADS * HEAD_DIM
        Dkv = NUM_KV_HEADS * HEAD_DIM
        return {'hidden_states': jax.random.normal(ks[0], (B, S, H), jnp.float32), 'w_q': jax.random.normal(ks[1], (H, Dq), jnp.float32) * 0.02, 'w_k': jax.random.normal(ks[2], (H, Dkv), jnp.float32) * 0.02, 'w_v': jax.random.normal(ks[3], (H, Dkv), jnp.float32) * 0.02, 'w_o': jax.random.normal(ks[4], (Dq, H), jnp.float32) * 0.02}
    _L0_attn_in = _L0_attn_setup()

    def _L0_ffn_setup():
        import jax, jax.numpy as jnp
        import numpy as np
        H = 512
        I = 1376
        CS = 8
        CB = 8192

        def _dequant(codebook, idx):
            return codebook[idx].reshape(idx.shape[0], -1)
        key = jax.random.key(seed)
        k0, k1, k2, k3, k4 = jax.random.split(key, 5)
        x = jax.random.normal(k0, (4, 256, H), dtype=jnp.float32)
        codebook = jax.random.normal(k1, (CB, CS), dtype=jnp.float32)
        idx_gate = jax.random.randint(k2, (I, H // CS), 0, CB, dtype=jnp.int32)
        idx_up = jax.random.randint(k3, (I, H // CS), 0, CB, dtype=jnp.int32)
        idx_down = jax.random.randint(k4, (H, I // CS), 0, CB, dtype=jnp.int32)
        return {'x': x, 'codebook': codebook, 'idx_gate': idx_gate, 'idx_up': idx_up, 'idx_down': idx_down}
    _L0_ffn_in = _L0_ffn_setup()

    def _L1_attn_setup():
        import jax, jax.numpy as jnp
        import numpy as np
        BATCH, SEQ, HIDDEN = (2, 512, 512)
        HEADS, HEAD_DIM, BLOCK = (32, 128, 32)
        LAYER_IDX, N_LAYERS = (1, 32)
        EPS = 1e-05

        def _decays():
            base = 1.0 / 2.0 ** (8.0 / HEADS)
            exponent = jnp.arange(HEADS, dtype=jnp.float32) + 1.0
            factor = 1.0 - LAYER_IDX / (N_LAYERS - 1 + 1e-05) + 1e-05
            slope = (base ** exponent * factor)[:, None, None]
            r = jnp.arange(BLOCK, dtype=jnp.float32) + 1.0
            q_decay = jnp.exp(-slope * r[:, None])
            k_decay = jnp.exp(-slope * (BLOCK - r)[:, None])
            diff = r[:, None] - r[None, :]
            diag = slope[None] * diff[None, None]
            diag = jnp.where(diag >= 0, -diag, -jnp.inf)
            diag_decay = jnp.exp(diag)
            block_decay = jnp.exp(-slope * BLOCK)
            return (q_decay, k_decay, diag_decay, block_decay)
        key = jax.random.key(seed)
        ks = jax.random.split(key, 5)
        s = 0.02
        return {'hidden_states': jax.random.normal(ks[0], (BATCH, SEQ, HIDDEN), jnp.float32), 'qkv_w': jax.random.normal(ks[1], (3 * HEADS * HEAD_DIM, HIDDEN), jnp.float32) * s, 'out_w': jax.random.normal(ks[2], (HIDDEN, HEADS * HEAD_DIM), jnp.float32) * s, 'gate_w': jax.random.normal(ks[3], (HEADS * HEAD_DIM, HIDDEN), jnp.float32) * s, 'norm_w': jnp.ones((HEADS * HEAD_DIM,), jnp.float32)}
    _L1_attn_in = _L1_attn_setup()

    def _L1_ffn_setup():
        import jax, jax.numpy as jnp
        import numpy as np
        DIM = 512
        HIDDEN = 1376
        B, S = (4, 256)

        def _qlinear(x, w_int, scale):
            w = w_int.astype(x.dtype) * scale
            return jnp.einsum('bsd,hd->bsh', x, w)
        key = jax.random.key(seed)
        k_x, k_g, k_u, k_d = jax.random.split(key, 4)
        x = jax.random.normal(k_x, (B, S, DIM), dtype=jnp.float32)
        w_gate = jax.random.randint(k_g, (HIDDEN, DIM), -127, 128, dtype=jnp.int32)
        w_up = jax.random.randint(k_u, (HIDDEN, DIM), -127, 128, dtype=jnp.int32)
        w_down = jax.random.randint(k_d, (DIM, HIDDEN), -127, 128, dtype=jnp.int32)
        scale_gate = jnp.float32(0.01)
        scale_up = jnp.float32(0.01)
        scale_down = jnp.float32(0.01)
        return {'x': x, 'w_gate': w_gate, 'w_up': w_up, 'w_down': w_down, 'scale_gate': scale_gate, 'scale_up': scale_up, 'scale_down': scale_down}
    _L1_ffn_in = _L1_ffn_setup()
    _d = {'L0_attn_hidden_states': _L0_attn_in['hidden_states'], 'L0_attn_w_q': _L0_attn_in['w_q'], 'L0_attn_w_k': _L0_attn_in['w_k'], 'L0_attn_w_v': _L0_attn_in['w_v'], 'L0_attn_w_o': _L0_attn_in['w_o'], 'L0_ffn_codebook': _L0_ffn_in['codebook'], 'L0_ffn_idx_gate': _L0_ffn_in['idx_gate'], 'L0_ffn_idx_up': _L0_ffn_in['idx_up'], 'L0_ffn_idx_down': _L0_ffn_in['idx_down'], 'L1_attn_qkv_w': _L1_attn_in['qkv_w'], 'L1_attn_out_w': _L1_attn_in['out_w'], 'L1_attn_gate_w': _L1_attn_in['gate_w'], 'L1_attn_norm_w': _L1_attn_in['norm_w'], 'L1_ffn_w_gate': _L1_ffn_in['w_gate'], 'L1_ffn_w_up': _L1_ffn_in['w_up'], 'L1_ffn_w_down': _L1_ffn_in['w_down'], 'L1_ffn_scale_gate': _L1_ffn_in['scale_gate'], 'L1_ffn_scale_up': _L1_ffn_in['scale_up'], 'L1_ffn_scale_down': _L1_ffn_in['scale_down']}
    _x0 = _d['L0_attn_hidden_states']
    _d['L0_attn_hidden_states'] = jax.random.normal(jax.random.fold_in(jax.random.key(seed), 1), (2, 512, 512), dtype=_x0.dtype)
    del _x0
    return _d

def reference(L0_attn_hidden_states, L0_attn_w_q, L0_attn_w_k, L0_attn_w_v, L0_attn_w_o, L0_ffn_codebook, L0_ffn_idx_gate, L0_ffn_idx_up, L0_ffn_idx_down, L1_attn_qkv_w, L1_attn_out_w, L1_attn_gate_w, L1_attn_norm_w, L1_ffn_w_gate, L1_ffn_w_up, L1_ffn_w_down, L1_ffn_scale_gate, L1_ffn_scale_up, L1_ffn_scale_down):

    def _L0_attn_ref(hidden_states, w_q, w_k, w_v, w_o):
        import jax, jax.numpy as jnp
        import numpy as np
        NUM_HEADS = 32
        NUM_KV_HEADS = 8
        HEAD_DIM = 128
        B, S, _ = hidden_states.shape
        Hq, Hkv, D = (NUM_HEADS, NUM_KV_HEADS, HEAD_DIM)
        g = Hq // Hkv
        scale = D ** (-0.5)
        q = (hidden_states @ w_q).reshape(B, S, Hkv, g, D)
        k = (hidden_states @ w_k).reshape(B, S, Hkv, D)
        v = (hidden_states @ w_v).reshape(B, S, Hkv, D)
        scores = jnp.einsum('bqhgd,bkhd->bhgqk', q, k) * scale
        causal = jnp.tril(jnp.ones((S, S), dtype=bool))
        scores = jnp.where(causal, scores, -jnp.inf)
        probs = jax.nn.softmax(scores.astype(jnp.float32), axis=-1).astype(q.dtype)
        attn = jnp.einsum('bhgqk,bkhd->bqhgd', probs, v)
        attn = attn.reshape(B, S, Hq * D)
        return attn @ w_o

    def _L0_ffn_ref(x, codebook, idx_gate, idx_up, idx_down):
        import jax, jax.numpy as jnp
        import numpy as np
        H = 512
        I = 1376
        CS = 8
        CB = 8192

        def _dequant(codebook, idx):
            return codebook[idx].reshape(idx.shape[0], -1)
        Wg = _dequant(codebook, idx_gate)
        Wu = _dequant(codebook, idx_up)
        Wd = _dequant(codebook, idx_down)
        g = jnp.einsum('bsh,ih->bsi', x, Wg)
        u = jnp.einsum('bsh,ih->bsi', x, Wu)
        h = jax.nn.silu(g) * u
        return jnp.einsum('bsi,hi->bsh', h, Wd)

    def _L1_attn_ref(hidden_states, qkv_w, out_w, gate_w, norm_w):
        import jax, jax.numpy as jnp
        import numpy as np
        BATCH, SEQ, HIDDEN = (2, 512, 512)
        HEADS, HEAD_DIM, BLOCK = (32, 128, 32)
        LAYER_IDX, N_LAYERS = (1, 32)
        EPS = 1e-05

        def _decays():
            base = 1.0 / 2.0 ** (8.0 / HEADS)
            exponent = jnp.arange(HEADS, dtype=jnp.float32) + 1.0
            factor = 1.0 - LAYER_IDX / (N_LAYERS - 1 + 1e-05) + 1e-05
            slope = (base ** exponent * factor)[:, None, None]
            r = jnp.arange(BLOCK, dtype=jnp.float32) + 1.0
            q_decay = jnp.exp(-slope * r[:, None])
            k_decay = jnp.exp(-slope * (BLOCK - r)[:, None])
            diff = r[:, None] - r[None, :]
            diag = slope[None] * diff[None, None]
            diag = jnp.where(diag >= 0, -diag, -jnp.inf)
            diag_decay = jnp.exp(diag)
            block_decay = jnp.exp(-slope * BLOCK)
            return (q_decay, k_decay, diag_decay, block_decay)
        b, s, _ = hidden_states.shape
        h, d, bs = (HEADS, HEAD_DIM, BLOCK)
        nb = s // bs
        q_decay, k_decay, diag_decay, block_decay = _decays()
        qkv = jax.nn.silu(hidden_states @ qkv_w.T)
        qkv = qkv.reshape(b, s, h, 3, d)
        q = jnp.moveaxis(qkv[:, :, :, 0], 2, 1)
        k = jnp.moveaxis(qkv[:, :, :, 1], 2, 1)
        v = jnp.moveaxis(qkv[:, :, :, 2], 2, 1)

        def to_blocks(x):
            return jnp.moveaxis(x.reshape(b, h, nb, bs, d), 2, 0)
        qb, kb, vb = (to_blocks(q), to_blocks(k), to_blocks(v))

        def step(kv, blk):
            cq, ck, cv = blk
            scores = jnp.einsum('bhnd,bhmd->bhnm', cq, ck) * diag_decay
            intra = jnp.einsum('bhnm,bhmd->bhnd', scores, cv)
            inter = jnp.einsum('bhnd,bhde->bhne', cq * q_decay, kv)
            kv_next = kv * block_decay + jnp.einsum('bhnd,bhne->bhde', ck * k_decay, cv)
            return (kv_next, intra + inter)
        kv0 = jnp.zeros((b, h, d, d), hidden_states.dtype)
        _, out_blocks = jax.lax.scan(step, kv0, (qb, kb, vb))
        attn = jnp.moveaxis(out_blocks, 0, 2)
        attn = attn.reshape(b, h, s, d).transpose(0, 2, 1, 3).reshape(b, s, h * d)
        xf = attn.astype(jnp.float32)
        xf = xf * jax.lax.rsqrt(jnp.mean(xf * xf, axis=-1, keepdims=True) + EPS)
        normed = norm_w * xf.astype(attn.dtype)
        gate = jax.nn.sigmoid(hidden_states @ gate_w.T)
        return gate * normed @ out_w.T

    def _L1_ffn_ref(x, w_gate, w_up, w_down, scale_gate, scale_up, scale_down):
        import jax, jax.numpy as jnp
        import numpy as np
        DIM = 512
        HIDDEN = 1376
        B, S = (4, 256)

        def _qlinear(x, w_int, scale):
            w = w_int.astype(x.dtype) * scale
            return jnp.einsum('bsd,hd->bsh', x, w)
        x_gate = _qlinear(x, w_gate, scale_gate)
        x_up = _qlinear(x, w_up, scale_up)
        x_mid = jax.nn.silu(x_gate) * x_up
        x_out = _qlinear(x_mid, w_down, scale_down)
        return x_out
    x = L0_attn_hidden_states
    x = _layernorm(x + _L0_attn_ref(x, L0_attn_w_q, L0_attn_w_k, L0_attn_w_v, L0_attn_w_o), axis=-1)
    x = _layernorm(x + _L0_ffn_ref(x, L0_ffn_codebook, L0_ffn_idx_gate, L0_ffn_idx_up, L0_ffn_idx_down), axis=-1)
    x = _layernorm(x + _L1_attn_ref(x, L1_attn_qkv_w, L1_attn_out_w, L1_attn_gate_w, L1_attn_norm_w), axis=-1)
    x = _layernorm(x + _L1_ffn_ref(x, L1_ffn_w_gate, L1_ffn_w_up, L1_ffn_w_down, L1_ffn_scale_gate, L1_ffn_scale_up, L1_ffn_scale_down), axis=-1)
    return x

_drawn_inputs = setup_inputs


def setup_inputs(seed=0):
    import zlib

    import numpy as np

    out = dict(_drawn_inputs(seed))
    spreads = {'L1_attn_norm_w': (1.0, 0.2)}
    factors = {}
    for name, (base, spread) in spreads.items():
        noise = np.random.default_rng([zlib.crc32(name.encode()), seed]).standard_normal(out[name].shape)
        drawn = base * np.exp(spread * noise) if base else spread * noise
        out[name] = jnp.asarray(drawn.astype(out[name].dtype))
    for name, factor in factors.items():
        out[name] = (out[name] * factor).astype(out[name].dtype)
    return out
```

```python
from contextlib import ExitStack

import concourse.bass as bass
from concourse import mybir

F32 = mybir.dt.float32
F32R = mybir.dt.float32r
I32 = mybir.dt.int32
U32 = mybir.dt.uint32
ALU = mybir.AluOpType
ACT = mybir.ActivationFunctionType

P = 128
TOK = 1024
SEQ = 512
TILES = TOK // P
D = 512
KB = D // P
HEADS = 32
KV_HEADS = 8
GROUP = HEADS // KV_HEADS
FF = 1376
FT = (FF + P - 1) // P
FLAST = FF - (FT - 1) * P
CODE = 8
NEG = -3.0e38
EPS = 1e-5
SCALE = float(P) ** -0.5
QT = SEQ // P
P_AT = [0, 128, 384, 768]
P_COLS = 1280
PIECES = [(0, [(0, q) for q in range(4)]),
          (512, [(1, q) for q in range(1, 4)]),
          (896, [(2, 2), (2, 3), (3, 3)])]
PT_AT = [0, 512, 896, 1152]
S_AT = [(2, 256), (2, 0), (1, 0), (0, 0)]


def attention_plan(first, last):
    plan = [("K", 0), ("K", 1), ("Q", 0)]
    if not first:
        plan += [("T", 7, 0), ("T", 7, 1), ("PV", 7, 0), ("T", 7, 2), ("PV", 7, 1), ("PV", 7, 2)]
    plan += [("V", 0), ("V", 1)]
    old = [] if first else [[("O", 1, t)] for t in range(4)]
    fills = {s: [("Q", s + 1)] + (old[s] if s < len(old) else []) for s in range(7)}
    fills[5] += [("O", 0, 0), ("O", 0, 1)]
    fills[6] += [("O", 0, 2)]
    fills[7] = [("O", 0, 3)]
    for s in range(8):
        f = fills[s]
        plan.append(("S", s))
        plan += f[:1]
        if s:
            plan += [("T", s - 1, 0), ("T", s - 1, 1)]
        plan.append(("N", s))
        plan += f[1:2]
        if s:
            plan += [("PV", s - 1, 0), ("T", s - 1, 2), ("PV", s - 1, 1)]
        plan += f[2:]
        if s:
            plan += [("PV", s - 1, 2)]
        if s == 4:
            plan.append(("W", "o"))
        if not last and s in (1, 2, 7):
            plan.append(("W", {1: "k", 2: "v", 7: "q"}[s]))
    return plan


def attention_tail():
    return [("T", 7, 0), ("T", 7, 1), ("PV", 7, 0), ("T", 7, 2), ("PV", 7, 1), ("PV", 7, 2)] \
        + [("O", 1, t) for t in range(4)]


class Counts:

    def __init__(self):
        plan = attention_plan(False, False)
        self.per = {k: self.tally(plan, k) for k in ("unit", "T", "PV", "S")}
        self.first = {k: self.tally(attention_plan(True, False), k) for k in self.per}

    @staticmethod
    def kind(e):
        return "unit" if e[0] in "KQVO" else e[0]

    def tally(self, plan, kind):
        return sum(1 for e in plan if self.kind(e) == kind and (kind != "PV" or e[2] == 2))

    def base(self, g, kind):
        if isinstance(g, int) and g == 0:
            return 0
        return g * self.per[kind] + (self.first[kind] - self.per[kind])


def build(nc, x, w_q, w_k, w_v, w_o, codebook, idx, qkv_w, out_w, gate_w, norm_w, decay,
          wf_gate, wf_up, wf_down, scales, out, wdram, phases="ABCD"):
    ctx = ExitStack()
    with ctx:
        def sb(name, shape, dt=F32):
            return ctx.enter_context(nc.sbuf_tensor(name, shape, dt))

        def sem(name):
            return ctx.enter_context(nc.semaphore(name))

        acc = sb("acc", [P, TILES, D])
        x_hi = sb("x_hi", [P, KB, TOK], F32R)
        x_lo = sb("x_lo", [P, KB, TOK], F32R)
        identity = sb("identity", [P, P])
        mask = sb("mask", [P, SEQ])
        eps = sb("eps", [P, 1])
        pace = sb("pace", [1, 1])
        pool_pace = sb("pool_pace", [1, 3])
        scale_sb = sb("scale_sb", [P, 3])
        codes_at = sb("codes_at", [P, 3, D // CODE], U32)
        gathered_rows = sb("gathered_rows", [P, 3, D])
        stats = sb("stats", [P, TILES, 6])
        mean_var = sb("mean_var", [P, TILES, 2])
        deviation = sb("deviation", [P, TILES])
        rstd = sb("rstd", [P, TILES])
        banks = [ctx.enter_context(nc.psum_tensor(f"bank{i}", [P, 512], F32)) for i in range(8)]

        def arenas(name, r_cols, f_cols):
            stack = ExitStack()

            def cutter(arena, total):
                at = [0]

                def cut(*shape):
                    n = 1
                    for s in shape:
                        n *= s
                    assert at[0] + n <= total, (name, at[0] + n, total)
                    view = arena[:, at[0]:at[0] + n]
                    at[0] += n
                    if len(shape) == 2:
                        view = view.rearrange("p (a b) -> p a b", a=shape[0])
                    elif len(shape) == 3:
                        view = view.rearrange("p (a b c) -> p a b c", a=shape[0], b=shape[1])
                    return view
                return cut
            rounded = stack.enter_context(nc.sbuf_tensor(f"rounded_{name}", [P, r_cols], F32R))
            plain = stack.enter_context(nc.sbuf_tensor(f"plain_{name}", [P, f_cols], F32))
            return cutter(rounded, r_cols), cutter(plain, f_cols), stack.close

        consts_ready = sem("consts_ready")
        may_load = sem("may_load")
        x_loaded = sem("x_loaded")
        block = ctx.enter_context(nc.Block())

        engines = {k: [] for k in ("sync", "gpsimd", "scalar", "vector", "tensor")}

        def norm_stage(n, ready_waits, normalise, turn, store=None):
            stat = sem(f"stat{n}")
            dev = sem(f"dev{n}")
            rs = sem(f"rs{n}")
            normed = sem(f"normed{n}")
            turned = sem(f"turned{n}")
            hi = sem(f"x_hi_done{n}")
            lo = sem(f"x_ready{n}")

            def vector(e):
                ready_waits(e)
                if normalise:
                    for i in range(TILES):
                        e.bn_stats(stats[:, i, :], acc[:, i, :]).then_inc(stat, 1)
                    for i in range(TILES):
                        e.wait_ge(stat, i + 1)
                        e.bn_aggr(mean_var[:, i, :], stats[:, i, :]).then_inc(stat, 1)
                    e.wait_ge(dev, 1)
                    e.reciprocal(rstd[:], deviation[:]).then_inc(rs, 1)
                    e.wait_ge(rs, 1)
                    for i in range(TILES):
                        e.tensor_scalar(acc[:, i, :], acc[:, i, :], mean_var[:, i, 0:1], rstd[:, i:i + 1],
                                        ALU.subtract, ALU.mult).then_inc(normed, 1)
                if turn:
                    for i in range(TILES):
                        e.wait_ge(hi, i + 1)
                        at = slice(i * P, (i + 1) * P)
                        e.tensor_tensor(x_lo[:, :, at], banks[i % 2][:].rearrange("p (a b) -> p a b", a=KB),
                                        x_hi[:, :, at].bitcast(F32), ALU.subtract).then_inc(lo, 1)

            def scalar(e):
                if normalise:
                    e.wait_ge(stat, 2 * TILES)
                    e.activation(deviation[:], mean_var[:, :, 1], ACT.Sqrt, bias=eps[:]).then_inc(dev, 1)
                if turn:
                    for i in range(TILES):
                        e.wait_ge(turned, i + 1)
                        at = slice(i * P, (i + 1) * P)
                        e.activation(x_hi[:, :, at], banks[i % 2][:].rearrange("p (a b) -> p a b", a=KB),
                                     ACT.Copy).then_inc(hi, 1)

            def tensor(e):
                if not turn:
                    return
                if not normalise:
                    e.wait_ge(consts_ready, 1)
                    e.wait_ge(x_loaded, 16)
                for i in range(TILES):
                    if normalise:
                        e.wait_ge(normed, i + 1)
                    if i >= 2:
                        e.wait_ge(lo, i - 1)
                    for c in range(KB):
                        t = e.transpose(banks[i % 2][:, c * P:(c + 1) * P], acc[:, i, c * P:(c + 1) * P],
                                        identity[:])
                    t.then_inc(turned, 1)

            def sync(e):
                if store is not None:
                    stored = sem("stored")
                    for i in range(TILES):
                        e.wait_ge(normed, i + 1)
                        e.dma_start(store[i * P:(i + 1) * P, :], acc[:, i, :]).then_inc(stored, 16)
                    e.wait_ge(stored, 16 * TILES)

            engines["vector"].append(vector)
            engines["scalar"].append(scalar)
            engines["tensor"].append(tensor)
            engines["sync"].append(sync)
            return lo

        def start_sync(e):
            e.dma_start(acc[:], x.rearrange("(t p) d -> p t d", p=P)).then_inc(x_loaded, 16)

        const_step = sem("const_step")

        def start_gpsimd(e):
            e.memset(identity[:], 0.0).then_inc(const_step, 1)
            e.memset(mask[:], 0.0).then_inc(const_step, 1)
            e.memset(eps[:], EPS).then_inc(const_step, 1)
            e.wait_ge(const_step, 3)
            e.affine_select(out=identity[:], in_=identity[:], compare_op=ALU.not_equal, fill=1.0, base=0,
                            pattern=[[-1, P]], channel_multiplier=1).then_inc(const_step, 1)
            e.affine_select(out=mask[:, SEQ - P:SEQ], in_=mask[:, SEQ - P:SEQ], compare_op=ALU.is_ge, fill=NEG,
                            base=0, pattern=[[-1, P]], channel_multiplier=1).then_inc(const_step, 1)
            e.wait_ge(const_step, 5)
            e.memset(stats[:, 0, 0:1], 0.0).then_inc(consts_ready, 1)

        engines["sync"].append(start_sync)
        engines["gpsimd"].append(start_gpsimd)

        x0_ready = norm_stage(0, lambda e: None, False, True)

        def three(e, out_ap, l_hi, l_lo, r_hi, r_lo, start, stop):
            e.matmul(out_ap, l_hi, r_hi, start=start, stop=False)
            e.matmul(out_ap, l_hi, r_lo, start=False, stop=False)
            return e.matmul(out_ap, l_lo, r_hi, start=False, stop=stop)

        if "A" in phases:
            cut_r, cut_f, close = arenas("a", 27136, 7712)
            W_SHAPE = {"k": (KB, P), "v": (KB, P), "q": (KB, GROUP * P), "o": (GROUP, D)}
            stage = {k: cut_f(*s) for k, s in W_SHAPE.items()}
            w_hi = {k: cut_r(*s) for k, s in W_SHAPE.items()}
            w_lo = {k: cut_r(*s) for k, s in W_SHAPE.items()}
            k_hi, k_lo = cut_r(TOK), cut_r(TOK)
            v_hi, v_lo = cut_r(TILES, P), cut_r(TILES, P)
            q_hi, q_lo = cut_r(2, SEQ), cut_r(2, SEQ)
            pt_hi, pt_lo = cut_r(P_COLS), cut_r(P_COLS)
            at_hi, at_lo = cut_r(2, GROUP, SEQ), cut_r(2, GROUP, SEQ)
            probs = cut_f(2, P_COLS)
            row_max, neg_max, row_sum, row_inv = (cut_f(2, QT) for _ in range(4))
            close()
            w_src = {
                "k": lambda g: w_k.rearrange("(c p) n -> p c n", p=P)[:, :, bass.ts(g, P)],
                "v": lambda g: w_v.rearrange("(c p) n -> p c n", p=P)[:, :, bass.ts(g, P)],
                "q": lambda g: w_q.rearrange("(c p) n -> p c n", p=P)[:, :, bass.ts(g, GROUP * P)],
                "o": lambda g: w_o.rearrange("(c p) n -> p c n", p=P)[:, bass.ts(g, GROUP), :],
            }
            cnt = Counts()
            w_loaded = {k: sem(f"w{k}_loaded") for k in "kvqo"}
            w_hi_done = {k: sem(f"w{k}_hi_done") for k in "kvqo"}
            w_ready = {k: sem(f"w{k}_ready") for k in "kvqo"}
            unit_made, unit_hi, unit_out = sem("unit_made"), sem("unit_hi"), sem("unit_out")
            scores_made, masked, neg_done = sem("scores_made"), sem("masked"), sem("neg_done")
            exp_done, inv_done, probs_ready = sem("exp_done"), sem("inv_done"), sem("probs_ready")
            t_made, t_hi, t_out = sem("t_made"), sem("t_hi"), sem("t_out")
            pv_made, pv_hi, pv_out = sem("pv_made"), sem("pv_hi"), sem("pv_out")
            S_BANK, T_BANK, O_BANK, U_BANK = 0, 3, 5, 6

            def groups(e, body):
                body(0, True, False)
                with e.Fori(1, KV_HEADS - 1) as g:
                    body(g, False, False)
                body(KV_HEADS - 1, False, True)

            def where(g, first, last, tail=False):
                plan = attention_tail() if tail else attention_plan(first, last)
                base = {k: cnt.base(g, k) for k in ("unit", "T", "PV", "S")}
                seen = {k: 0 for k in base}
                last_q = 0
                for n, e in enumerate(plan):
                    k = cnt.kind(e)
                    if k in seen and (k != "PV" or e[2] == 2):
                        seen[k] += 1
                    yield e, seen, base, plan, n

            def unit_number(plan, base, what):
                n = 0
                for e in plan:
                    if cnt.kind(e) == "unit":
                        n += 1
                    if e == what:
                        return base["unit"] + n
                raise KeyError(what)

            def a_sync(e):
                def load(k, g):
                    e.dma_start(stage[k], w_src[k](g)).then_inc(w_loaded[k], 16)
                for k in "kvqo":
                    load(k, 0)

                def body(g, first, last):
                    if last:
                        return
                    for k in "kvqo":
                        e.wait_ge(w_ready[k], g + 1)
                        load(k, g + 1)
                body(0, True, False)
                with e.Fori(1, KV_HEADS - 1) as g:
                    body(g, False, False)

            def a_tensor(e):
                def product(kind, bank, item, waits=None):
                    if kind == "K":
                        r = slice(item[1] * SEQ, (item[1] + 1) * SEQ)
                        for c in range(KB):
                            m = three(e, bank[:], w_hi["k"][:, c, :], w_lo["k"][:, c, :], x_hi[:, c, r],
                                      x_lo[:, c, r], c == 0, c == KB - 1)
                    elif kind == "Q":
                        b, h = divmod(item[1], GROUP)
                        r = slice(b * SEQ, (b + 1) * SEQ)
                        for c in range(KB):
                            m = three(e, bank[:], w_hi["q"][:, c, h * P:(h + 1) * P],
                                      w_lo["q"][:, c, h * P:(h + 1) * P], x_hi[:, c, r], x_lo[:, c, r],
                                      c == 0, c == KB - 1)
                    elif kind == "V":
                        for i in range(4):
                            t = item[1] * 4 + i
                            r = slice(t * P, (t + 1) * P)
                            for c in range(KB):
                                m = three(e, bank[:, i * P:(i + 1) * P], x_hi[:, c, r], x_lo[:, c, r],
                                          w_hi["v"][:, c, :], w_lo["v"][:, c, :], c == 0, c == KB - 1)
                    else:
                        b, t = item[1:]
                        r = slice(t * P, (t + 1) * P)
                        for h in range(GROUP):
                            m = three(e, bank[:], at_hi[:, b, h, r], at_lo[:, b, h, r], w_hi["o"][:, h, :],
                                      w_lo["o"][:, h, :], h == 0, h == GROUP - 1)
                    return m

                def run(g, first, last, tail=False):
                    for item, seen, base, plan, n in where(g, first, last, tail):
                        k = item[0]
                        if k in "KQVO" and cnt.kind(item) == "unit":
                            u = seen["unit"]
                            if not (first and u <= 2):
                                e.wait_ge(unit_out, base["unit"] + u - 2)
                            if k == "K" and item[1] == 0:
                                e.wait_ge(w_ready["k"], g + 1)
                            if k == "V" and item[1] == 0:
                                e.wait_ge(w_ready["v"], g + 1)
                            if k == "Q" and item[1] == 0:
                                e.wait_ge(w_ready["q"], g + 1)
                            if k == "O" and item[1] == 0 and item[2] == 0:
                                e.wait_ge(w_ready["o"], g + 1)
                                e.wait_ge(pv_out, g * 8 + 4)
                            if k == "O" and item[1] == 1 and item[2] == 0:
                                e.wait_ge(pv_out, g * 8)
                            product(k, banks[U_BANK + (u - 1) % 2], item).then_inc(unit_made, 1)
                        elif k == "S":
                            s = item[1]
                            b = s // GROUP
                            e.wait_ge(unit_out, unit_number(plan, base, ("Q", s)))
                            if not (first and s == 0):
                                e.wait_ge(masked, (g * 8 + s) * QT)
                            for q in range(QT):
                                bank, at = S_AT[q]
                                r = slice(q * P, (q + 1) * P)
                                ks = slice(b * SEQ, b * SEQ + (q + 1) * P)
                                m = three(e, banks[S_BANK + bank][:, at:at + (q + 1) * P], q_hi[:, s % 2, r],
                                          q_lo[:, s % 2, r], k_hi[:, ks], k_lo[:, ks], True, True)
                            m.then_inc(scores_made, 1)
                        elif k == "T":
                            s, piece = item[1:]
                            G = g - 1 if s == 7 and not isinstance(g, int) else (g - 1 if s == 7 else g)
                            if piece == 0:
                                e.wait_ge(probs_ready, G * 8 + s + 1)
                            tn = (G * 8 + s) * 3 + piece
                            par = (s + piece) % 2
                            if not (isinstance(G, int) and G == 0 and s * 3 + piece < 2):
                                e.wait_ge(t_out, tn - 1)
                            for i, (j, q) in enumerate(PIECES[piece][1]):
                                m = e.transpose(banks[T_BANK + (3 * s + piece) % 2][:, i * P:(i + 1) * P],
                                                probs[:, s % 2, P_AT[q] + j * P:P_AT[q] + (j + 1) * P], identity[:])
                            m.then_inc(t_made, 1)
                        elif k == "PV":
                            s, piece = item[1:]
                            G = g - 1 if s == 7 else g
                            b = s // GROUP
                            e.wait_ge(t_out, (G * 8 + s) * 3 + piece + 1)
                            if piece == 0:
                                if s == 0:
                                    e.wait_ge(unit_out, unit_number(plan, base, ("V", 1)))
                                if not (isinstance(G, int) and G == 0 and s == 0):
                                    e.wait_ge(pv_out, G * 8 + s)
                            for j in {0: [0], 1: [1], 2: [2, 3]}[piece]:
                                t = b * 4 + j
                                cols = slice(PT_AT[j], PT_AT[j] + (QT - j) * P)
                                m = three(e, banks[O_BANK][:, j * P:SEQ], v_hi[:, t, :], v_lo[:, t, :],
                                          pt_hi[:, cols], pt_lo[:, cols], j == 0, j == 3)
                            if piece == 2:
                                m.then_inc(pv_made, 1)

                e.wait_ge(x0_ready, TILES)
                groups(e, run)
                run(KV_HEADS, False, False, True)

            def a_scalar(e):
                def prep(k, g):
                    e.wait_ge(w_loaded[k], (g + 1) * 16)
                    if not (isinstance(g, int) and g == 0):
                        if k == "k":
                            e.wait_ge(unit_made, cnt.base(g - 1, "unit") + 2)
                        if k == "v":
                            e.wait_ge(unit_made, cnt.base(g - 1, "unit") + 5)
                        if k == "q":
                            e.wait_ge(unit_made, cnt.base(g, "unit") - 1)
                        if k == "o":
                            e.wait_ge(unit_made, cnt.base(g, "unit") + 13)
                    e.activation(w_hi[k], stage[k], ACT.Copy).then_inc(w_hi_done[k], 1)

                def run(g, first, last, tail=False):
                    for item, seen, base, plan, n in where(g, first, last, tail):
                        k = item[0]
                        if k in ("K", "Q", "V"):
                            u = base["unit"] + seen["unit"]
                            bank = banks[U_BANK + (seen["unit"] - 1) % 2]
                            e.wait_ge(unit_made, u)
                            if k == "K":
                                r = slice(item[1] * SEQ, (item[1] + 1) * SEQ)
                                if not first:
                                    e.wait_ge(scores_made, g * 8)
                                e.activation(k_hi[:, r], bank[:], ACT.Copy).then_inc(unit_hi, 1)
                            elif k == "Q":
                                s = item[1]
                                if not (first and s < 2):
                                    e.wait_ge(scores_made, g * 8 + s - 1)
                                e.activation(q_hi[:, s % 2, :], bank[:], ACT.Copy, scale=SCALE).then_inc(unit_hi, 1)
                            else:
                                if not first:
                                    e.wait_ge(pv_made, g * 8)
                                r = slice(item[1] * 4, item[1] * 4 + 4)
                                e.activation(v_hi[:, r, :], bank[:].rearrange("p (a b) -> p a b", b=P),
                                             ACT.Copy).then_inc(unit_hi, 1)
                        elif k == "S":
                            s = item[1]
                            n_s = g * 8 + s
                            e.wait_ge(neg_done, n_s + 1)
                            for q in range(QT):
                                c = slice(P_AT[q], P_AT[q] + (q + 1) * P)
                                e.activation(probs[:, s % 2, c], probs[:, s % 2, c], ACT.Exp,
                                             bias=neg_max[:, s % 2, q:q + 1],
                                             accum_out=row_sum[:, s % 2, q:q + 1]).then_inc(exp_done, 1)
                        elif k == "T":
                            s, piece = item[1:]
                            G = g - 1 if s == 7 else g
                            at, blocks = PIECES[piece]
                            w = len(blocks) * P
                            e.wait_ge(t_made, (G * 8 + s) * 3 + piece + 1)
                            if not (isinstance(G, int) and G == 0 and s == 0):
                                e.wait_ge(pv_made, G * 8 + s)
                            e.activation(pt_hi[:, at:at + w], banks[T_BANK + (3 * s + piece) % 2][:, 0:w],
                                         ACT.Copy).then_inc(t_hi, 1)
                        elif k == "PV" and item[2] == 2:
                            s = item[1]
                            G = g - 1 if s == 7 else g
                            b, h = divmod(s, GROUP)
                            e.wait_ge(pv_made, G * 8 + s + 1)
                            if h == 0:
                                if not (isinstance(G, int) and G == 0):
                                    e.wait_ge(unit_made, cnt.base(G, "unit") + (0 if b == 0 else 13))
                            e.activation(at_hi[:, b, h, :], banks[O_BANK][:], ACT.Copy).then_inc(pv_hi, 1)
                        elif k == "W":
                            prep(item[1], g if item[1] == "o" else g + 1)

                for k in "kqv":
                    prep(k, 0)
                groups(e, run)
                run(KV_HEADS, False, False, True)

            def a_vector(e):
                def prep(k, g):
                    e.wait_ge(w_hi_done[k], g + 1)
                    e.tensor_tensor(w_lo[k], stage[k], w_hi[k].bitcast(F32), ALU.subtract).then_inc(w_ready[k], 1)

                def run(g, first, last, tail=False):
                    n_hi = 0
                    for item, seen, base, plan, n in where(g, first, last, tail):
                        k = item[0]
                        if k in ("K", "Q", "V"):
                            n_hi += 1
                            bank = banks[U_BANK + (seen["unit"] - 1) % 2]
                            e.wait_ge(unit_hi, g * 12 + n_hi)
                            if k == "K":
                                r = slice(item[1] * SEQ, (item[1] + 1) * SEQ)
                                e.tensor_tensor(k_lo[:, r], bank[:], k_hi[:, r].bitcast(F32),
                                                ALU.subtract).then_inc(unit_out, 1)
                            elif k == "Q":
                                s = item[1]
                                e.scalar_tensor_tensor(out=q_lo[:, s % 2, :], in0=bank[:], scalar=SCALE,
                                                       in1=q_hi[:, s % 2, :].bitcast(F32), op0=ALU.mult,
                                                       op1=ALU.subtract).then_inc(unit_out, 1)
                            else:
                                r = slice(item[1] * 4, item[1] * 4 + 4)
                                e.tensor_tensor(v_lo[:, r, :], bank[:].rearrange("p (a b) -> p a b", b=P),
                                                v_hi[:, r, :].bitcast(F32), ALU.subtract).then_inc(unit_out, 1)
                        elif k == "O":
                            t = item[1] * 4 + item[2]
                            e.wait_ge(unit_made, base["unit"] + seen["unit"])
                            e.tensor_tensor(acc[:, t, :], acc[:, t, :], banks[U_BANK + (seen["unit"] - 1) % 2][:],
                                            ALU.add).then_inc(unit_out, 1)
                        elif k == "S":
                            s = item[1]
                            n_s = g * 8 + s
                            e.wait_ge(scores_made, n_s + 1)
                            if not (first and s < 2):
                                e.wait_ge(t_made, (n_s - 1) * 3)
                            e.memset(pace[:], 0.0)
                            for q in range(QT):
                                bank, at = S_AT[q]
                                c = slice(P_AT[q], P_AT[q] + (q + 1) * P)
                                e.tensor_tensor_reduce(probs[:, s % 2, c], banks[S_BANK + bank][:, at:at + (q + 1) * P],
                                                       mask[:, SEQ - (q + 1) * P:SEQ], 1.0, NEG, ALU.add, ALU.max,
                                                       row_max[:, s % 2, q:q + 1]).then_inc(masked, 1)
                            e.wait_ge(masked, (n_s + 1) * QT)
                            e.tensor_scalar(neg_max[:, s % 2, :], row_max[:, s % 2, :], -1.0, None,
                                            ALU.mult).then_inc(neg_done, 1)
                        elif k == "N":
                            s = item[1]
                            n_s = g * 8 + s
                            e.wait_ge(exp_done, (n_s + 1) * QT)
                            e.reciprocal(row_inv[:, s % 2, :], row_sum[:, s % 2, :]).then_inc(inv_done, 1)
                            e.wait_ge(inv_done, n_s + 1)
                            for q in range(QT):
                                c = slice(P_AT[q], P_AT[q] + (q + 1) * P)
                                m = e.tensor_scalar(probs[:, s % 2, c], probs[:, s % 2, c],
                                                    row_inv[:, s % 2, q:q + 1], None, ALU.mult)
                            m.then_inc(probs_ready, 1)
                        elif k == "T":
                            s, piece = item[1:]
                            G = g - 1 if s == 7 else g
                            at, blocks = PIECES[piece]
                            w = len(blocks) * P
                            e.wait_ge(t_hi, (G * 8 + s) * 3 + piece + 1)
                            e.tensor_tensor(pt_lo[:, at:at + w], banks[T_BANK + (3 * s + piece) % 2][:, 0:w],
                                            pt_hi[:, at:at + w].bitcast(F32), ALU.subtract).then_inc(t_out, 1)
                        elif k == "PV" and item[2] == 2:
                            s = item[1]
                            G = g - 1 if s == 7 else g
                            b, h = divmod(s, GROUP)
                            e.wait_ge(pv_hi, G * 8 + s + 1)
                            e.tensor_tensor(at_lo[:, b, h, :], banks[O_BANK][:], at_hi[:, b, h, :].bitcast(F32),
                                            ALU.subtract).then_inc(pv_out, 1)
                        elif k == "W":
                            prep(item[1], g if item[1] == "o" else g + 1)

                e.wait_ge(consts_ready, 1)
                for k in "kqv":
                    prep(k, 0)
                groups(e, run)
                run(KV_HEADS, False, False, True)

            engines["sync"].append(a_sync)
            engines["scalar"].append(a_scalar)
            engines["vector"].append(a_vector)
            engines["tensor"].append(a_tensor)
            a_units = cnt.base(KV_HEADS, "unit") + 4

            x1_ready = norm_stage(1, lambda e: e.wait_ge(unit_out, a_units), True, "B" in phases,
                                 out if "B" not in phases else None)

        if "B" in phases:
            idx_loaded = [sem(f"idx_loaded{k}") for k in range(3)]
            gathered = [sem(f"gathered{k}") for k in range(3)]
            written = [sem(f"written{k}") for k in range(3)]
            N_CODES = D // CODE
            paced = sem("paced")

            def gather_gpsimd(e):
                def load_idx(k, t):
                    e.dma_start(codes_at[:, k, :].bitcast(I32), idx[bass.ts(t, 1), k, :, :].rearrange("a p c -> (a p) c")
                                ).then_inc(idx_loaded[k], 16)

                def write(k, t):
                    e.wait_ge(gathered[k], (t + 1) * 16 * N_CODES)
                    e.dma_start(wdram[bass.ts(t * 3 + k, 1), :, :].rearrange("a p c -> (a p) c"),
                                gathered_rows[:, k, :]).then_inc(written[k], 16)

                def body(t, first, last):
                    for k in range(3):
                        if not first:
                            e.wait_ge(paced, t * 3 + k)
                        e.wait_ge(idx_loaded[k], (t + 1) * 16)
                        if not first:
                            e.wait_ge(written[k], t * 16)
                        for c in range(N_CODES):
                            if c == 0:
                                e.tensor_tensor(pool_pace[:, k:k + 1], eps[0:1, :], eps[0:1, :],
                                                ALU.add).then_inc(paced, 1)
                            e.indirect_dma_start(gathered_rows[:, k, c * CODE:(c + 1) * CODE], None, codebook,
                                                 bass.IndirectOffsetOnAxis(ap=codes_at[:, k, c:c + 1], axis=0)
                                                 ).then_inc(gathered[k], 16)
                        if k:
                            write(k - 1, t)
                            if not last:
                                load_idx(k - 1, t + 1)
                    write(2, t)
                    if not last:
                        load_idx(2, t + 1)
                for k in range(3):
                    load_idx(k, 0)
                body(0, True, False)
                with e.Fori(1, FT - 1) as t:
                    body(t, False, False)
                body(FT - 1, False, True)

            engines["gpsimd"].append(gather_gpsimd)

        def mlp(name, ready, coded):
            cut_r, cut_f, close = arenas(name, 10240, 5120)
            g_hi, g_lo = cut_r(2, KB, P), cut_r(2, KB, P)
            u_hi, u_lo = cut_r(2, KB, P), cut_r(2, KB, P)
            d_hi, d_lo = cut_r(2, D), cut_r(2, D)
            h_hi, h_lo = cut_r(2, TOK), cut_r(2, TOK)
            stage = [cut_f(3, D), cut_f(3, D)]
            gate = cut_f(2, SEQ)
            inner = cut_f(2, SEQ)
            close()
            G_BANK, U_BANK, D_BANK, T_BANK = 0, 2, 4, 6
            s = {k: sem(f"{name}_{k}") for k in
                 ("loaded", "g_made", "u_made", "silu_done", "inner_done", "h_hi_done", "h_ready",
                  "w_made", "w_hi_done", "w_ready", "down_made", "down_out", "scales_loaded")}

            def tiles(e, body):
                body(0, 0, P)
                body(1, 1, P)
                with e.Fori(0, (FT - 3) // 2) as i:
                    body(i * 2 + 2, 0, P)
                    body(i * 2 + 3, 1, P)
                body(FT - 1, 0, FLAST)

            def is_int(t, v):
                return isinstance(t, int) and t == v

            def sync(e):
                def load(t, par, m):
                    rows = t * P if isinstance(t, int) else e.snap(t * P)
                    tiles3 = t * 3 if isinstance(t, int) else e.snap(t * 3)
                    whole_tiles, left, so_far = (v if isinstance(t, int) else e.snap(v) for v in
                                                 ((t + 1) * 16, (t - 1) * 3, t * per_load))
                    if coded:
                        for k in range(3):
                            e.wait_ge(written[k], whole_tiles)
                        e.sem_inc(may_load, 1)
                    if not (isinstance(t, int) and t < 2):
                        e.wait_ge(s["w_made"] if coded else s["w_ready"], left)
                        e.sem_inc(may_load, 1)
                    if not is_int(t, 0):
                        e.wait_ge(s["loaded"], so_far)
                    e.wait_ge(ready, 1)
                    e.sem_inc(may_load, 1)
                    done = s["loaded"]
                    if coded:
                        e.dma_start(stage[par], wdram[bass.ds(tiles3, 3), :, :].rearrange("k p c -> p k c")).then_inc(done, 16)
                        return
                    for k, w in enumerate((wf_gate, wf_up)):
                        e.dma_start(stage[par][:, k, :].rearrange("p (a b) -> p a b", a=KB)[:, :, 0:m].bitcast(I32),
                                    w.rearrange("(c p) n -> p c n", p=P)[:, :, bass.ds(rows, m)]).then_inc(done, 16)
                    e.dma_start(stage[par][0:m, 2, :].bitcast(I32), wf_down[bass.ds(rows, m), :]).then_inc(done, 16)
                if not coded:
                    e.dma_start(scale_sb[:], scales.to_broadcast([P, 3])).then_inc(s["scales_loaded"], 16)
                tiles(e, load)

            per_load = 16 if coded else 48

            def dest(k, par, lo):
                return {0: (g_hi, g_lo), 1: (u_hi, u_lo), 2: (d_hi, d_lo)}[k][lo][:, par]

            def width(k, m, ap):
                if k == 2:
                    return ap[0:m, :]
                return ap[:, :, 0:m]

            def source(k, par, m):
                b = banks[T_BANK + (par + k) % 2][:] if coded else stage[par][:, k, :].bitcast(I32)
                return width(k, m, b if k == 2 else b.rearrange("p (a b) -> p a b", a=KB))

            def scale_of(k, m):
                return scale_sb[0:(m if k == 2 else P), k:k + 1]

            def next_of(t, par, m):
                if is_int(t, FT - 1):
                    return None
                return t + 1, 1 - par, P

            def tensor(e):
                def turn(k, t, par, m):
                    if k == 0:
                        e.wait_ge(s["loaded"], (t + 1) * per_load)
                    if not (isinstance(t, int) and 3 * t + k < 2):
                        e.wait_ge(s["w_ready"], t * 3 + k - 1)
                    for c in range(KB):
                        x_ = e.transpose(banks[T_BANK + (par + k) % 2][:, c * P:(c + 1) * P],
                                         stage[par][:, k, c * P:(c + 1) * P], identity[:])
                    x_.then_inc(s["w_made"], 1)

                def up(t, par, m, half):
                    r = slice(half * SEQ, (half + 1) * SEQ)
                    for k, (hi, lo, bank, made, out_) in enumerate(
                            ((g_hi, g_lo, G_BANK, "g_made", "silu_done"), (u_hi, u_lo, U_BANK, "u_made", "inner_done"))):
                        if half == 0:
                            e.wait_ge(s["w_ready"], t * 3 + k + 1)
                        if not is_int(t, 0):
                            e.wait_ge(s[out_], t * 2 + half - 1)
                        for c in range(KB):
                            x_ = three(e, banks[bank + half][0:m, :], hi[:, par, c, 0:m], lo[:, par, c, 0:m],
                                       x_hi[:, c, r], x_lo[:, c, r], c == 0, c == KB - 1)
                        x_.then_inc(s[made], 1)

                def down(t, par, m):
                    e.wait_ge(s["w_ready"], t * 3 + 3)
                    e.wait_ge(s["h_ready"], t * 2 + 2)
                    for i in range(TILES):
                        if not (is_int(t, 0) and i < 2):
                            e.wait_ge(s["down_out"], t * TILES + i - 1)
                        r = slice(i * P, (i + 1) * P)
                        three(e, banks[D_BANK + i % 2][:], h_hi[0:m, par, r], h_lo[0:m, par, r], d_hi[0:m, par, :],
                              d_lo[0:m, par, :], True, True).then_inc(s["down_made"], 1)

                def body(t, par, m):
                    nxt = next_of(t, par, m)
                    up(t, par, m, 0)
                    if coded and nxt:
                        turn(0, *nxt)
                        turn(1, *nxt)
                    up(t, par, m, 1)
                    if not is_int(t, 0):
                        down(t - 1, 1 - par, P)
                    if coded and nxt:
                        turn(2, *nxt)

                e.wait_ge(ready, TILES)
                if coded:
                    for k in range(3):
                        turn(k, 0, 0, P)
                tiles(e, body)
                down(FT - 1, 0, FLAST)

            def scalar(e):
                def part(k, t, par, m):
                    if coded:
                        e.wait_ge(s["w_made"], t * 3 + k + 1)
                    elif k == 0:
                        e.wait_ge(s["loaded"], (t + 1) * per_load)
                    if not (isinstance(t, int) and t < 2):
                        if k < 2:
                            e.wait_ge(s["u_made"], (t - 1) * 2)
                        else:
                            e.wait_ge(s["down_made"], (t - 1) * TILES)
                    e.activation(width(k, m, dest(k, par, 0)), source(k, par, m), ACT.Copy,
                                 scale=1.0 if coded else scale_of(k, m)).then_inc(s["w_hi_done"], 1)

                def silu(t, par, m, half):
                    e.wait_ge(s["g_made"], t * 2 + half + 1)
                    if not is_int(t, 0):
                        e.wait_ge(s["inner_done"], t * 2 + half - 1)
                    e.activation(gate[0:m, half, :], banks[G_BANK + half][0:m, :], ACT.Silu).then_inc(s["silu_done"], 1)

                def high(t, par, m, half):
                    e.wait_ge(s["inner_done"], t * 2 + half + 1)
                    if not (isinstance(t, int) and t < 2):
                        e.wait_ge(s["down_made"], (t - 1) * TILES)
                    r = slice(half * SEQ, (half + 1) * SEQ)
                    e.activation(h_hi[0:m, par, r], inner[0:m, half, :], ACT.Copy).then_inc(s["h_hi_done"], 1)

                def body(t, par, m):
                    nxt = next_of(t, par, m)
                    silu(t, par, m, 0)
                    if nxt:
                        part(0, *nxt)
                        part(1, *nxt)
                    silu(t, par, m, 1)
                    high(t, par, m, 0)
                    high(t, par, m, 1)
                    if nxt:
                        part(2, *nxt)

                e.wait_ge(ready, 1)
                if not coded:
                    e.wait_ge(s["scales_loaded"], 16)
                for k in range(3):
                    part(k, 0, 0, P)
                tiles(e, body)

            def vector(e):
                def part(k, t, par, m):
                    e.wait_ge(s["w_hi_done"], t * 3 + k + 1)
                    e.scalar_tensor_tensor(out=width(k, m, dest(k, par, 1)), in0=source(k, par, m),
                                           scalar=1.0 if coded else scale_of(k, m),
                                           in1=width(k, m, dest(k, par, 0)).bitcast(F32), op0=ALU.mult,
                                           op1=ALU.subtract).then_inc(s["w_ready"], 1)

                def mult(t, par, m, half):
                    e.wait_ge(s["silu_done"], t * 2 + half + 1)
                    e.wait_ge(s["u_made"], t * 2 + half + 1)
                    if not is_int(t, 0):
                        e.wait_ge(s["h_ready"], t * 2 + half - 1)
                    e.tensor_tensor(inner[0:m, half, :], gate[0:m, half, :], banks[U_BANK + half][0:m, :],
                                    ALU.mult).then_inc(s["inner_done"], 1)

                def low(t, par, m, half):
                    r = slice(half * SEQ, (half + 1) * SEQ)
                    e.wait_ge(s["h_hi_done"], t * 2 + half + 1)
                    e.tensor_tensor(h_lo[0:m, par, r], inner[0:m, half, :], h_hi[0:m, par, r].bitcast(F32),
                                    ALU.subtract).then_inc(s["h_ready"], 1)

                def add(t):
                    for i in range(TILES):
                        e.wait_ge(s["down_made"], t * TILES + i + 1)
                        e.tensor_tensor(acc[:, i, :], acc[:, i, :], banks[D_BANK + i % 2][:],
                                        ALU.add).then_inc(s["down_out"], 1)

                def body(t, par, m):
                    nxt = next_of(t, par, m)
                    mult(t, par, m, 0)
                    if nxt:
                        part(0, *nxt)
                        part(1, *nxt)
                    mult(t, par, m, 1)
                    low(t, par, m, 0)
                    low(t, par, m, 1)
                    if not is_int(t, 0):
                        add(t - 1)
                    if nxt:
                        part(2, *nxt)

                for k in range(3):
                    part(k, 0, 0, P)
                tiles(e, body)
                add(FT - 1)

            engines["sync"].append(sync)
            engines["scalar"].append(scalar)
            engines["vector"].append(vector)
            engines["tensor"].append(tensor)
            return s["down_out"]

        if "B" in phases:
            coded_out = mlp("code", x1_ready, True)
            x2_ready = norm_stage(2, lambda e: e.wait_ge(coded_out, FT * TILES), True, "C" in phases,
                                  out if "C" not in phases else None)

        if "C" in phases:
            STEPS = 2 * HEADS
            CHUNKS = SEQ // P
            DEC = 2 * P + 2
            cut_r, cut_f, close = arenas("c", 16640, 15700)
            LIN = "kqvgo"
            c_stage = {k: cut_f(KB, P) for k in "kqvg"} | {"o": cut_f(D)}
            c_hi = {k: cut_r(KB, P) for k in "kqvg"} | {"o": cut_r(D)}
            c_lo = {k: cut_r(KB, P) for k in "kqvg"} | {"o": cut_r(D)}
            k_f, gate_f = cut_f(2, SEQ), cut_f(2, SEQ)
            q_f, v_f = cut_f(SEQ), cut_f(SEQ)
            k_h, k_l, q_h, q_l, v_h, v_l = (cut_r(2, SEQ) for _ in range(6))
            kn_h, kn_l = cut_r(CHUNKS, P), cut_r(CHUNKS, P)
            s_f, s_h, s_l = cut_f(CHUNKS, P), cut_r(SEQ), cut_r(SEQ)
            KVS = CHUNKS - 1
            kv_f, kv_h, kv_l = cut_f(KVS, P), cut_r(KVS, P), cut_r(KVS, P)
            inter_f, o_f, y_f = cut_f(CHUNKS, P), cut_f(SEQ), cut_f(SEQ)
            y_h, y_l = cut_r(2, SEQ), cut_r(2, SEQ)
            square, sum_sq = cut_f(SEQ), cut_f(2, SEQ)
            proj = cut_f(TILES, D)
            dec_stage, dec = cut_f(DEC + 1), cut_f(DEC + 1)
            rms, rms_inv, ones = cut_f(TILES), cut_f(TILES), cut_f(2)
            close()
            diag_decay = dec[:, 0:P].unsqueeze(1).to_broadcast([P, CHUNKS, P])
            q_decay = dec[:, P:2 * P].unsqueeze(1).to_broadcast([P, KVS, P])
            k_decay, block_decay, weight = (dec[:, DEC - 2 + i:DEC - 1 + i] for i in range(3))
            U, O_B, N_B, S_B, KV_B, INTRA_B, INTER_B = 0, 2, 3, 4, 5, 6, 7
            c = {k: sem(f"c_{k}") for k in
                 ("unit_made", "unit_out", "part_hi", "part_ready", "n_made", "kn_hi", "kn_ready", "s_made", "s_masked",
                  "s_hi", "s_ready", "kv_made", "kv_summed", "kv_chain", "kv_hi", "kv_ready", "intra_made",
                  "inter_made", "inter_scaled", "o_done", "y_done", "y_hi", "y_ready", "o_made", "o_added",
                  "squared", "sq_done", "dec_loaded", "dec_ready", "zeroed", "rms_made", "rms_sqrt", "rms_ready",
                  "rms_used")}
            c_loaded = {k: sem(f"c_{k}_loaded") for k in LIN}
            c_hi_done = {k: sem(f"c_{k}_hi_done") for k in LIN}
            c_ready = {k: sem(f"c_{k}_ready") for k in LIN}

            def late(n, k):
                return not isinstance(n, int) or n >= k

            def heads(e, body):
                body(0, True, False)
                with e.Fori(1, HEADS - 1) as h:
                    body(h, False, False)
                body(HEADS - 1, False, True)

            def c_sync(e):
                qkv = qkv_w.rearrange("(c p) (h n) -> p c h n", p=P, n=3 * P)
                src = {
                    "q": lambda h: qkv[:, :, bass.ds(h, 1), 0:P].rearrange("p c a n -> p (c a) n"),
                    "k": lambda h: qkv[:, :, bass.ds(h, 1), P:2 * P].rearrange("p c a n -> p (c a) n"),
                    "v": lambda h: qkv[:, :, bass.ds(h, 1), 2 * P:3 * P].rearrange("p c a n -> p (c a) n"),
                    "g": lambda h: gate_w.rearrange("(c p) (h n) -> p c h n", p=P, n=P)[:, :, bass.ds(h, 1), :]
                    .rearrange("p c a n -> p (c a) n"),
                    "o": lambda h: out_w.rearrange("(h p) n -> p h n", p=P)[:, bass.ds(h, 1), :]
                    .rearrange("p a n -> p (a n)"),
                }

                def load(h):
                    now = h if isinstance(h, int) else e.snap(h)
                    for k in "kqvgo":
                        if late(h, 1):
                            e.wait_ge(c_ready[k], now)
                        e.wait_ge(x2_ready, 1)
                        e.sem_inc(may_load, 1)
                        e.dma_start(c_stage[k], src[k](now)).then_inc(c_loaded[k], 16)
                    if late(h, 1):
                        e.wait_ge(c["dec_ready"], now)
                        e.sem_inc(may_load, 1)
                    e.dma_start(dec_stage[:, 0:DEC], decay[bass.ds(now, 1), :, :].rearrange("a p n -> (a p) n")
                                ).then_inc(c["dec_loaded"], 16)
                    e.dma_start(dec_stage[:, DEC:DEC + 1], norm_w[bass.ds(now, 1), :, :].rearrange("a p n -> (a p) n")
                                ).then_inc(c["dec_loaded"], 16)

                load(0)
                with e.Fori(1, HEADS) as h:
                    load(h)

            def c_tensor(e):
                def unit(k, h, n, b):
                    i = "kqvg".index(k)
                    if b == 0:
                        e.wait_ge(c_ready[k], h + 1)
                    if late(n * 4 + i, 2):
                        e.wait_ge(c["unit_out"], n * 4 + i - 1)
                    bank = banks[U + i % 2]
                    r = slice(b * SEQ, (b + 1) * SEQ)
                    if k == "v":
                        for j in range(CHUNKS):
                            t = slice(b * SEQ + j * P, b * SEQ + (j + 1) * P)
                            for a in range(KB):
                                m = three(e, bank[:, j * P:(j + 1) * P], x_hi[:, a, t], x_lo[:, a, t],
                                          c_hi[k][:, a, :], c_lo[k][:, a, :], a == 0, a == KB - 1)
                    else:
                        for a in range(KB):
                            m = three(e, bank[:], c_hi[k][:, a, :], c_lo[k][:, a, :], x_hi[:, a, r], x_lo[:, a, r],
                                      a == 0, a == KB - 1)
                    m.then_inc(c["unit_made"], 1)

                def chunk(j):
                    return slice(j * P, (j + 1) * P)

                def turn_keys(m, p):
                    e.wait_ge(c["unit_out"], m * 4 + 1)
                    if late(m, 1):
                        e.wait_ge(c["kn_ready"], m)
                    for j in range(CHUNKS):
                        x_ = e.transpose(banks[N_B][:, chunk(j)], k_f[:, p, chunk(j)], identity[:])
                    x_.then_inc(c["n_made"], 1)

                def scores(m, p):
                    e.wait_ge(c["part_ready"], m * 3 + 2)
                    if late(m, 1):
                        e.wait_ge(c["s_masked"], m)
                    for j in range(CHUNKS):
                        x_ = three(e, banks[S_B][:, chunk(j)], k_h[:, p, chunk(j)], k_l[:, p, chunk(j)],
                                   q_h[:, p, chunk(j)], q_l[:, p, chunk(j)], True, True)
                    x_.then_inc(c["s_made"], 1)

                def states(m, p):
                    e.wait_ge(c["part_ready"], m * 3 + 3)
                    e.wait_ge(c["kn_ready"], m + 1)
                    if late(m, 1):
                        e.wait_ge(c["kv_summed"], m)
                    for j in range(KVS):
                        x_ = three(e, banks[KV_B][:, chunk(j)], kn_h[:, j, :], kn_l[:, j, :], v_h[:, p, chunk(j)],
                                   v_l[:, p, chunk(j)], True, True)
                    x_.then_inc(c["kv_made"], 1)

                def intra(m, p):
                    e.wait_ge(c["s_ready"], m + 1)
                    if late(m, 1):
                        e.wait_ge(c["o_done"], m)
                    for j in range(CHUNKS):
                        x_ = three(e, banks[INTRA_B][:, chunk(j)], v_h[:, p, chunk(j)], v_l[:, p, chunk(j)],
                                   s_h[:, chunk(j)], s_l[:, chunk(j)], True, True)
                    x_.then_inc(c["intra_made"], 1)

                def inter(m, p):
                    e.wait_ge(c["kv_ready"], m + 1)
                    if late(m, 1):
                        e.wait_ge(c["inter_scaled"], m)
                    for j in range(KVS):
                        x_ = three(e, banks[INTER_B][:, chunk(j)], kv_h[:, j, :], kv_l[:, j, :],
                                   q_h[:, p, chunk(j + 1)], q_l[:, p, chunk(j + 1)], True, True)
                    x_.then_inc(c["inter_made"], 1)

                def out_tile(o, head, p, i):
                    if i == 0:
                        e.wait_ge(c["y_ready"], o + 1)
                        e.wait_ge(c_ready["o"], head + 1)
                    if late(o * 4 + i, 1):
                        e.wait_ge(c["o_added"], o * 4 + i)
                    three(e, banks[O_B][:], y_h[:, p, chunk(i)], y_l[:, p, chunk(i)], c_hi["o"], c_lo["o"],
                          True, True).then_inc(c["o_made"], 1)

                def step(h, b, units, n, attend, project):
                    m, o = n - 1, n - 2
                    head_o = h - 1
                    for k, i in (("k", 0), (None, 1), ("q", 2), ("v", 3)):
                        if k and units:
                            unit(k, h, n, b)
                        if k == "q" and project:
                            out_tile(o, head_o, b, 2)
                        if k == "k" and project:
                            out_tile(o, head_o, b, 0)
                        if k == "v" and project:
                            out_tile(o, head_o, b, 3)
                        if k == "k" and attend:
                            turn_keys(m, 1 - b)
                            scores(m, 1 - b)
                        if k is None and project:
                            out_tile(o, head_o, b, 1)
                        if k == "q" and attend:
                            states(m, 1 - b)
                            intra(m, 1 - b)
                        if k == "v" and attend:
                            inter(m, 1 - b)
                    if units:
                        unit("g", h, n, b)

                def body(h, first, last):
                    step(h, 0, True, h * 2, not first, not first)
                    step(h, 1, True, h * 2 + 1, True, not first)

                e.wait_ge(x2_ready, TILES)
                heads(e, body)
                step(HEADS, 0, False, STEPS, True, True)
                step(HEADS, 1, False, STEPS + 1, False, True)
                e.wait_ge(c["sq_done"], STEPS)
                for i in range(TILES):
                    x_ = e.matmul(banks[U][:, 2 * i:2 * i + 2], sum_sq[:, i // 4, chunk(i % 4)], ones,
                                  start=True, stop=True)
                x_.then_inc(c["rms_made"], 1)

            def c_scalar(e):
                def prep(k, h):
                    e.wait_ge(c_loaded[k], (h + 1) * 16)
                    if late(h, 1):
                        if k == "o":
                            e.wait_ge(c["o_made"], h * 8)
                        else:
                            e.wait_ge(c["unit_made"], (h * 2 - 1) * 4 + "kqvg".index(k) + 1)
                    e.activation(c_hi[k], c_stage[k], ACT.Copy).then_inc(c_hi_done[k], 1)

                def unit(k, n, b):
                    i = "kqvg".index(k)
                    e.wait_ge(c["unit_made"], n * 4 + i + 1)
                    dst = {"k": k_f[:, b, :], "q": q_f, "v": v_f, "g": gate_f[:, b, :]}[k]
                    if k == "k" and late(n, 2):
                        e.wait_ge(c["s_made"], n - 1)
                    if k == "q" and late(n, 1):
                        e.wait_ge(c["part_ready"], n * 3 - 1)
                    if k == "q" and late(n, 2):
                        e.wait_ge(c["inter_made"], n - 1)
                    if k == "v" and late(n, 1):
                        e.wait_ge(c["part_ready"], n * 3)
                    if k == "g" and late(n, 2):
                        e.wait_ge(c["y_done"], n - 1)
                    e.activation(dst, banks[U + i % 2][:], ACT.Sigmoid if k == "g" else ACT.Silu
                                 ).then_inc(c["unit_out"], 1)
                    if k != "g":
                        hi = {"k": k_h, "q": q_h, "v": v_h}[k][:, b, :]
                        e.wait_ge(c["unit_out"], n * 4 + i + 1)
                        e.activation(hi, dst, ACT.Copy).then_inc(c["part_hi"], 1)

                def scores_high(m):
                    e.wait_ge(c["s_masked"], m + 1)
                    if late(m, 1):
                        e.wait_ge(c["intra_made"], m)
                    e.activation(s_h, s_f.rearrange("p a b -> p (a b)"), ACT.Copy).then_inc(c["s_hi"], 1)

                def states_high(m):
                    e.wait_ge(c["kv_summed"], m + 1)
                    if late(m, 1):
                        e.wait_ge(c["inter_made"], m)
                    e.activation(kv_h, kv_f, ACT.Copy).then_inc(c["kv_hi"], 1)

                def out_high(m, p):
                    e.wait_ge(c["y_done"], m + 1)
                    if late(m, 2):
                        e.wait_ge(c["o_made"], (m - 1) * 4)
                    e.activation(y_h[:, p, :], y_f, ACT.Copy).then_inc(c["y_hi"], 1)

                def step(h, b, n, units, attend, first, last):
                    m = n - 1
                    if units:
                        unit("k", n, b)
                    if units and b == 0 and not first:
                        prep("g", h)
                    if attend:
                        keys_of(h, b, m)
                        scores_high(m)
                    if units:
                        unit("q", n, b)
                        if b == 1 and not last:
                            prep("k", h + 1)
                    if attend:
                        states_high(m)
                    if units:
                        unit("v", n, b)
                        if b == 1:
                            if not last:
                                prep("q", h + 1)
                            prep("o", h)
                    if attend:
                        out_high(m, 1 - b)
                    if units:
                        unit("g", n, b)
                        if b == 1 and not last:
                            prep("v", h + 1)

                def keys_of(h, b, m):
                    e.wait_ge(c["dec_ready"], h + b)
                    e.wait_ge(c["n_made"], m + 1)
                    if late(m, 1):
                        e.wait_ge(c["kv_made"], m)
                    e.activation(kn_h, banks[N_B][:].rearrange("p (a b) -> p a b", a=CHUNKS), ACT.Copy,
                                 scale=k_decay).then_inc(c["kn_hi"], 1)

                def body(h, first, last):
                    step(h, 0, h * 2, True, not first, first, last)
                    step(h, 1, h * 2 + 1, True, True, first, last)

                e.wait_ge(x2_ready, 1)
                for k in "kqvg":
                    prep(k, 0)
                heads(e, body)
                step(HEADS, 0, STEPS, False, True, False, True)
                e.wait_ge(c["rms_made"], 1)
                e.activation(rms, banks[U][:, 0:2 * TILES:2], ACT.Sqrt, bias=eps[:],
                             scale=1.0 / (HEADS * P)).then_inc(c["rms_sqrt"], 1)

            def c_vector(e):
                def low(k, n, b):
                    i = "kqv".index(k)
                    src = {"k": k_f[:, b, :], "q": q_f, "v": v_f}[k]
                    hi = {"k": k_h, "q": q_h, "v": v_h}[k][:, b, :]
                    lo = {"k": k_l, "q": q_l, "v": v_l}[k][:, b, :]
                    e.wait_ge(c["part_hi"], n * 3 + i + 1)
                    e.tensor_tensor(lo, src, hi.bitcast(F32), ALU.subtract).then_inc(c["part_ready"], 1)

                def keys_and_scores(m):
                    e.wait_ge(c["kn_hi"], m + 1)
                    e.scalar_tensor_tensor(out=kn_l, in0=banks[N_B][:].rearrange("p (a b) -> p a b", a=CHUNKS),
                                           scalar=k_decay, in1=kn_h.bitcast(F32), op0=ALU.mult,
                                           op1=ALU.subtract).then_inc(c["kn_ready"], 1)
                    e.wait_ge(c["s_made"], m + 1)
                    if late(m, 1):
                        e.wait_ge(c["s_ready"], m)
                    e.tensor_tensor(s_f, banks[S_B][:].rearrange("p (a b) -> p a b", a=CHUNKS), diag_decay,
                                    ALU.mult).then_inc(c["s_masked"], 1)
                    e.wait_ge(c["s_hi"], m + 1)
                    e.tensor_tensor(s_l, s_f.rearrange("p a b -> p (a b)"), s_h.bitcast(F32),
                                    ALU.subtract).then_inc(c["s_ready"], 1)

                def sums(m):
                    e.wait_ge(c["kv_made"], m + 1)
                    if late(m, 1):
                        e.wait_ge(c["kv_ready"], m)
                    e.tensor_copy(kv_f[:, 0, :], banks[KV_B][:, 0:P]).then_inc(c["kv_chain"], 1)
                    for j in range(1, KVS):
                        e.wait_ge(c["kv_chain"], m * (KVS - 1) + j)
                        e.scalar_tensor_tensor(out=kv_f[:, j, :], in0=kv_f[:, j - 1, :], scalar=block_decay,
                                               in1=banks[KV_B][:, j * P:(j + 1) * P], op0=ALU.mult, op1=ALU.add
                                               ).then_inc(c["kv_chain"] if j < KVS - 1 else c["kv_summed"], 1)
                    e.wait_ge(c["kv_hi"], m + 1)
                    e.tensor_tensor(kv_l, kv_f, kv_h.bitcast(F32), ALU.subtract).then_inc(c["kv_ready"], 1)

                def outputs(m, p):
                    e.wait_ge(c["inter_made"], m + 1)
                    e.wait_ge(c["zeroed"], 1)
                    e.tensor_tensor(inter_f[:, 1:CHUNKS, :],
                                    banks[INTER_B][:, 0:KVS * P].rearrange("p (a b) -> p a b", a=KVS), q_decay,
                                    ALU.mult).then_inc(c["inter_scaled"], 1)
                    e.wait_ge(c["inter_scaled"], m + 1)
                    e.wait_ge(c["intra_made"], m + 1)
                    if late(m, 1):
                        e.wait_ge(c["sq_done"], m)
                    e.tensor_tensor(o_f, inter_f.rearrange("p a b -> p (a b)"), banks[INTRA_B][:],
                                    ALU.add).then_inc(c["o_done"], 1)
                    e.wait_ge(c["o_done"], m + 1)
                    e.wait_ge(c["unit_out"], m * 4 + 4)
                    e.scalar_tensor_tensor(out=y_f, in0=o_f, scalar=weight, in1=gate_f[:, p, :], op0=ALU.mult,
                                           op1=ALU.mult).then_inc(c["y_done"], 1)
                    e.wait_ge(c["y_hi"], m + 1)
                    e.tensor_tensor(y_l[:, p, :], y_f, y_h[:, p, :].bitcast(F32),
                                    ALU.subtract).then_inc(c["y_ready"], 1)

                def add(o, p, i):
                    e.wait_ge(c["o_made"], o * 4 + i + 1)
                    t = p * 4 + i
                    e.tensor_tensor(proj[:, t, :], proj[:, t, :], banks[O_B][:], ALU.add).then_inc(c["o_added"], 1)

                def step(h, b, n, units, attend, project):
                    m, o = n - 1, n - 2
                    if units:
                        low("k", n, b)
                    if project:
                        add(o, b, 0)
                    if attend:
                        e.wait_ge(c["dec_ready"], h + b)
                        keys_and_scores(m)
                    if project:
                        add(o, b, 1)
                    if units:
                        low("q", n, b)
                    if project:
                        add(o, b, 2)
                    if attend:
                        sums(m)
                    if units:
                        low("v", n, b)
                    if project:
                        add(o, b, 3)
                    if attend:
                        outputs(m, 1 - b)

                def body(h, first, last):
                    step(h, 0, h * 2, True, not first, not first)
                    step(h, 1, h * 2 + 1, True, True, not first)

                e.wait_ge(x2_ready, 1)
                e.wait_ge(c["zeroed"], 1)
                heads(e, body)
                step(HEADS, 0, STEPS, False, True, True)
                step(HEADS, 1, STEPS + 1, False, False, True)
                e.wait_ge(c["rms_sqrt"], 1)
                e.reciprocal(rms_inv, rms).then_inc(c["rms_ready"], 1)
                e.wait_ge(c["rms_ready"], 1)
                e.wait_ge(c["o_added"], STEPS * 4)
                for t in range(TILES):
                    e.scalar_tensor_tensor(out=acc[:, t, :], in0=proj[:, t, :], scalar=rms_inv[:, t:t + 1],
                                           in1=acc[:, t, :], op0=ALU.mult, op1=ALU.add).then_inc(c["rms_used"], 1)

            def c_gpsimd(e):
                def low(k, h):
                    e.wait_ge(c_hi_done[k], h + 1)
                    e.tensor_tensor(c_lo[k], c_stage[k], c_hi[k].bitcast(F32), ALU.subtract).then_inc(c_ready[k], 1)

                def decays(h):
                    e.wait_ge(c["dec_loaded"], (h + 1) * 32)
                    if late(h, 1):
                        e.wait_ge(c["y_done"], h * 2)
                    e.tensor_tensor(dec, dec_stage, ones[:, 0:1].to_broadcast([P, DEC + 1]), ALU.mult
                                    ).then_inc(c["dec_ready"], 1)

                def square_sum(m, p):
                    e.wait_ge(c["o_done"], m + 1)
                    e.tensor_tensor(square, o_f, o_f, ALU.mult).then_inc(c["squared"], 1)
                    e.wait_ge(c["squared"], m + 1)
                    e.tensor_tensor(sum_sq[:, p, :], sum_sq[:, p, :], square, ALU.add).then_inc(c["sq_done"], 1)

                def body(h, first, last):
                    if not first:
                        low("g", h)
                        square_sum(h * 2 - 1, 1)
                    decays(h)
                    if not last:
                        low("k", h + 1)
                        low("q", h + 1)
                    low("o", h)
                    square_sum(h * 2, 0)
                    if not last:
                        low("v", h + 1)

                e.wait_ge(x2_ready, 1)
                e.memset(proj, 0.0)
                e.memset(sum_sq, 0.0)
                e.memset(ones, 1.0)
                e.memset(inter_f[:, 0, :], 0.0).then_inc(c["zeroed"], 1)
                e.wait_ge(c["zeroed"], 1)
                for k in "kqvg":
                    low(k, 0)
                heads(e, body)
                square_sum(STEPS - 1, 1)

            engines["sync"].append(c_sync)
            engines["scalar"].append(c_scalar)
            engines["vector"].append(c_vector)
            engines["tensor"].append(c_tensor)
            engines["gpsimd"].append(c_gpsimd)
            x3_ready = norm_stage(3, lambda e: e.wait_ge(c["rms_used"], TILES), True, "D" in phases,
                                  out if "D" not in phases else None)

        if "D" in phases:
            whole_out = mlp("int", x3_ready, False)
            norm_stage(4, lambda e: e.wait_ge(whole_out, FT * TILES), True, False, out)

        @block.sync
        def _(e):
            for f in engines["sync"]:
                f(e)

        @block.gpsimd
        def _(e):
            for f in engines["gpsimd"]:
                f(e)

        @block.scalar
        def _(e):
            for f in engines["scalar"]:
                f(e)

        @block.vector
        def _(e):
            for f in engines["vector"]:
                f(e)

        @block.tensor
        def _(e):
            for f in engines["tensor"]:
                f(e)


def host_arrays(inputs):
    import numpy as np
    a = {k.split("_", 2)[2] if "ffn" not in k else k.replace("_ffn_", "_"): np.asarray(v) for k, v in inputs.items()}
    pad = FT * P - FF

    def tiles_of_rows(i):
        return np.pad(i, ((0, pad), (0, 0))).reshape(FT, P, D // CODE)

    down = np.pad(a["L0_idx_down"], ((0, 0), (0, pad // CODE))).reshape(KB, P, FT, P // CODE)
    idx = np.stack([tiles_of_rows(a["L0_idx_gate"]), tiles_of_rows(a["L0_idx_up"]),
                    down.transpose(2, 1, 0, 3).reshape(FT, P, KB * P // CODE)], 1)
    slope = (np.float32(1.0 / 2.0 ** (8.0 / HEADS)) ** (np.arange(HEADS, dtype=np.float32) + 1)
             * np.float32(1.0 - 1 / (31 + 1e-05) + 1e-05)).astype(np.float64)
    n = np.arange(P, dtype=np.float64)
    gap = n[None, :] - n[:, None]
    diag = np.where(gap >= 0, np.exp(-slope[:, None, None] * np.maximum(gap, 0)), 0)
    q_decay = np.broadcast_to(np.exp(-slope[:, None, None] * (n + 1)), (HEADS, P, P))
    k_decay = np.exp(-slope[:, None, None] * (P - 1 - n)[None, :, None])
    block_decay = np.broadcast_to(np.exp(-slope[:, None, None] * P), (HEADS, P, 1))
    decay = np.concatenate([diag, q_decay, k_decay, block_decay], 2).astype(np.float32)
    return {
        "x": a["hidden_states"].reshape(TOK, D), "w_q": a["w_q"], "w_k": a["w_k"], "w_v": a["w_v"],
        "w_o": a["w_o"], "codebook": a["L0_codebook"], "idx": np.ascontiguousarray(idx),
        "qkv_w": np.ascontiguousarray(a["qkv_w"].T), "out_w": np.ascontiguousarray(a["out_w"].T),
        "gate_w": np.ascontiguousarray(a["gate_w"].T), "norm_w": a["norm_w"].reshape(HEADS, P, 1),
        "decay": decay,
        "wf_gate": np.ascontiguousarray(a["L1_w_gate"].T), "wf_up": np.ascontiguousarray(a["L1_w_up"].T),
        "wf_down": np.ascontiguousarray(a["L1_w_down"].T),
        "scales": np.stack([a["L1_scale_gate"], a["L1_scale_up"], a["L1_scale_down"]]).reshape(1, 3),
    }


_INS = ["x", "w_q", "w_k", "w_v", "w_o", "codebook", "idx", "qkv_w", "out_w", "gate_w", "norm_w", "decay",
        "wf_gate", "wf_up", "wf_down", "scales"]


def kernel(**inputs):
    import numpy as _np
    import concourse.bacc as _bacc
    from concourse import mybir as _mybir
    from concourse.bass_utils import run_bass_kernel_spmd as _run

    nc = _bacc.Bacc("TRN2", target_bir_lowering=False, num_devices=1)
    laid = host_arrays(inputs)
    arrays, args = {}, []
    for name in _INS:
        a = _np.ascontiguousarray(laid[name])
        arrays[f"in_{name}_dram"] = a
        args.append(nc.dram_tensor(f"in_{name}_dram", a.shape, _mybir.dt.from_np(a.dtype), kind="ExternalInput").ap())
    out = nc.dram_tensor("out_0_dram", (TOK, D), F32, kind="ExternalOutput").ap()
    weights = nc.dram_tensor("coded_weights_dram", (3 * FT, P, D), F32, kind="Internal").ap()
    build(nc, *args, out, weights)
    r = _run(nc, [arrays], core_ids=[0])
    return r.results[0]["out_0_dram"].reshape(TOK // SEQ, SEQ, D)
```

```python
from contextlib import ExitStack

import concourse.bass as bass
from concourse import mybir

F32 = mybir.dt.float32
F32R = mybir.dt.float32r
I32 = mybir.dt.int32
BF16 = mybir.dt.bfloat16
F16 = mybir.dt.float16
AX = mybir.AxisListType
U32 = mybir.dt.uint32
ALU = mybir.AluOpType
ACT = mybir.ActivationFunctionType

P = 128
TOK = 1024
SEQ = 512
TILES = TOK // P
D = 512
KB = D // P
HEADS = 32
KV_HEADS = 8
GROUP = HEADS // KV_HEADS
FF = 1376
FT = (FF + P - 1) // P
FLAST = FF - (FT - 1) * P
CODE = 8
NEG = -3.0e38
EPS = 1e-5
SCALE = float(P) ** -0.5
QT = SEQ // P
P_AT = [0, 128, 384, 768]
P_COLS = 1280
PIECES = [(0, [(0, q) for q in range(4)]),
          (512, [(1, q) for q in range(1, 4)]),
          (896, [(2, 2), (2, 3), (3, 3)])]
PT_AT = [0, 512, 896, 1152]
S_AT = [(2, 256), (2, 0), (1, 0), (0, 0)]


def attention_plan(first, last):
    plan = [("K", 0)]
    if not first:
        plan += [("T", 7, 0), ("T", 7, 1)]
    plan += [("K", 1)]
    if not first:
        plan += [("PV", 7, 0), ("T", 7, 2)]
    plan += [("Q", 0)]
    if not first:
        plan += [("PV", 7, 1), ("PV", 7, 2)]
    plan += [("V", 0), ("V", 1), ("X", 0)]
    old = [] if first else [[("O", 1, t)] for t in range(4)]
    fills = {s: [("Q", s + 1)] + (old[s] if s < len(old) else []) for s in range(7)}
    fills[0].insert(1, ("X", 1))
    fills[4] = [("Q", 5), ("Q", 6)]
    fills[5] = [("Q", 7), ("O", 0, 0)]
    fills[6] = [("O", 0, 1), ("O", 0, 2)]
    fills[7] = [("O", 0, 3)]
    for s in range(8):
        f = fills[s]
        if s:
            plan += [("T", s - 1, 0), ("T", s - 1, 1)]
        plan.append(("S", s))
        plan += f[:1]
        plan.append(("E", s))
        if s:
            plan += [("PV", s - 1, 0), ("T", s - 1, 2), ("PV", s - 1, 1)]
        plan.append(("N", s))
        plan += f[1:2]
        if s:
            plan += [("PV", s - 1, 2)]
        plan += f[2:]
        if s == 4:
            plan.append(("W", "o"))
        if not last and s in (1, 2, 7):
            plan.append(("W", {1: "k", 2: "v", 7: "q"}[s]))
    return plan


def attention_tail():
    return [("T", 7, 0), ("T", 7, 1), ("PV", 7, 0), ("T", 7, 2), ("PV", 7, 1), ("PV", 7, 2)] \
        + [("O", 1, t) for t in range(4)]


class Counts:

    def __init__(self):
        plan = attention_plan(False, False)
        self.per = {k: self.tally(plan, k) for k in ("unit", "T", "PV", "S")}
        self.first = {k: self.tally(attention_plan(True, False), k) for k in self.per}

    @staticmethod
    def kind(e):
        return "unit" if e[0] in "KQVXO" else e[0]

    def tally(self, plan, kind):
        return sum(1 for e in plan if self.kind(e) == kind and (kind != "PV" or e[2] == 2))

    def base(self, g, kind):
        if isinstance(g, int) and g == 0:
            return 0
        return g * self.per[kind] + (self.first[kind] - self.per[kind])


def build(nc, x, w_q, w_k, w_v, w_o, codebook, idx, qkv_w, out_w, gate_w, norm_w, decay,
          wf_gate, wf_up, wf_down, scales, out, wdram, phases="ABCD"):
    ctx = ExitStack()
    with ctx:
        def sb(name, shape, dt=F32):
            return ctx.enter_context(nc.sbuf_tensor(name, shape, dt))

        def sem(name):
            return ctx.enter_context(nc.semaphore(name))

        acc = sb("acc", [P, TILES, D])
        x_hi = sb("x_hi", [P, KB, TOK], F32R)
        x_lo = sb("x_lo", [P, KB, TOK], F32R)
        identity = sb("identity", [P, P])
        mask = sb("mask", [P, SEQ])
        eps = sb("eps", [P, 1])
        pace = sb("pace", [1, 1])
        pool_pace = sb("pool_pace", [1, 2])
        scale_sb = sb("scale_sb", [P, 3])
        LO = 16
        HI_BLOCKS = codebook.shape[0] // LO // P
        row_number = sb("row_number", [P, HI_BLOCKS])
        entry_number = sb("entry_number", [P, LO])
        codes_at = sb("codes_at", [P, 2, D // CODE], U32)
        gathered_rows = sb("gathered_rows", [P, 2, D])
        stats = sb("stats", [P, TILES, 6])
        mean_var = sb("mean_var", [P, TILES, 2])
        deviation = sb("deviation", [P, TILES])
        rstd = sb("rstd", [P, TILES])
        banks = [ctx.enter_context(nc.psum_tensor(f"bank{i}", [P, 512], F32)) for i in range(8)]

        def arenas(name, r_cols, f_cols, h_cols=0):
            stack = ExitStack()

            def cutter(arena, total):
                at = [0]

                def cut(*shape):
                    n = 1
                    for s in shape:
                        n *= s
                    assert at[0] + n <= total, (name, at[0] + n, total)
                    view = arena[:, at[0]:at[0] + n]
                    at[0] += n
                    if len(shape) == 2:
                        view = view.rearrange("p (a b) -> p a b", a=shape[0])
                    elif len(shape) == 3:
                        view = view.rearrange("p (a b c) -> p a b c", a=shape[0], b=shape[1])
                    return view
                return cut
            rounded = stack.enter_context(nc.sbuf_tensor(f"rounded_{name}", [P, r_cols], F32R))
            plain = stack.enter_context(nc.sbuf_tensor(f"plain_{name}", [P, f_cols], F32))
            if h_cols:
                halves = [stack.enter_context(nc.sbuf_tensor(f"{t}_{name}", [P, h_cols], dt))
                          for t, dt in (("bf16", BF16), ("fp16", F16))]
                return cutter(rounded, r_cols), cutter(plain, f_cols), [cutter(h, h_cols) for h in halves], stack.close
            return cutter(rounded, r_cols), cutter(plain, f_cols), stack.close

        consts_ready = sem("consts_ready")
        may_load = sem("may_load")
        x_loaded = sem("x_loaded")
        block = ctx.enter_context(nc.Block())

        engines = {k: [] for k in ("sync", "gpsimd", "scalar", "vector", "tensor")}

        def norm_stage(n, ready_waits, normalise, turn, store=None):
            stat = sem(f"stat{n}")
            dev = sem(f"dev{n}")
            rs = sem(f"rs{n}")
            normed = sem(f"normed{n}")
            turned = sem(f"turned{n}")
            hi = sem(f"x_hi_done{n}")
            lo = sem(f"x_ready{n}")

            def vector(e):
                ready_waits(e)
                if normalise:
                    for i in range(TILES):
                        e.bn_stats(stats[:, i, :], acc[:, i, :]).then_inc(stat, 1)
                    for i in range(TILES):
                        e.wait_ge(stat, i + 1)
                        e.bn_aggr(mean_var[:, i, :], stats[:, i, :]).then_inc(stat, 1)
                    e.wait_ge(dev, 1)
                    e.reciprocal(rstd[:], deviation[:]).then_inc(rs, 1)
                    e.wait_ge(rs, 1)
                    for i in range(TILES):
                        e.tensor_scalar(acc[:, i, :], acc[:, i, :], mean_var[:, i, 0:1], rstd[:, i:i + 1],
                                        ALU.subtract, ALU.mult).then_inc(normed, 1)
                if turn:
                    for i in range(TILES):
                        e.wait_ge(hi, i + 1)
                        at = slice(i * P, (i + 1) * P)
                        e.tensor_tensor(x_lo[:, :, at], banks[i % 2][:].rearrange("p (a b) -> p a b", a=KB),
                                        x_hi[:, :, at].bitcast(F32), ALU.subtract).then_inc(lo, 1)

            def scalar(e):
                if normalise:
                    e.wait_ge(stat, 2 * TILES)
                    e.activation(deviation[:], mean_var[:, :, 1], ACT.Sqrt, bias=eps[:]).then_inc(dev, 1)
                if turn:
                    for i in range(TILES):
                        e.wait_ge(turned, i + 1)
                        at = slice(i * P, (i + 1) * P)
                        e.activation(x_hi[:, :, at], banks[i % 2][:].rearrange("p (a b) -> p a b", a=KB),
                                     ACT.Copy).then_inc(hi, 1)

            def tensor(e):
                if not turn:
                    return
                if not normalise:
                    e.wait_ge(consts_ready, 1)
                    e.wait_ge(x_loaded, 16)
                for i in range(TILES):
                    if normalise:
                        e.wait_ge(normed, i + 1)
                    if i >= 2:
                        e.wait_ge(lo, i - 1)
                    for c in range(KB):
                        t = e.transpose(banks[i % 2][:, c * P:(c + 1) * P], acc[:, i, c * P:(c + 1) * P],
                                        identity[:])
                    t.then_inc(turned, 1)

            def sync(e):
                if store is not None:
                    stored = sem("stored")
                    for i in range(TILES):
                        e.wait_ge(normed, i + 1)
                        e.dma_start(store[i * P:(i + 1) * P, :], acc[:, i, :]).then_inc(stored, 16)
                    e.wait_ge(stored, 16 * TILES)

            engines["vector"].append(vector)
            engines["scalar"].append(scalar)
            engines["tensor"].append(tensor)
            engines["sync"].append(sync)
            return lo

        def start_sync(e):
            e.dma_start(acc[:], x.rearrange("(t p) d -> p t d", p=P)).then_inc(x_loaded, 16)

        const_step = sem("const_step")

        def start_gpsimd(e):
            e.memset(identity[:], 0.0).then_inc(const_step, 1)
            e.memset(mask[:], 0.0).then_inc(const_step, 1)
            e.memset(eps[:], EPS).then_inc(const_step, 1)
            e.wait_ge(const_step, 3)
            e.affine_select(out=identity[:], in_=identity[:], compare_op=ALU.not_equal, fill=1.0, base=0,
                            pattern=[[-1, P]], channel_multiplier=1).then_inc(const_step, 1)
            e.affine_select(out=mask[:, SEQ - P:SEQ], in_=mask[:, SEQ - P:SEQ], compare_op=ALU.is_ge, fill=NEG,
                            base=0, pattern=[[-1, P]], channel_multiplier=1).then_inc(const_step, 1)
            e.iota(row_number[:], pattern=[[P, HI_BLOCKS]], base=0, channel_multiplier=1,
                   allow_small_or_imprecise_dtypes=True).then_inc(const_step, 1)
            e.iota(entry_number[:], pattern=[[1, LO]], base=0, channel_multiplier=0,
                   allow_small_or_imprecise_dtypes=True).then_inc(const_step, 1)
            e.wait_ge(const_step, 7)
            e.memset(stats[:, 0, 0:1], 0.0).then_inc(consts_ready, 1)

        engines["sync"].append(start_sync)
        if "B" in phases:
            idx_loaded = [sem(f"idx_loaded{k}") for k in range(2)]

            def load_idx(e, k, t):
                e.dma_start(codes_at[:, k, :].bitcast(I32), idx[bass.ts(t, 1), k, :, :].rearrange("a p c -> (a p) c")
                            ).then_inc(idx_loaded[k], 16)

            def first_codes(e):
                load_idx(e, 0, 0)
                load_idx(e, 1, 0)
            engines["gpsimd"].append(first_codes)
        engines["gpsimd"].append(start_gpsimd)

        x0_ready = norm_stage(0, lambda e: None, False, True)

        def three(e, out_ap, l_hi, l_lo, r_hi, r_lo, start, stop):
            e.matmul(out_ap, l_hi, r_hi, start=start, stop=False)
            e.matmul(out_ap, l_hi, r_lo, start=False, stop=False)
            return e.matmul(out_ap, l_lo, r_hi, start=False, stop=stop)

        if "A" in phases:
            cut_r, cut_f, close = arenas("a", 27136, 8736)
            W_SHAPE = {"k": (KB, P), "v": (KB, P), "q": (KB, GROUP * P), "o": (GROUP, D)}
            stage = {k: cut_f(*s) for k, s in W_SHAPE.items()}
            w_hi = {k: cut_r(*s) for k, s in W_SHAPE.items()}
            w_lo = {k: cut_r(*s) for k, s in W_SHAPE.items()}
            k_hi, k_lo = cut_r(TOK), cut_r(TOK)
            v_hi, v_lo = cut_r(TILES, P), cut_r(TILES, P)
            q_hi, q_lo = cut_r(2, SEQ), cut_r(2, SEQ)
            pt_hi, pt_lo = cut_r(P_COLS), cut_r(P_COLS)
            at_hi, at_lo = cut_r(2, GROUP, SEQ), cut_r(2, GROUP, SEQ)
            probs = cut_f(2, P_COLS)
            v_whole = cut_f(2, SEQ)
            row_max, neg_max, row_sum, row_inv = (cut_f(2, QT) for _ in range(4))
            close()
            w_src = {
                "k": lambda g: w_k.rearrange("(c p) n -> p c n", p=P)[:, :, bass.ts(g, P)],
                "v": lambda g: w_v.rearrange("(c p) n -> p c n", p=P)[:, :, bass.ts(g, P)],
                "q": lambda g: w_q.rearrange("(c p) n -> p c n", p=P)[:, :, bass.ts(g, GROUP * P)],
                "o": lambda g: w_o.rearrange("(c p) n -> p c n", p=P)[:, bass.ts(g, GROUP), :],
            }
            cnt = Counts()
            w_loaded = {k: sem(f"w{k}_loaded") for k in "kvqo"}
            w_hi_done = {k: sem(f"w{k}_hi_done") for k in "kvqo"}
            w_ready = {k: sem(f"w{k}_ready") for k in "kvqo"}
            unit_made, unit_hi, unit_out = sem("unit_made"), sem("unit_hi"), sem("unit_out")
            scores_made, masked, neg_done = sem("scores_made"), sem("masked"), sem("neg_done")
            exp_done, inv_done, probs_ready = sem("exp_done"), sem("inv_done"), sem("probs_ready")
            t_made, t_hi, t_out = sem("t_made"), sem("t_hi"), sem("t_out")
            pv_made, pv_hi, pv_out = sem("pv_made"), sem("pv_hi"), sem("pv_out")
            S_BANK, T_BANK, O_BANK, U_BANK = 0, 3, 5, 6

            def groups(e, body):
                body(0, True, False)
                with e.Fori(1, KV_HEADS - 1) as g:
                    body(g, False, False)
                body(KV_HEADS - 1, False, True)

            def where(g, first, last, tail=False):
                plan = attention_tail() if tail else attention_plan(first, last)
                base = {k: cnt.base(g, k) for k in ("unit", "T", "PV", "S")}
                seen = {k: 0 for k in base}
                last_q = 0
                for n, e in enumerate(plan):
                    k = cnt.kind(e)
                    if k in seen and (k != "PV" or e[2] == 2):
                        seen[k] += 1
                    yield e, seen, base, plan, n

            def unit_number(plan, base, what):
                n = 0
                for e in plan:
                    if cnt.kind(e) == "unit":
                        n += 1
                    if e == what:
                        return base["unit"] + n
                raise KeyError(what)

            def a_sync(e):
                def load(k, g):
                    e.dma_start(stage[k], w_src[k](g)).then_inc(w_loaded[k], 16)
                for k in "kvqo":
                    load(k, 0)

                def body(g, first, last):
                    if last:
                        return
                    for k in "kvqo":
                        e.wait_ge(w_ready[k], g + 1)
                        load(k, g + 1)
                body(0, True, False)
                with e.Fori(1, KV_HEADS - 1) as g:
                    body(g, False, False)

            def a_tensor(e):
                def product(kind, bank, item, waits=None):
                    if kind == "K":
                        r = slice(item[1] * SEQ, (item[1] + 1) * SEQ)
                        for c in range(KB):
                            m = three(e, bank[:], w_hi["k"][:, c, :], w_lo["k"][:, c, :], x_hi[:, c, r],
                                      x_lo[:, c, r], c == 0, c == KB - 1)
                    elif kind == "Q":
                        b, h = divmod(item[1], GROUP)
                        r = slice(b * SEQ, (b + 1) * SEQ)
                        for c in range(KB):
                            m = three(e, bank[:], w_hi["q"][:, c, h * P:(h + 1) * P],
                                      w_lo["q"][:, c, h * P:(h + 1) * P], x_hi[:, c, r], x_lo[:, c, r],
                                      c == 0, c == KB - 1)
                    elif kind == "V":
                        r = slice(item[1] * SEQ, (item[1] + 1) * SEQ)
                        for c in range(KB):
                            m = three(e, bank[:], w_hi["v"][:, c, :], w_lo["v"][:, c, :], x_hi[:, c, r],
                                      x_lo[:, c, r], c == 0, c == KB - 1)
                    elif kind == "X":
                        for i in range(4):
                            r = slice(i * P, (i + 1) * P)
                            m = e.transpose(bank[:, r], v_whole[:, item[1], r], identity[:])
                    else:
                        b, t = item[1:]
                        r = slice(t * P, (t + 1) * P)
                        for h in range(GROUP):
                            m = three(e, bank[:], at_hi[:, b, h, r], at_lo[:, b, h, r], w_hi["o"][:, h, :],
                                      w_lo["o"][:, h, :], h == 0, h == GROUP - 1)
                    return m

                def run(g, first, last, tail=False):
                    for item, seen, base, plan, n in where(g, first, last, tail):
                        k = item[0]
                        if cnt.kind(item) == "unit":
                            u = seen["unit"]
                            if not (first and u <= 2):
                                e.wait_ge(unit_out, base["unit"] + u - 2)
                            if k == "K" and item[1] == 0:
                                e.wait_ge(w_ready["k"], g + 1)
                            if k == "V" and item[1] == 0:
                                e.wait_ge(w_ready["v"], g + 1)
                            if k == "Q" and item[1] == 0:
                                e.wait_ge(w_ready["q"], g + 1)
                            if k == "X":
                                e.wait_ge(unit_out, unit_number(plan, base, ("V", item[1])))
                            if k == "O" and item[1] == 0 and item[2] == 0:
                                e.wait_ge(w_ready["o"], g + 1)
                                e.wait_ge(pv_out, g * 8 + 4)
                            if k == "O" and item[1] == 1 and item[2] == 0:
                                e.wait_ge(pv_out, g * 8)
                            product(k, banks[U_BANK + (u - 1) % 2], item).then_inc(unit_made, 1)
                        elif k == "S":
                            s = item[1]
                            b = s // GROUP
                            e.wait_ge(unit_out, unit_number(plan, base, ("Q", s)))
                            if not (first and s == 0):
                                e.wait_ge(masked, (g * 8 + s) * QT)
                            for q in range(QT):
                                bank, at = S_AT[q]
                                r = slice(q * P, (q + 1) * P)
                                ks = slice(b * SEQ, b * SEQ + (q + 1) * P)
                                m = three(e, banks[S_BANK + bank][:, at:at + (q + 1) * P], q_hi[:, s % 2, r],
                                          q_lo[:, s % 2, r], k_hi[:, ks], k_lo[:, ks], True, True)
                            m.then_inc(scores_made, 1)
                        elif k == "T":
                            s, piece = item[1:]
                            G = g - 1 if s == 7 and not isinstance(g, int) else (g - 1 if s == 7 else g)
                            if piece == 0:
                                e.wait_ge(probs_ready, G * 8 + s + 1)
                            tn = (G * 8 + s) * 3 + piece
                            par = (s + piece) % 2
                            if not (isinstance(G, int) and G == 0 and s * 3 + piece < 2):
                                e.wait_ge(t_out, tn - 1)
                            for i, (j, q) in enumerate(PIECES[piece][1]):
                                m = e.transpose(banks[T_BANK + (3 * s + piece) % 2][:, i * P:(i + 1) * P],
                                                probs[:, s % 2, P_AT[q] + j * P:P_AT[q] + (j + 1) * P], identity[:])
                            m.then_inc(t_made, 1)
                        elif k == "PV":
                            s, piece = item[1:]
                            G = g - 1 if s == 7 else g
                            b = s // GROUP
                            e.wait_ge(t_out, (G * 8 + s) * 3 + piece + 1)
                            if piece == 0:
                                if s == 0:
                                    e.wait_ge(unit_out, unit_number(plan, base, ("X", 1)))
                                if not (isinstance(G, int) and G == 0 and s == 0):
                                    e.wait_ge(pv_out, G * 8 + s)
                            for j in {0: [0], 1: [1], 2: [2, 3]}[piece]:
                                t = b * 4 + j
                                cols = slice(PT_AT[j], PT_AT[j] + (QT - j) * P)
                                m = three(e, banks[O_BANK][:, j * P:SEQ], v_hi[:, t, :], v_lo[:, t, :],
                                          pt_hi[:, cols], pt_lo[:, cols], j == 0, j == 3)
                            if piece == 2:
                                m.then_inc(pv_made, 1)

                e.wait_ge(x0_ready, TILES)
                groups(e, run)
                run(KV_HEADS, False, False, True)

            def a_scalar(e):
                def prep(k, g):
                    e.wait_ge(w_loaded[k], (g + 1) * 16)
                    if not (isinstance(g, int) and g == 0):
                        if k == "k":
                            e.wait_ge(unit_made, cnt.base(g - 1, "unit") + 2)
                        if k == "v":
                            e.wait_ge(unit_made, cnt.base(g - 1, "unit") + 5)
                        if k == "q":
                            e.wait_ge(unit_made, cnt.base(g, "unit") - 1)
                        if k == "o":
                            e.wait_ge(unit_made, cnt.base(g, "unit") + 15)
                    e.activation(w_hi[k], stage[k], ACT.Copy).then_inc(w_hi_done[k], 1)

                def run(g, first, last, tail=False):
                    for item, seen, base, plan, n in where(g, first, last, tail):
                        k = item[0]
                        if k in ("K", "Q", "X"):
                            u = base["unit"] + seen["unit"]
                            bank = banks[U_BANK + (seen["unit"] - 1) % 2]
                            e.wait_ge(unit_made, u)
                            if k == "K":
                                r = slice(item[1] * SEQ, (item[1] + 1) * SEQ)
                                if not first:
                                    e.wait_ge(scores_made, g * 8)
                                e.activation(k_hi[:, r], bank[:], ACT.Copy).then_inc(unit_hi, 1)
                            elif k == "Q":
                                s = item[1]
                                if not (first and s < 2):
                                    e.wait_ge(scores_made, g * 8 + s - 1)
                                e.activation(q_hi[:, s % 2, :], bank[:], ACT.Copy, scale=SCALE).then_inc(unit_hi, 1)
                            else:
                                if not first:
                                    e.wait_ge(pv_made, g * 8)
                                r = slice(item[1] * 4, item[1] * 4 + 4)
                                e.activation(v_hi[:, r, :], bank[:].rearrange("p (a b) -> p a b", b=P),
                                             ACT.Copy).then_inc(unit_hi, 1)
                        elif k == "E":
                            s = item[1]
                            n_s = g * 8 + s
                            e.wait_ge(neg_done, n_s + 1)
                            for q in range(QT):
                                c = slice(P_AT[q], P_AT[q] + (q + 1) * P)
                                e.activation(probs[:, s % 2, c], probs[:, s % 2, c], ACT.Exp,
                                             bias=neg_max[:, s % 2, q:q + 1],
                                             accum_out=row_sum[:, s % 2, q:q + 1]).then_inc(exp_done, 1)
                        elif k == "T":
                            s, piece = item[1:]
                            G = g - 1 if s == 7 else g
                            at, blocks = PIECES[piece]
                            w = len(blocks) * P
                            e.wait_ge(t_made, (G * 8 + s) * 3 + piece + 1)
                            if not (isinstance(G, int) and G == 0 and s == 0):
                                e.wait_ge(pv_made, G * 8 + s)
                            e.activation(pt_hi[:, at:at + w], banks[T_BANK + (3 * s + piece) % 2][:, 0:w],
                                         ACT.Copy).then_inc(t_hi, 1)
                        elif k == "PV" and item[2] == 2:
                            s = item[1]
                            G = g - 1 if s == 7 else g
                            b, h = divmod(s, GROUP)
                            e.wait_ge(pv_made, G * 8 + s + 1)
                            if h == 0:
                                if not (isinstance(G, int) and G == 0):
                                    e.wait_ge(unit_made, cnt.base(G, "unit") + (0 if b == 0 else 15))
                            e.activation(at_hi[:, b, h, :], banks[O_BANK][:], ACT.Copy).then_inc(pv_hi, 1)
                        elif k == "W":
                            prep(item[1], g if item[1] == "o" else g + 1)

                for k in "kqv":
                    prep(k, 0)
                groups(e, run)
                run(KV_HEADS, False, False, True)

            def a_vector(e):
                def prep(k, g):
                    e.wait_ge(w_hi_done[k], g + 1)
                    e.tensor_tensor(w_lo[k], stage[k], w_hi[k].bitcast(F32), ALU.subtract).then_inc(w_ready[k], 1)

                def run(g, first, last, tail=False):
                    n_hi = 0
                    for item, seen, base, plan, n in where(g, first, last, tail):
                        k = item[0]
                        if k == "V":
                            e.wait_ge(unit_made, base["unit"] + seen["unit"])
                            e.tensor_copy(v_whole[:, item[1], :], banks[U_BANK + (seen["unit"] - 1) % 2][:]
                                          ).then_inc(unit_out, 1)
                        elif k in ("K", "Q", "X"):
                            n_hi += 1
                            bank = banks[U_BANK + (seen["unit"] - 1) % 2]
                            e.wait_ge(unit_hi, g * 12 + n_hi)
                            if k == "K":
                                r = slice(item[1] * SEQ, (item[1] + 1) * SEQ)
                                e.tensor_tensor(k_lo[:, r], bank[:], k_hi[:, r].bitcast(F32),
                                                ALU.subtract).then_inc(unit_out, 1)
                            elif k == "Q":
                                s = item[1]
                                e.scalar_tensor_tensor(out=q_lo[:, s % 2, :], in0=bank[:], scalar=SCALE,
                                                       in1=q_hi[:, s % 2, :].bitcast(F32), op0=ALU.mult,
                                                       op1=ALU.subtract).then_inc(unit_out, 1)
                            else:
                                r = slice(item[1] * 4, item[1] * 4 + 4)
                                e.tensor_tensor(v_lo[:, r, :], bank[:].rearrange("p (a b) -> p a b", b=P),
                                                v_hi[:, r, :].bitcast(F32), ALU.subtract).then_inc(unit_out, 1)
                        elif k == "O":
                            t = item[1] * 4 + item[2]
                            e.wait_ge(unit_made, base["unit"] + seen["unit"])
                            e.tensor_tensor(acc[:, t, :], acc[:, t, :], banks[U_BANK + (seen["unit"] - 1) % 2][:],
                                            ALU.add).then_inc(unit_out, 1)
                        elif k == "S":
                            s = item[1]
                            n_s = g * 8 + s
                            e.wait_ge(scores_made, n_s + 1)
                            if not (first and s < 2):
                                e.wait_ge(t_made, (n_s - 1) * 3)
                            e.memset(pace[:], 0.0)
                            for q in range(QT):
                                bank, at = S_AT[q]
                                c = slice(P_AT[q], P_AT[q] + (q + 1) * P)
                                e.tensor_tensor_reduce(probs[:, s % 2, c], banks[S_BANK + bank][:, at:at + (q + 1) * P],
                                                       mask[:, SEQ - (q + 1) * P:SEQ], 1.0, NEG, ALU.add, ALU.max,
                                                       row_max[:, s % 2, q:q + 1]).then_inc(masked, 1)
                            e.wait_ge(masked, (n_s + 1) * QT)
                            e.tensor_scalar(neg_max[:, s % 2, :], row_max[:, s % 2, :], -1.0, None,
                                            ALU.mult).then_inc(neg_done, 1)
                        elif k == "N":
                            s = item[1]
                            n_s = g * 8 + s
                            e.wait_ge(exp_done, (n_s + 1) * QT)
                            e.reciprocal(row_inv[:, s % 2, :], row_sum[:, s % 2, :]).then_inc(inv_done, 1)
                            e.wait_ge(inv_done, n_s + 1)
                            for q in range(QT):
                                c = slice(P_AT[q], P_AT[q] + (q + 1) * P)
                                m = e.tensor_scalar(probs[:, s % 2, c], probs[:, s % 2, c],
                                                    row_inv[:, s % 2, q:q + 1], None, ALU.mult)
                            m.then_inc(probs_ready, 1)
                        elif k == "T":
                            s, piece = item[1:]
                            G = g - 1 if s == 7 else g
                            at, blocks = PIECES[piece]
                            w = len(blocks) * P
                            e.wait_ge(t_hi, (G * 8 + s) * 3 + piece + 1)
                            e.tensor_tensor(pt_lo[:, at:at + w], banks[T_BANK + (3 * s + piece) % 2][:, 0:w],
                                            pt_hi[:, at:at + w].bitcast(F32), ALU.subtract).then_inc(t_out, 1)
                        elif k == "PV" and item[2] == 2:
                            s = item[1]
                            G = g - 1 if s == 7 else g
                            b, h = divmod(s, GROUP)
                            e.wait_ge(pv_hi, G * 8 + s + 1)
                            e.tensor_tensor(at_lo[:, b, h, :], banks[O_BANK][:], at_hi[:, b, h, :].bitcast(F32),
                                            ALU.subtract).then_inc(pv_out, 1)
                        elif k == "W":
                            prep(item[1], g if item[1] == "o" else g + 1)

                e.wait_ge(consts_ready, 1)
                for k in "kqv":
                    prep(k, 0)
                groups(e, run)
                run(KV_HEADS, False, False, True)

            engines["sync"].append(a_sync)
            engines["scalar"].append(a_scalar)
            engines["vector"].append(a_vector)
            engines["tensor"].append(a_tensor)
            a_units = cnt.base(KV_HEADS, "unit") + 4

            x1_ready = norm_stage(1, lambda e: e.wait_ge(unit_out, a_units), True, "B" in phases,
                                 out if "B" not in phases else None)

        if "B" in phases:
            gathered = [sem(f"gathered{k}") for k in range(2)]
            written = [sem(f"written{k}") for k in range(2)]
            N_CODES = D // CODE
            paced = sem("paced")

            def gather_gpsimd(e):
                def write(k, t):
                    e.wait_ge(gathered[k], (t + 1) * 16 * N_CODES)
                    e.dma_start(wdram[bass.ts(t * 2 + k, 1), :, :].rearrange("a p c -> (a p) c"),
                                gathered_rows[:, k, :]).then_inc(written[k], 16)

                def body(t, first, last):
                    m = FLAST if last else P
                    for k in range(2):
                        if not first:
                            e.wait_ge(paced, t * 2 + k)
                        e.wait_ge(idx_loaded[k], (t + 1) * 16)
                        if not first:
                            e.wait_ge(written[k], t * 16)
                        for c in range(N_CODES):
                            if c == 0:
                                e.tensor_tensor(pool_pace[:, k:k + 1], eps[0:1, :], eps[0:1, :],
                                                ALU.add).then_inc(paced, 1)
                            e.indirect_dma_start(gathered_rows[0:m, k, c * CODE:(c + 1) * CODE], None, codebook,
                                                 bass.IndirectOffsetOnAxis(ap=codes_at[0:m, k, c:c + 1], axis=0)
                                                 ).then_inc(gathered[k], 16)
                        if k:
                            write(k - 1, t)
                            if not last:
                                load_idx(e, k - 1, t + 1)
                    write(1, t)
                    if not last:
                        load_idx(e, 1, t + 1)
                body(0, True, False)
                with e.Fori(1, FT - 1) as t:
                    body(t, False, False)
                body(FT - 1, False, True)

            engines["gpsimd"].append(gather_gpsimd)

        def mlp(name, ready, coded):
            if coded:
                cut_r, cut_f, (cut_b, cut_h), close = arenas(name, 10240, 9600, 6200)
            else:
                cut_r, cut_f, close = arenas(name, 10240, 5120)
            g_hi, g_lo = cut_r(2, KB, P), cut_r(2, KB, P)
            u_hi, u_lo = cut_r(2, KB, P), cut_r(2, KB, P)
            d_hi, d_lo = cut_r(2, D), cut_r(2, D)
            h_hi, h_lo = cut_r(2, TOK), cut_r(2, TOK)
            stage = [cut_f(3, D), cut_f(3, D)]
            gate = cut_f(2, SEQ)
            inner = cut_f(2, SEQ)
            if coded:
                ROUND = SEQ // P
                ROUNDS = KB * (P // CODE) // ROUND
                NIDX = ROUND * ROUNDS
                book = cut_f(HI_BLOCKS, LO * CODE)
                rest = cut_f(2, HI_BLOCKS * LO * CODE)
                parts = [cut_b(HI_BLOCKS, LO * CODE) for _ in range(3)]
                row_hot = cut_b(2, HI_BLOCKS, SEQ)
                spread = cut_h(2, SEQ)
                hi_half = cut_h(NIDX)
                identity_h = cut_h(P)
                codes_d, hi_int, lo_int = (cut_f(NIDX) for _ in range(3))
                entry_hot = cut_f(NIDX, LO)
                lo_f = cut_f(NIDX)
                masked_f = cut_f(2, SEQ)
                down_rows = cut_f(D)
                pick = {k: sem(f"pick_{k}") for k in
                        ("book_loaded", "book_part", "codes_loaded", "codes_split", "codes_ready",
                         "last_up", "spread_made", "spread_copied", "hot", "picked", "masked", "reduced")}
            close()
            G_BANK, U_BANK, D_BANK, T_BANK, D_RING = 0, 2, 4, 6, 4
            s = {k: sem(f"{name}_{k}") for k in
                 ("loaded", "g_made", "u_made", "silu_done", "inner_done", "h_hi_done", "h_ready",
                  "w_made", "w_hi_done", "w_ready", "down_made", "down_out", "scales_loaded")}

            def tiles(e, body):
                pairs = (FT - 5) // 2 if coded else (FT - 3) // 2
                body(0, 0, P)
                body(1, 1, P)
                with e.Fori(0, pairs) as i:
                    body(i * 2 + 2, 0, P)
                    body(i * 2 + 3, 1, P)
                for t in range(2 * pairs + 2, FT - 1):
                    body(t, t % 2, P)
                body(FT - 1, 0, FLAST)

            def is_int(t, v):
                return isinstance(t, int) and t == v

            def late(n, k):
                return not isinstance(n, int) or n >= k

            def sync(e):
                def load(t, par, m):
                    rows = t * P if isinstance(t, int) else e.snap(t * P)
                    tiles2 = t * 2 if isinstance(t, int) else e.snap(t * 2)
                    now = t if isinstance(t, int) else e.snap(t)
                    whole_tiles, left, so_far = (v if isinstance(t, int) else e.snap(v) for v in
                                                 ((t + 1) * 16, (t - 1) * 3, t * per_load))
                    if coded:
                        if not is_int(t, 0):
                            e.wait_ge(pick["codes_ready"], now)
                        e.wait_ge(ready, 1)
                        e.sem_inc(may_load, 1)
                        e.dma_start(codes_d.bitcast(I32), idx[bass.ds(now, 1), 2, :, :].rearrange("a p c -> (a p) c")
                                    ).then_inc(pick["codes_loaded"], 16)
                        for k in range(1 if is_int(t, FT - 1) else 2):
                            e.wait_ge(written[k], whole_tiles)
                        e.sem_inc(may_load, 1)
                    if not (isinstance(t, int) and t < 2):
                        e.wait_ge(s["w_made"] if coded else s["w_ready"], left)
                        e.sem_inc(may_load, 1)
                    if not is_int(t, 0):
                        e.wait_ge(s["loaded"], so_far)
                    e.wait_ge(ready, 1)
                    e.sem_inc(may_load, 1)
                    done = s["loaded"]
                    if coded:
                        n = 1 if is_int(t, FT - 1) else 2
                        e.dma_start(stage[par][:, 0:n, :], wdram[bass.ds(tiles2, n), :, :].rearrange("k p c -> p k c")
                                    ).then_inc(done, 16)
                        if is_int(t, FT - 1):
                            e.wait_ge(written[1], whole_tiles)
                            e.dma_start(stage[par][:, 1, :], wdram[tiles2 + 1, :, :]).then_inc(pick["last_up"], 16)
                        return
                    for k, w in enumerate((wf_gate, wf_up)):
                        e.dma_start(stage[par][:, k, :].rearrange("p (a b) -> p a b", a=KB)[:, :, 0:m].bitcast(I32),
                                    w.rearrange("(c p) n -> p c n", p=P)[:, :, bass.ds(rows, m)]).then_inc(done, 16)
                    e.dma_start(stage[par][0:m, 2, :].bitcast(I32), wf_down[bass.ds(rows, m), :]).then_inc(done, 16)
                if not coded:
                    e.dma_start(scale_sb[:], scales.to_broadcast([P, 3])).then_inc(s["scales_loaded"], 16)
                else:
                    e.wait_ge(ready, 1)
                    e.dma_start(book, codebook.rearrange("(b p l) k -> p b (l k)", p=P, l=LO)
                                ).then_inc(pick["book_loaded"], 16)
                tiles(e, load)

            per_load = 16 if coded else 48

            def dest(k, par, lo):
                return {0: (g_hi, g_lo), 1: (u_hi, u_lo), 2: (d_hi, d_lo)}[k][lo][:, par]

            def width(k, m, ap):
                if k == 2:
                    return ap[0:m, :]
                return ap[:, :, 0:m]

            def source(k, par, m):
                b = banks[T_BANK + (par + k) % 2][:] if coded else stage[par][:, k, :].bitcast(I32)
                return width(k, m, b if k == 2 else b.rearrange("p (a b) -> p a b", a=KB))

            def scale_of(k, m):
                return scale_sb[0:(m if k == 2 else P), k:k + 1]

            def next_of(t, par, m):
                if is_int(t, FT - 1):
                    return None
                return t + 1, 1 - par, P

            def tensor(e):
                def turn(k, t, par, m):
                    if k == 0:
                        e.wait_ge(s["loaded"], (t + 1) * per_load)
                    if k == 1 and is_int(t, FT - 1):
                        e.wait_ge(pick["last_up"], 16)
                    if not (isinstance(t, int) and 3 * t + k < 2):
                        e.wait_ge(s["w_ready"], t * 3 + k - 1)
                    if k < 2 and late(t, 2):
                        e.wait_ge(s["down_out"], (t if is_int(t, FT - 1) else t - 1) * TILES)
                    if k == 2:
                        e.wait_ge(pick["reduced"], (t + 1) * ROUNDS)
                    for c in range(KB):
                        src = down_rows[:, c * P:(c + 1) * P] if k == 2 else stage[par][:, k, c * P:(c + 1) * P]
                        x_ = e.transpose(banks[T_BANK + (par + k) % 2][:, c * P:(c + 1) * P], src, identity[:])
                    x_.then_inc(s["w_made"], 1)

                def gather(t, par):
                    def spread_rows(q):
                        if late(t * ROUNDS + q, 2):
                            e.wait_ge(pick["spread_copied"], t * ROUNDS + q - 1)
                        for g in range(ROUND):
                            c = q * ROUND + g
                            x_ = e.matmul(banks[U_BANK + q % 2][:, g * P:(g + 1) * P],
                                          hi_half[:, c:c + 1].to_broadcast([P, P]), identity_h, start=True, stop=True)
                        x_.then_inc(pick["spread_made"], 1)

                    def pick_rows(q):
                        e.wait_ge(pick["hot"], t * ROUNDS + q + 1)
                        if late(t * ROUNDS + q, 2):
                            e.wait_ge(pick["masked"], t * ROUNDS + q - 1)
                        for g in range(ROUND):
                            for b in range(HI_BLOCKS):
                                for n, part in enumerate(parts):
                                    x_ = e.matmul(banks[G_BANK + q % 2][:, g * P:(g + 1) * P],
                                                  row_hot[:, q % 2, b, g * P:(g + 1) * P], part[:, b, :],
                                                  start=(b == 0 and n == 0), stop=(b == HI_BLOCKS - 1 and n == 2))
                        x_.then_inc(pick["picked"], 1)

                    e.wait_ge(pick["codes_ready"], t + 1)
                    for q in range(2):
                        if not is_int(t, 0):
                            e.wait_ge(s["inner_done"], t * 2 - 1 + q)
                        spread_rows(q)
                        if late(t, 2):
                            down_tile(t - 2, par, P, q)
                    if late(t, 2):
                        down_tile(t - 2, par, P, 2)
                        down_tile(t - 2, par, P, 3)
                    if not is_int(t, 0):
                        e.wait_ge(s["silu_done"], t * 2)
                    for q in range(ROUNDS):
                        pick_rows(q)
                        if q + 2 < ROUNDS:
                            spread_rows(q + 2)
                        if late(t, 2) and q + 4 < TILES:
                            down_tile(t - 2, par, P, q + 4)
                        if q >= ROUNDS - 2 and not is_int(t, FT - 1):
                            turn(q - (ROUNDS - 2), t, par, P)
                    if is_int(t, FT - 1):
                        down(t - 1, 1 - par, P)
                        turn(0, t, par, P)

                def up(t, par, m, half, matrices=(0, 1)):
                    r = slice(half * SEQ, (half + 1) * SEQ)
                    for k in matrices:
                        hi, lo, bank, made, out_ = ((g_hi, g_lo, G_BANK, "g_made", "silu_done"),
                                                    (u_hi, u_lo, U_BANK, "u_made", "inner_done"))[k]
                        if half == 0:
                            e.wait_ge(s["w_ready"], t * 3 + k + 1)
                        if coded and half == 0:
                            e.wait_ge(pick["spread_copied" if k else "masked"], (t + 1) * ROUNDS)
                        if not coded and not is_int(t, 0):
                            e.wait_ge(s[out_], t * 2 + half - 1)
                        for c in range(KB):
                            x_ = three(e, banks[bank + half][0:m, :], hi[:, par, c, 0:m], lo[:, par, c, 0:m],
                                       x_hi[:, c, r], x_lo[:, c, r], c == 0, c == KB - 1)
                        x_.then_inc(s[made], 1)

                def down_tile(t, par, m, i):
                    if i == 0:
                        e.wait_ge(s["w_ready"], t * 3 + 3)
                    if i == 0 or (is_int(t, FT - 1) and i == TILES // 2):
                        e.wait_ge(s["h_ready"], t * 2 + (1 if is_int(t, FT - 1) and i == 0 else 2))
                    if coded and i == T_BANK - D_BANK:
                        e.wait_ge(s["w_ready"], t * 3 + (3 if isinstance(t, int) and t >= FT - 2 else 6))
                    if not (is_int(t, 0) and i < D_RING):
                        e.wait_ge(s["down_out"], t * TILES + i + 1 - D_RING)
                    r = slice(i * P, (i + 1) * P)
                    three(e, banks[D_BANK + i % D_RING][:], h_hi[0:m, par, r], h_lo[0:m, par, r], d_hi[0:m, par, :],
                          d_lo[0:m, par, :], True, True).then_inc(s["down_made"], 1)

                def down(t, par, m):
                    for i in range(TILES):
                        down_tile(t, par, m, i)

                def body(t, par, m):
                    nxt = next_of(t, par, m)
                    if coded and not nxt:
                        up(t, par, m, 0, (0,))
                        up(t, par, m, 1, (0,))
                        turn(1, t, par, m)
                        turn(2, t, par, m)
                        up(t, par, m, 0, (1,))
                        up(t, par, m, 1, (1,))
                        return
                    up(t, par, m, 0)
                    if coded:
                        turn(2, t, par, m)
                    up(t, par, m, 1)
                    if coded and nxt:
                        gather(*nxt[0:2])
                    elif not is_int(t, 0):
                        down(t - 1, 1 - par, P)

                e.wait_ge(ready, TILES)
                if coded:
                    gather(0, 0)
                tiles(e, body)
                down(FT - 1, 0, FLAST)

            def scalar(e):
                def part(k, t, par, m):
                    if coded:
                        e.wait_ge(s["w_made"], t * 3 + k + 1)
                    elif k == 0:
                        e.wait_ge(s["loaded"], (t + 1) * per_load)
                    if not (isinstance(t, int) and t < 2):
                        if k < 2:
                            e.wait_ge(s["u_made"], (t - 1) * 2)
                        else:
                            e.wait_ge(s["down_made"], (t - 1) * TILES)
                    e.activation(width(k, m, dest(k, par, 0)), source(k, par, m), ACT.Copy,
                                 scale=1.0 if coded else scale_of(k, m)).then_inc(s["w_hi_done"], 1)

                def silu(t, par, m, half):
                    e.wait_ge(s["g_made"], t * 2 + half + 1)
                    if not is_int(t, 0):
                        e.wait_ge(s["inner_done"], t * 2 + half - 1)
                    e.activation(gate[0:m, half, :], banks[G_BANK + half][0:m, :], ACT.Silu).then_inc(s["silu_done"], 1)

                def high(t, par, m, half):
                    e.wait_ge(s["inner_done"], t * 2 + half + 1)
                    if not (isinstance(t, int) and t < 2):
                        e.wait_ge(s["down_made"], (t - 1) * TILES)
                    r = slice(half * SEQ, (half + 1) * SEQ)
                    e.activation(h_hi[0:m, par, r], inner[0:m, half, :], ACT.Copy).then_inc(s["h_hi_done"], 1)

                def spread_copies(t, rounds):
                    for q in rounds:
                        e.wait_ge(pick["spread_made"], t * ROUNDS + q + 1)
                        if late(t * ROUNDS + q, 2):
                            e.wait_ge(pick["hot"], t * ROUNDS + q - 1)
                        e.activation(spread[:, q % 2, :], banks[U_BANK + q % 2][:], ACT.Copy
                                     ).then_inc(pick["spread_copied"], 1)

                def body(t, par, m):
                    nxt = next_of(t, par, m)
                    silu(t, par, m, 0)
                    if not nxt:
                        if coded:
                            silu(t, par, m, 1)
                            part(1, t, par, P)
                            part(2, t, par, P)
                        high(t, par, m, 0)
                        if not coded:
                            silu(t, par, m, 1)
                        high(t, par, m, 1)
                        return
                    if nxt and not coded:
                        part(0, *nxt)
                        part(1, *nxt)
                    elif coded:
                        part(2, t, par, P)
                    silu(t, par, m, 1)
                    high(t, par, m, 0)
                    if nxt and coded:
                        spread_copies(nxt[0], range(2))
                    high(t, par, m, 1)
                    if nxt and coded:
                        spread_copies(nxt[0], range(2, ROUNDS))
                        part(0, *nxt)
                        if not is_int(nxt[0], FT - 1):
                            part(1, *nxt)
                    elif nxt:
                        part(2, *nxt)

                e.wait_ge(ready, 1)
                if not coded:
                    e.wait_ge(s["scales_loaded"], 16)
                else:
                    spread_copies(0, range(ROUNDS))
                for k in range(2 if coded else 3):
                    part(k, 0, 0, P)
                tiles(e, body)

            def vector(e):
                def part(k, t, par, m):
                    e.wait_ge(s["w_hi_done"], t * 3 + k + 1)
                    e.scalar_tensor_tensor(out=width(k, m, dest(k, par, 1)), in0=source(k, par, m),
                                           scalar=1.0 if coded else scale_of(k, m),
                                           in1=width(k, m, dest(k, par, 0)).bitcast(F32), op0=ALU.mult,
                                           op1=ALU.subtract).then_inc(s["w_ready"], 1)

                def mult(t, par, m, half):
                    e.wait_ge(s["silu_done"], t * 2 + half + 1)
                    e.wait_ge(s["u_made"], t * 2 + half + 1)
                    if not is_int(t, 0):
                        e.wait_ge(s["h_ready"], t * 2 + half - 1)
                    e.tensor_tensor(inner[0:m, half, :], gate[0:m, half, :], banks[U_BANK + half][0:m, :],
                                    ALU.mult).then_inc(s["inner_done"], 1)

                def low(t, par, m, half):
                    r = slice(half * SEQ, (half + 1) * SEQ)
                    e.wait_ge(s["h_hi_done"], t * 2 + half + 1)
                    e.tensor_tensor(h_lo[0:m, par, r], inner[0:m, half, :], h_hi[0:m, par, r].bitcast(F32),
                                    ALU.subtract).then_inc(s["h_ready"], 1)

                def add_tile(t, i):
                    e.wait_ge(s["down_made"], t * TILES + i + 1)
                    e.tensor_tensor(acc[:, i, :], acc[:, i, :], banks[D_BANK + i % D_RING][:],
                                    ALU.add).then_inc(s["down_out"], 1)

                def add(t):
                    for i in range(TILES):
                        add_tile(t, i)

                def split_book():
                    left = book.rearrange("p a b -> p (a b)")
                    e.wait_ge(pick["book_loaded"], 16)
                    for n in range(3):
                        flat = parts[n].rearrange("p a b -> p (a b)")
                        e.tensor_copy(flat, left).then_inc(pick["book_part"], 1)
                        e.wait_ge(pick["book_part"], 2 * n + 1)
                        if n < 2:
                            e.tensor_tensor(rest[:, n, :], left, flat, ALU.subtract).then_inc(pick["book_part"], 1)
                            e.wait_ge(pick["book_part"], 2 * n + 2)
                            left = rest[:, n, :]

                def split_codes(t):
                    e.wait_ge(pick["codes_loaded"], (t + 1) * 16)
                    if not is_int(t, 0):
                        e.wait_ge(pick["reduced"], t * ROUNDS)
                    e.tensor_scalar(hi_int.bitcast(I32), codes_d.bitcast(I32), LO.bit_length() - 1, None,
                                    ALU.logical_shift_right).then_inc(pick["codes_split"], 1)
                    e.tensor_scalar(lo_int.bitcast(I32), codes_d.bitcast(I32), LO - 1, None,
                                    ALU.bitwise_and).then_inc(pick["codes_split"], 1)
                    e.wait_ge(pick["codes_split"], t * 3 + 2)
                    e.tensor_copy(hi_half, hi_int.bitcast(I32))
                    e.tensor_copy(lo_f, lo_int.bitcast(I32)).then_inc(pick["codes_split"], 1)
                    e.wait_ge(pick["codes_split"], t * 3 + 3)
                    e.tensor_tensor(entry_hot, lo_f.unsqueeze(2).to_broadcast([P, NIDX, LO]),
                                    entry_number[:].unsqueeze(1).to_broadcast([P, NIDX, LO]), ALU.is_equal
                                    ).then_inc(pick["codes_ready"], 1)

                def gather(t, par, lows=None):
                    def hot(q):
                        e.wait_ge(pick["spread_copied"], t * ROUNDS + q + 1)
                        if late(t * ROUNDS + q, 2):
                            e.wait_ge(pick["picked"], t * ROUNDS + q - 1)
                        for b in range(HI_BLOCKS):
                            x_ = e.tensor_scalar(row_hot[:, q % 2, b, :], spread[:, q % 2, :],
                                                 row_number[:, b:b + 1], None, ALU.is_equal)
                        x_.then_inc(pick["hot"], 1)

                    def take(q):
                        e.wait_ge(pick["picked"], t * ROUNDS + q + 1)
                        if late(t * ROUNDS + q, 2):
                            e.wait_ge(pick["reduced"], t * ROUNDS + q - 1)
                        e.tensor_tensor(masked_f[:, q % 2, :].rearrange("p (a b) -> p a b", b=CODE),
                                        banks[G_BANK + q % 2][:].rearrange("p (a b) -> p a b", b=CODE),
                                        entry_hot.rearrange("p a b -> p (a b)")[:, q * ROUND * LO:(q + 1) * ROUND * LO]
                                        .unsqueeze(2).to_broadcast([P, ROUND * LO, CODE]), ALU.mult
                                        ).then_inc(pick["masked"], 1)
                        e.wait_ge(pick["masked"], t * ROUNDS + q + 1)
                        w = ROUND * CODE
                        e.tensor_reduce(down_rows[:, q * w:(q + 1) * w].rearrange("p (g k) -> p g k", g=ROUND),
                                        masked_f[:, q % 2, :].rearrange("p (g l k) -> p g k l", g=ROUND, l=LO),
                                        AX.X, ALU.add).then_inc(pick["reduced"], 1)

                    for q in range(2):
                        hot(q)
                        if lows is not None:
                            lows(q)
                    for q in range(ROUNDS):
                        if late(t, 2) and q < TILES:
                            add_tile(t - 2, q)
                        take(q)
                        if q + 2 < ROUNDS:
                            hot(q + 2)
                        if q >= ROUNDS - 2 and not is_int(t, FT - 1):
                            part(q - (ROUNDS - 2), t, par, P)
                    if is_int(t, FT - 1):
                        add(t - 1)
                        part(0, t, par, P)

                def body(t, par, m):
                    nxt = next_of(t, par, m)
                    if nxt and coded:
                        split_codes(nxt[0])
                    if not nxt:
                        if coded:
                            part(1, t, par, P)
                            part(2, t, par, P)
                        for half in range(2):
                            mult(t, par, m, half)
                            low(t, par, m, half)
                        if not coded:
                            add(t - 1)
                        return
                    mult(t, par, m, 0)
                    if nxt and not coded:
                        part(0, *nxt)
                        part(1, *nxt)
                    elif coded:
                        part(2, t, par, P)
                    mult(t, par, m, 1)
                    if nxt and coded:
                        gather(nxt[0], nxt[1], lambda half: low(t, par, m, half))
                        return
                    low(t, par, m, 0)
                    low(t, par, m, 1)
                    if not is_int(t, 0):
                        add(t - 1)
                    if nxt:
                        part(2, *nxt)

                if coded:
                    e.tensor_copy(identity_h, identity[:])
                    split_book()
                    split_codes(0)
                    gather(0, 0)
                else:
                    for k in range(3):
                        part(k, 0, 0, P)
                tiles(e, body)
                add(FT - 1)

            engines["sync"].append(sync)
            engines["scalar"].append(scalar)
            engines["vector"].append(vector)
            engines["tensor"].append(tensor)
            return s["down_out"]

        if "B" in phases:
            coded_out = mlp("code", x1_ready, True)
            x2_ready = norm_stage(2, lambda e: e.wait_ge(coded_out, FT * TILES), True, "C" in phases,
                                  out if "C" not in phases else None)

        if "C" in phases:
            STEPS = 2 * HEADS
            CHUNKS = SEQ // P
            cut_r, cut_f, close = arenas("c", 14848, 13600)
            LIN = "kqvgo"
            c_stage = {k: cut_f(KB, P) for k in "kqvg"} | {"o": cut_f(D)}
            c_hi = {k: cut_r(KB, P) for k in "kqvg"} | {"o": cut_r(D)}
            c_lo = {k: cut_r(KB, P) for k in "kqvg"} | {"o": cut_r(D)}
            gate_f = cut_f(2, SEQ)
            whole = {k: cut_f(SEQ) for k in "kqv"}
            k_h, k_l, q_h, q_l = (cut_r(2, SEQ) for _ in range(4))
            v_h, v_l = cut_r(CHUNKS, P), cut_r(CHUNKS, P)
            s_f, s_h, s_l = cut_f(P_COLS), cut_r(P_COLS), cut_r(P_COLS)
            y_f = cut_f(SEQ)
            y_h, y_l = cut_r(2, SEQ), cut_r(2, SEQ)
            square, sum_sq = cut_f(SEQ), cut_f(2, SEQ)
            proj = cut_f(TILES, D)
            dec_stage, dec = cut_f(SEQ + 2), cut_f(SEQ + 2)
            rms, rms_inv, ones = cut_f(TILES), cut_f(TILES), cut_f(2)
            close()
            weight = dec[:, SEQ:SEQ + 1]
            U, O_B, V_B, S_B, Y_B = 0, 2, 3, 4, 7
            c = {k: sem(f"c_{k}") for k in
                 ("unit_made", "unit_out", "part_hi", "part_ready", "v_turned", "v_hi", "v_ready", "s_made", "s_scaled",
                  "s_hi", "s_ready", "y_made", "y_done", "y_hi", "y_ready", "o_made", "o_added",
                  "squared", "sq_done", "dec_loaded", "dec_ready", "zeroed", "rms_made", "rms_sqrt", "rms_ready",
                  "rms_used")}
            c_loaded = {k: sem(f"c_w{k}_loaded") for k in LIN}
            c_hi_done = {k: sem(f"c_w{k}_hi_done") for k in LIN}
            c_ready = {k: sem(f"c_w{k}_ready") for k in LIN}
            S_PIECES = [(0, SEQ, [(0, 0)]), (512, 384, [(1, 0)]), (896, 384, [(2, 0), (3, 256)])]

            def late(n, k):
                return not isinstance(n, int) or n >= k

            def heads(e, body):
                body(0, True, False)
                with e.Fori(1, HEADS - 1) as h:
                    body(h, False, False)
                body(HEADS - 1, False, True)

            def c_sync(e):
                qkv = qkv_w.rearrange("(c p) (h n) -> p c h n", p=P, n=3 * P)
                src = {
                    "q": lambda h: qkv[:, :, bass.ds(h, 1), 0:P].rearrange("p c a n -> p (c a) n"),
                    "k": lambda h: qkv[:, :, bass.ds(h, 1), P:2 * P].rearrange("p c a n -> p (c a) n"),
                    "v": lambda h: qkv[:, :, bass.ds(h, 1), 2 * P:3 * P].rearrange("p c a n -> p (c a) n"),
                    "g": lambda h: gate_w.rearrange("(c p) (h n) -> p c h n", p=P, n=P)[:, :, bass.ds(h, 1), :]
                    .rearrange("p c a n -> p (c a) n"),
                    "o": lambda h: out_w.rearrange("(h p) n -> p h n", p=P)[:, bass.ds(h, 1), :]
                    .rearrange("p a n -> p (a n)"),
                }

                def load(h):
                    now = h if isinstance(h, int) else e.snap(h)
                    for k in "kqvgo":
                        if late(h, 1):
                            e.wait_ge(c_ready[k], now)
                        e.wait_ge(x2_ready, 1)
                        e.sem_inc(may_load, 1)
                        e.dma_start(c_stage[k], src[k](now)).then_inc(c_loaded[k], 16)
                    if late(h, 1):
                        e.wait_ge(c["dec_ready"], now)
                        e.sem_inc(may_load, 1)
                    e.dma_start(dec_stage[:, 0:SEQ], decay[bass.ds(now, 1), :, :].rearrange("a p n -> (a p) n")
                                ).then_inc(c["dec_loaded"], 16)
                    e.dma_start(dec_stage[:, SEQ:SEQ + 1], norm_w[bass.ds(now, 1), :, :].rearrange("a p n -> (a p) n")
                                ).then_inc(c["dec_loaded"], 16)

                load(0)
                with e.Fori(1, HEADS) as h:
                    load(h)

            def c_tensor(e):
                def chunk(j):
                    return slice(j * P, (j + 1) * P)

                def unit(k, n, b, h):
                    i = "kqvg".index(k)
                    if b == 0:
                        e.wait_ge(c_ready[k], h + 1)
                    if late(n * 4 + i, 2):
                        e.wait_ge(c["unit_out"], n * 4 + i - 1)
                    r = slice(b * SEQ, (b + 1) * SEQ)
                    for a in range(KB):
                        m = three(e, banks[U + i % 2][:], c_hi[k][:, a, :], c_lo[k][:, a, :], x_hi[:, a, r],
                                  x_lo[:, a, r], a == 0, a == KB - 1)
                    m.then_inc(c["unit_made"], 1)

                def turn_values(m):
                    e.wait_ge(c["unit_out"], m * 4 + 3)
                    if late(m, 1):
                        e.wait_ge(c["v_ready"], m)
                    for j in range(CHUNKS):
                        x_ = e.transpose(banks[V_B][:, chunk(j)], whole["v"][:, chunk(j)], identity[:])
                    x_.then_inc(c["v_turned"], 1)

                def scores(m, p):
                    e.wait_ge(c["part_ready"], m * 2 + 2)
                    for i, (at, w, blocks) in enumerate(S_PIECES):
                        if late(m, 1):
                            e.wait_ge(c["s_scaled"], m * 4 + (-3, -2, 0)[i])
                        for j, col in blocks:
                            x_ = three(e, banks[S_B + i][:, col:col + SEQ - j * P], k_h[:, p, chunk(j)],
                                       k_l[:, p, chunk(j)], q_h[:, p, j * P:SEQ], q_l[:, p, j * P:SEQ], True, True)
                        x_.then_inc(c["s_made"], 1)

                def values(m):
                    e.wait_ge(c["v_ready"], m + 1)
                    e.wait_ge(c["s_ready"], m * 3 + 3)
                    if late(m, 1):
                        e.wait_ge(c["y_done"], m)
                        e.wait_ge(c["squared"], m)
                    for j in range(CHUNKS):
                        cols = slice(PT_AT[j], PT_AT[j] + (QT - j) * P)
                        x_ = three(e, banks[Y_B][:, j * P:SEQ], v_h[:, j, :], v_l[:, j, :], s_h[:, cols],
                                   s_l[:, cols], j == 0, j == CHUNKS - 1)
                    x_.then_inc(c["y_made"], 1)

                def out_tile(o, head, p, i):
                    if i == 0:
                        e.wait_ge(c["y_ready"], o + 1)
                        e.wait_ge(c_ready["o"], head + 1)
                    if late(o * 4 + i, 1):
                        e.wait_ge(c["o_added"], o * 4 + i)
                    three(e, banks[O_B][:], y_h[:, p, chunk(i)], y_l[:, p, chunk(i)], c_hi["o"], c_lo["o"],
                          True, True).then_inc(c["o_made"], 1)

                def step(h, b, units, n, attend, project):
                    m, o = n - 1, n - 2
                    if attend:
                        turn_values(m)
                    for k, i in (("k", 0), ("q", 1), ("v", 2), ("g", 3)):
                        if units:
                            unit(k, n, b, h)
                        if project:
                            out_tile(o, h - 1, b, i)
                        if attend and k == "k":
                            scores(m, 1 - b)
                        if attend and k == "v":
                            values(m)

                def body(h, first, last):
                    step(h, 0, True, h * 2, not first, not first)
                    step(h, 1, True, h * 2 + 1, True, not first)

                e.wait_ge(x2_ready, TILES)
                heads(e, body)
                step(HEADS, 0, False, STEPS, True, True)
                step(HEADS, 1, False, STEPS + 1, False, True)
                e.wait_ge(c["sq_done"], STEPS)
                for i in range(TILES):
                    x_ = e.matmul(banks[U][:, 2 * i:2 * i + 2], sum_sq[:, i // 4, chunk(i % 4)], ones,
                                  start=True, stop=True)
                x_.then_inc(c["rms_made"], 1)

            def c_scalar(e):
                def prep(k, h):
                    e.wait_ge(c_loaded[k], (h + 1) * 16)
                    if late(h, 1):
                        if k == "o":
                            e.wait_ge(c["o_made"], h * 8)
                        else:
                            e.wait_ge(c["unit_made"], (h * 2 - 1) * 4 + "kqvg".index(k) + 1)
                    e.activation(c_hi[k], c_stage[k], ACT.Copy).then_inc(c_hi_done[k], 1)

                def unit(k, n, b):
                    i = "kqvg".index(k)
                    e.wait_ge(c["unit_made"], n * 4 + i + 1)
                    dst = gate_f[:, b, :] if k == "g" else whole[k]
                    if k in "kq" and late(n, 1):
                        e.wait_ge(c["part_ready"], n * 2 - (1 if k == "k" else 0))
                    if k == "v" and late(n, 1):
                        e.wait_ge(c["v_turned"], n)
                    if k == "g" and late(n, 2):
                        e.wait_ge(c["y_done"], n - 1)
                    e.activation(dst, banks[U + i % 2][:], ACT.Sigmoid if k == "g" else ACT.Silu
                                 ).then_inc(c["unit_out"], 1)
                    if k in "kq":
                        hi = {"k": k_h, "q": q_h}[k][:, b, :]
                        e.wait_ge(c["unit_out"], n * 4 + i + 1)
                        if late(n, 2):
                            e.wait_ge(c["s_made"], (n - 1) * 3)
                        e.activation(hi, dst, ACT.Copy).then_inc(c["part_hi"], 1)

                def values_high(m):
                    e.wait_ge(c["v_turned"], m + 1)
                    if late(m, 1):
                        e.wait_ge(c["y_made"], m)
                    e.activation(v_h, banks[V_B][:].rearrange("p (a b) -> p a b", a=CHUNKS),
                                 ACT.Copy).then_inc(c["v_hi"], 1)

                def scores_high(m):
                    for i, (at, w, blocks) in enumerate(S_PIECES):
                        e.wait_ge(c["s_scaled"], m * 4 + (1, 2, 4)[i])
                        if i == 0 and late(m, 1):
                            e.wait_ge(c["y_made"], m)
                        e.activation(s_h[:, at:at + w], s_f[:, at:at + w], ACT.Copy).then_inc(c["s_hi"], 1)

                def squares(m):
                    e.wait_ge(c["y_made"], m + 1)
                    if late(m, 1):
                        e.wait_ge(c["sq_done"], m)
                    e.activation(square, banks[Y_B][:], ACT.Square).then_inc(c["squared"], 1)

                def out_high(m, p):
                    e.wait_ge(c["y_done"], m + 1)
                    if late(m, 2):
                        e.wait_ge(c["o_made"], (m - 1) * 4)
                    e.activation(y_h[:, p, :], y_f, ACT.Copy).then_inc(c["y_hi"], 1)

                def step(h, b, n, units, attend, first, last):
                    m = n - 1
                    if attend:
                        values_high(m)
                    if units:
                        unit("k", n, b)
                        if b == 0 and not first:
                            prep("g", h)
                    if attend:
                        scores_high(m)
                    if units:
                        unit("q", n, b)
                        if b == 1 and not last:
                            prep("k", h + 1)
                        unit("v", n, b)
                        if b == 1 and not last:
                            prep("q", h + 1)
                    if attend:
                        squares(m)
                        out_high(m, 1 - b)
                    if units:
                        if b == 1 and not last:
                            prep("v", h + 1)
                        unit("g", n, b)
                        if b == 1:
                            prep("o", h)

                def body(h, first, last):
                    step(h, 0, h * 2, True, not first, first, last)
                    step(h, 1, h * 2 + 1, True, True, first, last)

                e.wait_ge(x2_ready, 1)
                for k in "kqvg":
                    prep(k, 0)
                heads(e, body)
                step(HEADS, 0, STEPS, False, True, False, True)
                e.wait_ge(c["rms_made"], 1)
                e.activation(rms, banks[U][:, 0:2 * TILES:2], ACT.Sqrt, bias=eps[:],
                             scale=1.0 / (HEADS * P)).then_inc(c["rms_sqrt"], 1)

            def c_vector(e):
                def low(k, n, b):
                    i = "kq".index(k)
                    hi = {"k": k_h, "q": q_h}[k][:, b, :]
                    lo = {"k": k_l, "q": q_l}[k][:, b, :]
                    e.wait_ge(c["part_hi"], n * 2 + i + 1)
                    e.tensor_tensor(lo, whole[k], hi.bitcast(F32), ALU.subtract).then_inc(c["part_ready"], 1)

                def values_low(m):
                    e.wait_ge(c["v_hi"], m + 1)
                    e.tensor_tensor(v_l, banks[V_B][:].rearrange("p (a b) -> p a b", a=CHUNKS), v_h.bitcast(F32),
                                    ALU.subtract).then_inc(c["v_ready"], 1)

                def scores_scaled(m):
                    for i, (at, w, blocks) in enumerate(S_PIECES):
                        e.wait_ge(c["s_made"], m * 3 + i + 1)
                        if i == 0 and late(m, 1):
                            e.wait_ge(c["s_ready"], m * 3)
                        for j, col in blocks:
                            n = SEQ - j * P
                            e.tensor_tensor(s_f[:, at + col:at + col + n], banks[S_B + i][:, col:col + n],
                                            dec[:, 0:n], ALU.mult).then_inc(c["s_scaled"], 1)

                def scores_low(m):
                    for i, (at, w, blocks) in enumerate(S_PIECES):
                        e.wait_ge(c["s_hi"], m * 3 + i + 1)
                        e.tensor_tensor(s_l[:, at:at + w], s_f[:, at:at + w], s_h[:, at:at + w].bitcast(F32),
                                        ALU.subtract).then_inc(c["s_ready"], 1)

                def outputs(m, p):
                    e.wait_ge(c["squared"], m + 1)
                    e.wait_ge(c["unit_out"], m * 4 + 4)
                    e.scalar_tensor_tensor(out=y_f, in0=banks[Y_B][:], scalar=weight, in1=gate_f[:, p, :],
                                           op0=ALU.mult, op1=ALU.mult).then_inc(c["y_done"], 1)
                    e.wait_ge(c["y_hi"], m + 1)
                    e.tensor_tensor(y_l[:, p, :], y_f, y_h[:, p, :].bitcast(F32),
                                    ALU.subtract).then_inc(c["y_ready"], 1)

                def add(o, p, i):
                    e.wait_ge(c["o_made"], o * 4 + i + 1)
                    t = p * 4 + i
                    e.tensor_tensor(proj[:, t, :], proj[:, t, :], banks[O_B][:], ALU.add).then_inc(c["o_added"], 1)

                def step(h, b, n, units, attend, project):
                    m, o = n - 1, n - 2
                    if attend:
                        values_low(m)
                    if units:
                        low("k", n, b)
                    if project:
                        add(o, b, 0)
                    if attend:
                        e.wait_ge(c["dec_ready"], h + b)
                        scores_scaled(m)
                    if attend:
                        scores_low(m)
                    if project:
                        add(o, b, 1)
                    if units:
                        low("q", n, b)
                    if project:
                        add(o, b, 2)
                    if attend:
                        outputs(m, 1 - b)
                    if project:
                        add(o, b, 3)

                def body(h, first, last):
                    step(h, 0, h * 2, True, not first, not first)
                    step(h, 1, h * 2 + 1, True, True, not first)

                e.wait_ge(x2_ready, 1)
                e.wait_ge(c["zeroed"], 1)
                heads(e, body)
                step(HEADS, 0, STEPS, False, True, True)
                step(HEADS, 1, STEPS + 1, False, False, True)
                e.wait_ge(c["rms_sqrt"], 1)
                e.reciprocal(rms_inv, rms).then_inc(c["rms_ready"], 1)
                e.wait_ge(c["rms_ready"], 1)
                e.wait_ge(c["o_added"], STEPS * 4)
                for t in range(TILES):
                    e.scalar_tensor_tensor(out=acc[:, t, :], in0=proj[:, t, :], scalar=rms_inv[:, t:t + 1],
                                           in1=acc[:, t, :], op0=ALU.mult, op1=ALU.add).then_inc(c["rms_used"], 1)

            def c_gpsimd(e):
                def low(k, h):
                    e.wait_ge(c_hi_done[k], h + 1)
                    e.tensor_tensor(c_lo[k], c_stage[k], c_hi[k].bitcast(F32), ALU.subtract).then_inc(c_ready[k], 1)

                def decays(h):
                    e.wait_ge(c["dec_loaded"], (h + 1) * 32)
                    if late(h, 1):
                        e.wait_ge(c["y_done"], h * 2)
                    e.tensor_tensor(dec[:, 0:SEQ + 1], dec_stage[:, 0:SEQ + 1], ones[:, 0:1].to_broadcast([P, SEQ + 1]),
                                    ALU.mult).then_inc(c["dec_ready"], 1)

                def square_sum(m, p):
                    e.wait_ge(c["squared"], m + 1)
                    e.tensor_tensor(sum_sq[:, p, :], sum_sq[:, p, :], square, ALU.add).then_inc(c["sq_done"], 1)

                def body(h, first, last):
                    if not first:
                        low("g", h)
                        square_sum(h * 2 - 1, 1)
                    decays(h)
                    if not last:
                        low("k", h + 1)
                        low("q", h + 1)
                    square_sum(h * 2, 0)
                    if not last:
                        low("v", h + 1)
                    low("o", h)

                e.wait_ge(x2_ready, 1)
                e.memset(proj, 0.0)
                e.memset(sum_sq, 0.0)
                e.memset(ones, 1.0).then_inc(c["zeroed"], 1)
                e.wait_ge(c["zeroed"], 1)
                for k in "kqvg":
                    low(k, 0)
                heads(e, body)
                square_sum(STEPS - 1, 1)

            engines["sync"].append(c_sync)
            engines["scalar"].append(c_scalar)
            engines["vector"].append(c_vector)
            engines["tensor"].append(c_tensor)
            engines["gpsimd"].append(c_gpsimd)
            x3_ready = norm_stage(3, lambda e: e.wait_ge(c["rms_used"], TILES), True, "D" in phases,
                                  out if "D" not in phases else None)

        if "D" in phases:
            whole_out = mlp("int", x3_ready, False)
            norm_stage(4, lambda e: e.wait_ge(whole_out, FT * TILES), True, False, out)

        @block.sync
        def _(e):
            for f in engines["sync"]:
                f(e)

        @block.gpsimd
        def _(e):
            for f in engines["gpsimd"]:
                f(e)

        @block.scalar
        def _(e):
            for f in engines["scalar"]:
                f(e)

        @block.vector
        def _(e):
            for f in engines["vector"]:
                f(e)

        @block.tensor
        def _(e):
            for f in engines["tensor"]:
                f(e)


def host_arrays(inputs):
    import numpy as np
    a = {k.split("_", 2)[2] if "ffn" not in k else k.replace("_ffn_", "_"): np.asarray(v) for k, v in inputs.items()}
    pad = FT * P - FF

    def tiles_of_rows(i):
        return np.pad(i, ((0, pad), (0, 0))).reshape(FT, P, D // CODE)

    down = np.pad(a["L0_idx_down"], ((0, 0), (0, pad // CODE))).reshape(KB, P, FT, P // CODE)
    idx = np.stack([tiles_of_rows(a["L0_idx_gate"]), tiles_of_rows(a["L0_idx_up"]),
                    down.transpose(2, 1, 0, 3).reshape(FT, P, KB * P // CODE)], 1)
    slope = (np.float32(1.0 / 2.0 ** (8.0 / HEADS)) ** (np.arange(HEADS, dtype=np.float32) + 1)
             * np.float32(1.0 - 1 / (31 + 1e-05) + 1e-05)).astype(np.float64)
    gap = np.arange(SEQ, dtype=np.float64)[None, :] - np.arange(P, dtype=np.float64)[:, None]
    decay = np.where(gap >= 0, np.exp(-slope[:, None, None] * np.maximum(gap, 0)), 0).astype(np.float32)
    return {
        "x": a["hidden_states"].reshape(TOK, D), "w_q": a["w_q"], "w_k": a["w_k"], "w_v": a["w_v"],
        "w_o": a["w_o"], "codebook": a["L0_codebook"], "idx": np.ascontiguousarray(idx),
        "qkv_w": np.ascontiguousarray(a["qkv_w"].T), "out_w": np.ascontiguousarray(a["out_w"].T),
        "gate_w": np.ascontiguousarray(a["gate_w"].T), "norm_w": a["norm_w"].reshape(HEADS, P, 1),
        "decay": decay,
        "wf_gate": np.ascontiguousarray(a["L1_w_gate"].T), "wf_up": np.ascontiguousarray(a["L1_w_up"].T),
        "wf_down": np.ascontiguousarray(a["L1_w_down"].T),
        "scales": np.stack([a["L1_scale_gate"], a["L1_scale_up"], a["L1_scale_down"]]).reshape(1, 3),
    }


_INS = ["x", "w_q", "w_k", "w_v", "w_o", "codebook", "idx", "qkv_w", "out_w", "gate_w", "norm_w", "decay",
        "wf_gate", "wf_up", "wf_down", "scales"]


def kernel(**inputs):
    import numpy as _np
    import concourse.bacc as _bacc
    from concourse import mybir as _mybir
    from concourse.bass_utils import run_bass_kernel_spmd as _run

    nc = _bacc.Bacc("TRN2", target_bir_lowering=False, num_devices=1)
    laid = host_arrays(inputs)
    arrays, args = {}, []
    for name in _INS:
        a = _np.ascontiguousarray(laid[name])
        arrays[f"in_{name}_dram"] = a
        args.append(nc.dram_tensor(f"in_{name}_dram", a.shape, _mybir.dt.from_np(a.dtype), kind="ExternalInput").ap())
    out = nc.dram_tensor("out_0_dram", (TOK, D), F32, kind="ExternalOutput").ap()
    weights = nc.dram_tensor("coded_weights_dram", (2 * FT, P, D), F32, kind="Internal").ap()
    build(nc, *args, out, weights)
    r = _run(nc, [arrays], core_ids=[0])
    return r.results[0]["out_0_dram"].reshape(TOK // SEQ, SEQ, D)
```

```python
from contextlib import ExitStack

import concourse.bass as bass
from concourse import mybir

F32 = mybir.dt.float32
F32R = mybir.dt.float32r
I32 = mybir.dt.int32
BF16 = mybir.dt.bfloat16
F16 = mybir.dt.float16
AX = mybir.AxisListType
U32 = mybir.dt.uint32
ALU = mybir.AluOpType
ACT = mybir.ActivationFunctionType

P = 128
TOK = 1024
SEQ = 512
TILES = TOK // P
D = 512
KB = D // P
HEADS = 32
KV_HEADS = 8
GROUP = HEADS // KV_HEADS
FF = 1376
FT = (FF + P - 1) // P
FLAST = FF - (FT - 1) * P
CODE = 8
NEG = -3.0e38
EPS = 1e-5
SCALE = float(P) ** -0.5
QT = SEQ // P
P_AT = [0, 128, 384, 768]
P_COLS = 1280
PIECES = [(0, [(0, q) for q in range(4)]),
          (512, [(1, q) for q in range(1, 4)]),
          (896, [(2, 2), (2, 3), (3, 3)])]
PT_AT = [0, 512, 896, 1152]
S_AT = [(2, 256), (2, 0), (1, 0), (0, 0)]


def attention_plan(first, last):
    plan = [("K", 0)]
    if not first:
        plan += [("T", 7, 0), ("T", 7, 1)]
    plan += [("K", 1)]
    if not first:
        plan += [("PV", 7, 0), ("T", 7, 2)]
    plan += [("Q", 0)]
    if not first:
        plan += [("PV", 7, 1), ("PV", 7, 2)]
    plan += [("V", 0), ("V", 1), ("X", 0)]
    old = [] if first else [[("O", 1, t)] for t in range(4)]
    fills = {s: [("Q", s + 1)] + (old[s] if s < len(old) else []) for s in range(7)}
    fills[0].append(("X", 1))
    fills[4] = [("Q", 5), ("Q", 6)]
    fills[5] = [("Q", 7), ("O", 0, 0)]
    fills[6] = [("O", 0, 1), ("O", 0, 2)]
    fills[7] = [("O", 0, 3)]
    mid = {s: [] for s in range(8)}
    end = {s: [] for s in range(8)}
    end[3] += [("W", "o", 0)]
    end[3] += [("W", "o", 1)]
    end[4] += [("W", "o", 2)]
    end[4] += [("W", "o", 3)]
    if not last:
        end[1], end[2] = [("W", "k", 0)], [("W", "v", 0)]
        end[6] += [("W", "q", 0)]
        end[6] += [("W", "q", 1)]
        end[7] += [("W", "q", 2)]
        end[7] += [("W", "q", 3)]
    for s in range(8):
        f = fills[s]
        plan.append(("S", s))
        if s:
            plan += [("T", s - 1, 0), ("T", s - 1, 1)]
        plan += f[:1]
        if s == 7:
            plan.append(("T", s - 1, 2))
        plan.append(("E", s))
        plan += mid[s]
        if s:
            plan.append(("PV", s - 1, 0))
            if s < 7:
                plan.append(("T", s - 1, 2))
            plan.append(("PV", s - 1, 1))
        plan.append(("N", s))
        plan += f[1:2]
        if s:
            plan += [("PV", s - 1, 2)]
        plan += f[2:]
        plan += end[s]
    return plan


def attention_tail():
    return [("T", 7, 0), ("T", 7, 1), ("PV", 7, 0), ("T", 7, 2), ("PV", 7, 1), ("PV", 7, 2)] \
        + [("O", 1, t) for t in range(4)]


class Counts:

    def __init__(self):
        plan = attention_plan(False, False)
        self.per = {k: self.tally(plan, k) for k in ("unit", "T", "PV", "S")}
        self.first = {k: self.tally(attention_plan(True, False), k) for k in self.per}

    @staticmethod
    def kind(e):
        return "unit" if e[0] in "KQVXO" else e[0]

    def tally(self, plan, kind):
        return sum(1 for e in plan if self.kind(e) == kind and (kind != "PV" or e[2] == 2))

    def base(self, g, kind):
        if isinstance(g, int) and g == 0:
            return 0
        return g * self.per[kind] + (self.first[kind] - self.per[kind])


def build(nc, x, w_q, w_k, w_v, w_o, codebook, idx, qkv_w, out_w, gate_w, norm_w, decay,
          wf_gate, wf_up, wf_down, scales, out, wdram, phases="ABCD"):
    ctx = ExitStack()
    with ctx:
        def sb(name, shape, dt=F32):
            return ctx.enter_context(nc.sbuf_tensor(name, shape, dt))

        def sem(name):
            return ctx.enter_context(nc.semaphore(name))

        acc = sb("acc", [P, TILES, D])
        x_hi = sb("x_hi", [P, KB, TOK], F32R)
        x_lo = sb("x_lo", [P, KB, TOK], F32R)
        identity = sb("identity", [P, P])
        mask = sb("mask", [P, SEQ])
        eps = sb("eps", [P, 1])
        pace = sb("pace", [1, 1])
        pool_pace = sb("pool_pace", [1, 2])
        scale_sb = sb("scale_sb", [P, 3])
        LO = 16
        HI_BLOCKS = codebook.shape[0] // LO // P
        row_number = sb("row_number", [P, HI_BLOCKS])
        entry_number = sb("entry_number", [P, LO])
        codes_at = sb("codes_at", [P, 2, D // CODE], U32)
        gathered_rows = sb("gathered_rows", [P, 2, D])
        stats = sb("stats", [P, TILES, 6])
        mean_var = sb("mean_var", [P, TILES, 2])
        deviation = sb("deviation", [P, TILES])
        rstd = sb("rstd", [P, TILES])
        banks = [ctx.enter_context(nc.psum_tensor(f"bank{i}", [P, 512], F32)) for i in range(8)]

        def arenas(name, r_cols, f_cols, h_cols=0):
            stack = ExitStack()

            def cutter(arena, total):
                at = [0]

                def cut(*shape):
                    n = 1
                    for s in shape:
                        n *= s
                    assert at[0] + n <= total, (name, at[0] + n, total)
                    view = arena[:, at[0]:at[0] + n]
                    at[0] += n
                    if len(shape) == 2:
                        view = view.rearrange("p (a b) -> p a b", a=shape[0])
                    elif len(shape) == 3:
                        view = view.rearrange("p (a b c) -> p a b c", a=shape[0], b=shape[1])
                    return view
                return cut
            rounded = stack.enter_context(nc.sbuf_tensor(f"rounded_{name}", [P, r_cols], F32R))
            plain = stack.enter_context(nc.sbuf_tensor(f"plain_{name}", [P, f_cols], F32))
            if h_cols:
                halves = [stack.enter_context(nc.sbuf_tensor(f"{t}_{name}", [P, h_cols], dt))
                          for t, dt in (("bf16", BF16), ("fp16", F16))]
                return cutter(rounded, r_cols), cutter(plain, f_cols), [cutter(h, h_cols) for h in halves], stack.close
            return cutter(rounded, r_cols), cutter(plain, f_cols), stack.close

        consts_ready = sem("consts_ready")
        may_load = sem("may_load")
        x_loaded = sem("x_loaded")
        block = ctx.enter_context(nc.Block())

        early = {}
        engines = {k: [] for k in ("sync", "gpsimd", "scalar", "vector", "tensor")}

        def norm_stage(n, finish, finished, normalise, turn, turn_bank=0, split_turns=False, store=None):
            HALF = TILES // 2
            TURN_RING = 4
            halves = [range(HALF), range(HALF, TILES)]
            if normalise:
                stat, aggregated, dev, rs, normed = (sem(f"{k}{n}") for k in ("stat", "aggregated", "dev", "rs", "normed"))
            if turn:
                turned, hi, lo = (sem(f"{k}{n}") for k in ("turned", "x_hi_done", "x_ready"))

            def low_of(e, i):
                e.wait_ge(hi, i + 1)
                at = slice(i * P, (i + 1) * P)
                e.tensor_tensor(x_lo[:, :, at], banks[turn_bank + i % TURN_RING][:].rearrange("p (a b) -> p a b", a=KB),
                                x_hi[:, :, at].bitcast(F32), ALU.subtract).then_inc(lo, 1)

            def lows_of_second_half(e):
                for i in halves[1]:
                    low_of(e, i)

            def vector(e):
                def stats_of(i):
                    finished(e, i)
                    e.bn_stats(stats[:, i, :], acc[:, i, :]).then_inc(stat, 1)

                def aggregate(half):
                    for i in halves[half]:
                        e.wait_ge(stat, i + 1)
                        e.bn_aggr(mean_var[:, i, :], stats[:, i, :]).then_inc(aggregated, 1)

                def normalised(half):
                    at = slice(half * HALF, (half + 1) * HALF)
                    e.wait_ge(dev, half + 1)
                    e.reciprocal(rstd[:, at], deviation[:, at]).then_inc(rs, 1)
                    e.wait_ge(rs, half + 1)
                    for i in halves[half]:
                        e.tensor_scalar(acc[:, i, :], acc[:, i, :], mean_var[:, i, 0:1], rstd[:, i:i + 1],
                                        ALU.subtract, ALU.mult).then_inc(normed, 1)

                def low(i):
                    if turn:
                        low_of(e, i)

                if normalise:
                    for i in range(HALF + 1):
                        finish(e, i)
                        if i:
                            stats_of(i - 1)
                    aggregate(0)
                    finish(e, HALF + 1)
                    stats_of(HALF)
                    normalised(0)
                    for i in range(HALF + 2, TILES):
                        finish(e, i)
                        stats_of(i - 1)
                    stats_of(TILES - 1)
                    low(0)
                    aggregate(1)
                    for i in range(1, HALF):
                        low(i)
                    normalised(1)
                else:
                    for i in halves[0]:
                        low(i)
                if turn and not split_turns:
                    lows_of_second_half(e)

            def highs(e, half):
                for i in halves[half]:
                    e.wait_ge(turned, i + 1)
                    at = slice(i * P, (i + 1) * P)
                    e.activation(x_hi[:, :, at], banks[turn_bank + i % TURN_RING][:].rearrange("p (a b) -> p a b", a=KB),
                                 ACT.Copy).then_inc(hi, 1)

            def scalar(e):
                for half in range(2):
                    if normalise:
                        at = slice(half * HALF, (half + 1) * HALF)
                        e.wait_ge(aggregated, (half + 1) * HALF)
                        e.activation(deviation[:, at], mean_var[:, at, 1], ACT.Sqrt, bias=eps[:]).then_inc(dev, 1)
                        if half == 0 and n in early:
                            early[n](e)
                    if turn and not (half and split_turns):
                        highs(e, half)

            def turns(e, half):
                for i in halves[half]:
                    if normalise:
                        e.wait_ge(normed, i + 1)
                    if i >= TURN_RING:
                        e.wait_ge(lo, i + 1 - TURN_RING)
                    for c in range(KB):
                        t = e.transpose(banks[turn_bank + i % TURN_RING][:, c * P:(c + 1) * P], acc[:, i, c * P:(c + 1) * P],
                                        identity[:])
                    t.then_inc(turned, 1)

            def tensor(e):
                if not turn:
                    return
                if not normalise:
                    e.wait_ge(consts_ready, 1)
                    e.wait_ge(x_loaded, 16)
                turns(e, 0)
                if not split_turns:
                    turns(e, 1)

            def sync(e):
                if store is not None:
                    stored = sem("stored")
                    for i in range(TILES):
                        e.wait_ge(normed, i + 1)
                        e.dma_start(store[i * P:(i + 1) * P, :], acc[:, i, :]).then_inc(stored, 16)
                    e.wait_ge(stored, 16 * TILES)

            def second_half(e, engine):
                if split_turns:
                    if engine == "tensor":
                        turns(e, 1)
                    elif engine == "scalar":
                        highs(e, 1)
                    else:
                        lows_of_second_half(e)
                if engine == "tensor":
                    e.wait_ge(lo, TILES)

            engines["vector"].append(vector)
            engines["scalar"].append(scalar)
            engines["tensor"].append(tensor)
            engines["sync"].append(sync)
            return (lo, second_half) if turn else (None, None)

        idx_loaded = [sem(f"idx_loaded{k}") for k in range(2)]

        first_idx_loaded = [sem(f"first_idx_loaded{k}") for k in range(2)]

        def load_idx(e, k, t, loaded):
            e.dma_start(codes_at[:, k, :].bitcast(I32), idx[bass.ts(t, 1), k, :, :].rearrange("a p c -> (a p) c")
                        ).then_inc(loaded[k], 16)

        def start_sync(e):
            if "B" in phases:
                load_idx(e, 0, 0, first_idx_loaded)
                load_idx(e, 1, 0, first_idx_loaded)
            e.dma_start(acc[:], x.rearrange("(t p) d -> p t d", p=P)).then_inc(x_loaded, 16)

        const_step = sem("const_step")

        zeroed = sem("zeroed")

        def start_vector(e):
            e.memset(identity[:], 0.0).then_inc(zeroed, 1)
            e.memset(mask[:], 0.0).then_inc(zeroed, 1)
            e.memset(eps[:], EPS).then_inc(zeroed, 1)
            e.memset(stats[:, 0, 0:1], 0.0).then_inc(zeroed, 1)

        def start_gpsimd(e):
            e.wait_ge(zeroed, 4)
            e.affine_select(out=identity[:], in_=identity[:], compare_op=ALU.not_equal, fill=1.0, base=0,
                            pattern=[[-1, P]], channel_multiplier=1).then_inc(const_step, 1)
            e.affine_select(out=mask[:, SEQ - P:SEQ], in_=mask[:, SEQ - P:SEQ], compare_op=ALU.is_ge, fill=NEG,
                            base=0, pattern=[[-1, P]], channel_multiplier=1).then_inc(const_step, 1)
            e.iota(row_number[:], pattern=[[P, HI_BLOCKS]], base=0, channel_multiplier=1,
                   allow_small_or_imprecise_dtypes=True).then_inc(const_step, 1)
            e.iota(entry_number[:], pattern=[[1, LO]], base=0, channel_multiplier=0,
                   allow_small_or_imprecise_dtypes=True).then_inc(const_step, 1)
            e.wait_ge(const_step, 4)
            e.memset(stats[:, 0, 0:1], 0.0).then_inc(consts_ready, 1)

        engines["sync"].append(start_sync)
        engines["gpsimd"].append(start_gpsimd)
        engines["vector"].append(start_vector)

        x0_ready, _ = norm_stage(0, None, None, False, True)

        def three(e, out_ap, l_hi, l_lo, r_hi, r_lo, start, stop):
            e.matmul(out_ap, l_hi, r_hi, start=start, stop=False)
            e.matmul(out_ap, l_hi, r_lo, start=False, stop=False)
            return e.matmul(out_ap, l_lo, r_hi, start=False, stop=stop)

        if "A" in phases:
            cut_r, cut_f, close = arenas("a", 27136, 8736)
            W_SHAPE = {"k": (KB, P), "v": (KB, P), "q": (KB, GROUP * P), "o": (GROUP, D)}
            stage = {k: cut_f(*s) for k, s in W_SHAPE.items()}
            w_hi = {k: cut_r(*s) for k, s in W_SHAPE.items()}
            w_lo = {k: cut_r(*s) for k, s in W_SHAPE.items()}
            k_hi, k_lo = cut_r(TOK), cut_r(TOK)
            v_hi, v_lo = cut_r(TILES, P), cut_r(TILES, P)
            q_hi, q_lo = cut_r(2, SEQ), cut_r(2, SEQ)
            pt_hi, pt_lo = cut_r(P_COLS), cut_r(P_COLS)
            at_hi, at_lo = cut_r(2, GROUP, SEQ), cut_r(2, GROUP, SEQ)
            probs = cut_f(2, P_COLS)
            v_whole = cut_f(2, SEQ)
            row_max, neg_max, row_sum, row_inv = (cut_f(2, QT) for _ in range(4))
            close()
            W_PARTS = {"k": 1, "v": 1, "q": KB, "o": GROUP}

            def w_part(w, k, part):
                return w if W_PARTS[k] == 1 else w[:, part, :]

            w_src = {
                "k": lambda g: w_k.rearrange("(c p) n -> p c n", p=P)[:, :, bass.ts(g, P)],
                "v": lambda g: w_v.rearrange("(c p) n -> p c n", p=P)[:, :, bass.ts(g, P)],
                "q": lambda g: w_q.rearrange("(c p) n -> p c n", p=P)[:, :, bass.ts(g, GROUP * P)],
                "o": lambda g: w_o.rearrange("(c p) n -> p c n", p=P)[:, bass.ts(g, GROUP), :],
            }
            cnt = Counts()
            w_loaded = {k: sem(f"w{k}_loaded") for k in "kvqo"}
            w_hi_done = {k: sem(f"w{k}_hi_done") for k in "kvqo"}
            w_ready = {k: sem(f"w{k}_ready") for k in "kvqo"}
            unit_made, unit_hi, unit_out = sem("unit_made"), sem("unit_hi"), sem("unit_out")
            scores_made, masked, neg_done = sem("scores_made"), sem("masked"), sem("neg_done")
            exp_done, inv_done, probs_ready = sem("exp_done"), sem("inv_done"), sem("probs_ready")
            t_made, t_hi, t_out = sem("t_made"), sem("t_hi"), sem("t_out")
            pv_made, pv_hi, pv_out = sem("pv_made"), sem("pv_hi"), sem("pv_out")
            S_BANK, T_BANK, O_BANK, U_BANK = 0, 3, 5, 6

            def groups(e, body):
                body(0, True, False)
                with e.Fori(1, KV_HEADS - 1) as g:
                    body(g, False, False)
                body(KV_HEADS - 1, False, True)

            def where(g, first, last, tail=False):
                plan = attention_tail() if tail else attention_plan(first, last)
                base = {k: cnt.base(g, k) for k in ("unit", "T", "PV", "S")}
                seen = {k: 0 for k in base}
                last_q = 0
                for n, e in enumerate(plan):
                    k = cnt.kind(e)
                    if k in seen and (k != "PV" or e[2] == 2):
                        seen[k] += 1
                    yield e, seen, base, plan, n

            def unit_number(plan, base, what):
                n = 0
                for e in plan:
                    if cnt.kind(e) == "unit":
                        n += 1
                    if e == what:
                        return base["unit"] + n
                raise KeyError(what)

            def a_sync(e):
                def load(k, g):
                    e.dma_start(stage[k], w_src[k](g)).then_inc(w_loaded[k], 16)
                for k in "kvqo":
                    load(k, 0)

                def body(g, first, last):
                    if last:
                        return
                    for k in "kvqo":
                        e.wait_ge(w_ready[k], (g + 1) * W_PARTS[k])
                        load(k, g + 1)
                body(0, True, False)
                with e.Fori(1, KV_HEADS - 1) as g:
                    body(g, False, False)

            def a_tensor(e):
                def product(kind, bank, item, waits=None):
                    if kind == "K":
                        r = slice(item[1] * SEQ, (item[1] + 1) * SEQ)
                        for c in range(KB):
                            m = three(e, bank[:], w_hi["k"][:, c, :], w_lo["k"][:, c, :], x_hi[:, c, r],
                                      x_lo[:, c, r], c == 0, c == KB - 1)
                    elif kind == "Q":
                        b, h = divmod(item[1], GROUP)
                        r = slice(b * SEQ, (b + 1) * SEQ)
                        for c in range(KB):
                            m = three(e, bank[:], w_hi["q"][:, c, h * P:(h + 1) * P],
                                      w_lo["q"][:, c, h * P:(h + 1) * P], x_hi[:, c, r], x_lo[:, c, r],
                                      c == 0, c == KB - 1)
                    elif kind == "V":
                        r = slice(item[1] * SEQ, (item[1] + 1) * SEQ)
                        for c in range(KB):
                            m = three(e, bank[:], w_hi["v"][:, c, :], w_lo["v"][:, c, :], x_hi[:, c, r],
                                      x_lo[:, c, r], c == 0, c == KB - 1)
                    elif kind == "X":
                        for i in range(4):
                            r = slice(i * P, (i + 1) * P)
                            m = e.transpose(bank[:, r], v_whole[:, item[1], r], identity[:])
                    else:
                        b, t = item[1:]
                        r = slice(t * P, (t + 1) * P)
                        for h in range(GROUP):
                            m = three(e, bank[:], at_hi[:, b, h, r], at_lo[:, b, h, r], w_hi["o"][:, h, :],
                                      w_lo["o"][:, h, :], h == 0, h == GROUP - 1)
                    return m

                def run(g, first, last, tail=False):
                    for item, seen, base, plan, n in where(g, first, last, tail):
                        k = item[0]
                        if cnt.kind(item) == "unit":
                            u = seen["unit"]
                            if not (first and u <= 2):
                                e.wait_ge(unit_out, base["unit"] + u - 2)
                            if k == "K" and item[1] == 0:
                                e.wait_ge(w_ready["k"], g + 1)
                            if k == "V" and item[1] == 0:
                                e.wait_ge(w_ready["v"], g + 1)
                            if k == "Q" and item[1] == 0:
                                e.wait_ge(w_ready["q"], (g + 1) * W_PARTS["q"])
                            if k == "X":
                                e.wait_ge(unit_out, unit_number(plan, base, ("V", item[1])))
                            if k == "O" and item[1] == 0 and item[2] == 0:
                                e.wait_ge(w_ready["o"], (g + 1) * W_PARTS["o"])
                                e.wait_ge(pv_out, g * 8 + 4)
                            if k == "O" and item[1] == 1 and item[2] == 0:
                                e.wait_ge(pv_out, g * 8)
                            product(k, banks[U_BANK + (u - 1) % 2], item).then_inc(unit_made, 1)
                        elif k == "S":
                            s = item[1]
                            b = s // GROUP
                            e.wait_ge(unit_out, unit_number(plan, base, ("Q", s)))
                            if not (first and s == 0):
                                e.wait_ge(masked, (g * 8 + s) * QT)
                            for q in range(QT):
                                bank, at = S_AT[q]
                                r = slice(q * P, (q + 1) * P)
                                ks = slice(b * SEQ, b * SEQ + (q + 1) * P)
                                m = three(e, banks[S_BANK + bank][:, at:at + (q + 1) * P], q_hi[:, s % 2, r],
                                          q_lo[:, s % 2, r], k_hi[:, ks], k_lo[:, ks], True, True)
                            m.then_inc(scores_made, 1)
                        elif k == "T":
                            s, piece = item[1:]
                            G = g - 1 if s == 7 and not isinstance(g, int) else (g - 1 if s == 7 else g)
                            if piece == 0:
                                e.wait_ge(probs_ready, G * 8 + s + 1)
                            tn = (G * 8 + s) * 3 + piece
                            par = (s + piece) % 2
                            if not (isinstance(G, int) and G == 0 and s * 3 + piece < 2):
                                e.wait_ge(t_out, tn - 1)
                            for i, (j, q) in enumerate(PIECES[piece][1]):
                                m = e.transpose(banks[T_BANK + (3 * s + piece) % 2][:, i * P:(i + 1) * P],
                                                probs[:, s % 2, P_AT[q] + j * P:P_AT[q] + (j + 1) * P], identity[:])
                            m.then_inc(t_made, 1)
                        elif k == "PV":
                            s, piece = item[1:]
                            G = g - 1 if s == 7 else g
                            b = s // GROUP
                            e.wait_ge(t_out, (G * 8 + s) * 3 + piece + 1)
                            if piece == 0:
                                if s == 0:
                                    e.wait_ge(unit_out, unit_number(plan, base, ("X", 1)))
                                if not (isinstance(G, int) and G == 0 and s == 0):
                                    e.wait_ge(pv_out, G * 8 + s)
                            for j in {0: [0], 1: [1], 2: [2, 3]}[piece]:
                                t = b * 4 + j
                                cols = slice(PT_AT[j], PT_AT[j] + (QT - j) * P)
                                m = three(e, banks[O_BANK][:, j * P:SEQ], v_hi[:, t, :], v_lo[:, t, :],
                                          pt_hi[:, cols], pt_lo[:, cols], j == 0, j == 3)
                            if piece == 2:
                                m.then_inc(pv_made, 1)

                e.wait_ge(x0_ready, TILES)
                groups(e, run)
                run(KV_HEADS, False, False, True)

            def a_scalar(e):
                def prep(k, g, part):
                    e.wait_ge(w_loaded[k], (g + 1) * 16)
                    if not (isinstance(g, int) and g == 0):
                        if k == "k":
                            e.wait_ge(unit_made, cnt.base(g - 1, "unit") + 2)
                        if k == "v":
                            e.wait_ge(unit_made, cnt.base(g - 1, "unit") + 5)
                        if k == "q":
                            e.wait_ge(unit_made, cnt.base(g, "unit") - 4)
                        if k == "o":
                            e.wait_ge(unit_made, cnt.base(g, "unit") + 15)
                    e.activation(w_part(w_hi[k], k, part), w_part(stage[k], k, part), ACT.Copy
                                 ).then_inc(w_hi_done[k], 1)

                def run(g, first, last, tail=False):
                    for item, seen, base, plan, n in where(g, first, last, tail):
                        k = item[0]
                        if k in ("K", "Q", "X"):
                            u = base["unit"] + seen["unit"]
                            bank = banks[U_BANK + (seen["unit"] - 1) % 2]
                            e.wait_ge(unit_made, u)
                            if k == "K":
                                r = slice(item[1] * SEQ, (item[1] + 1) * SEQ)
                                if not first:
                                    e.wait_ge(scores_made, g * 8)
                                e.activation(k_hi[:, r], bank[:], ACT.Copy).then_inc(unit_hi, 1)
                            elif k == "Q":
                                s = item[1]
                                if not (first and s < 2):
                                    e.wait_ge(scores_made, g * 8 + s - 1)
                                e.activation(q_hi[:, s % 2, :], bank[:], ACT.Copy, scale=SCALE).then_inc(unit_hi, 1)
                            else:
                                if not first:
                                    e.wait_ge(pv_made, g * 8)
                                r = slice(item[1] * 4, item[1] * 4 + 4)
                                e.activation(v_hi[:, r, :], bank[:].rearrange("p (a b) -> p a b", b=P),
                                             ACT.Copy).then_inc(unit_hi, 1)
                        elif k == "E":
                            s = item[1]
                            n_s = g * 8 + s
                            e.wait_ge(neg_done, n_s + 1)
                            for q in range(QT):
                                c = slice(P_AT[q], P_AT[q] + (q + 1) * P)
                                e.activation(probs[:, s % 2, c], probs[:, s % 2, c], ACT.Exp,
                                             bias=neg_max[:, s % 2, q:q + 1],
                                             accum_out=row_sum[:, s % 2, q:q + 1]).then_inc(exp_done, 1)
                        elif k == "T":
                            s, piece = item[1:]
                            G = g - 1 if s == 7 else g
                            at, blocks = PIECES[piece]
                            w = len(blocks) * P
                            e.wait_ge(t_made, (G * 8 + s) * 3 + piece + 1)
                            if not (isinstance(G, int) and G == 0 and s == 0):
                                e.wait_ge(pv_made, G * 8 + s)
                            e.activation(pt_hi[:, at:at + w], banks[T_BANK + (3 * s + piece) % 2][:, 0:w],
                                         ACT.Copy).then_inc(t_hi, 1)
                        elif k == "PV" and item[2] == 2:
                            s = item[1]
                            G = g - 1 if s == 7 else g
                            b, h = divmod(s, GROUP)
                            e.wait_ge(pv_made, G * 8 + s + 1)
                            if h == 0:
                                if not (isinstance(G, int) and G == 0):
                                    e.wait_ge(unit_made, cnt.base(G, "unit") + (0 if b == 0 else 15))
                            e.activation(at_hi[:, b, h, :], banks[O_BANK][:], ACT.Copy).then_inc(pv_hi, 1)
                        elif k == "W":
                            prep(item[1], g if item[1] == "o" else g + 1, item[2])

                for k in "kqv":
                    for part in range(W_PARTS[k]):
                        prep(k, 0, part)
                groups(e, run)
                run(KV_HEADS, False, False, True)

            def a_vector(e):
                def prep(k, g, part):
                    e.wait_ge(w_hi_done[k], g * W_PARTS[k] + part + 1)
                    e.tensor_tensor(w_part(w_lo[k], k, part), w_part(stage[k], k, part),
                                    w_part(w_hi[k], k, part).bitcast(F32), ALU.subtract).then_inc(w_ready[k], 1)

                def run(g, first, last, tail=False):
                    n_hi = 0
                    for item, seen, base, plan, n in where(g, first, last, tail):
                        k = item[0]
                        if k == "V":
                            e.wait_ge(unit_made, base["unit"] + seen["unit"])
                            e.tensor_copy(v_whole[:, item[1], :], banks[U_BANK + (seen["unit"] - 1) % 2][:]
                                          ).then_inc(unit_out, 1)
                        elif k in ("K", "Q", "X"):
                            n_hi += 1
                            bank = banks[U_BANK + (seen["unit"] - 1) % 2]
                            e.wait_ge(unit_hi, g * 12 + n_hi)
                            if k == "K":
                                r = slice(item[1] * SEQ, (item[1] + 1) * SEQ)
                                e.tensor_tensor(k_lo[:, r], bank[:], k_hi[:, r].bitcast(F32),
                                                ALU.subtract).then_inc(unit_out, 1)
                            elif k == "Q":
                                s = item[1]
                                e.scalar_tensor_tensor(out=q_lo[:, s % 2, :], in0=bank[:], scalar=SCALE,
                                                       in1=q_hi[:, s % 2, :].bitcast(F32), op0=ALU.mult,
                                                       op1=ALU.subtract).then_inc(unit_out, 1)
                            else:
                                r = slice(item[1] * 4, item[1] * 4 + 4)
                                e.tensor_tensor(v_lo[:, r, :], bank[:].rearrange("p (a b) -> p a b", b=P),
                                                v_hi[:, r, :].bitcast(F32), ALU.subtract).then_inc(unit_out, 1)
                        elif k == "O":
                            t = item[1] * 4 + item[2]
                            e.wait_ge(unit_made, base["unit"] + seen["unit"])
                            e.tensor_tensor(acc[:, t, :], acc[:, t, :], banks[U_BANK + (seen["unit"] - 1) % 2][:],
                                            ALU.add).then_inc(unit_out, 1)
                        elif k == "S":
                            s = item[1]
                            n_s = g * 8 + s
                            e.wait_ge(scores_made, n_s + 1)
                            if not (first and s < 2):
                                e.wait_ge(t_made, (n_s - 1) * 3)
                            e.memset(pace[:], 0.0)
                            for q in range(QT):
                                bank, at = S_AT[q]
                                c = slice(P_AT[q], P_AT[q] + (q + 1) * P)
                                e.tensor_tensor_reduce(probs[:, s % 2, c], banks[S_BANK + bank][:, at:at + (q + 1) * P],
                                                       mask[:, SEQ - (q + 1) * P:SEQ], 1.0, NEG, ALU.add, ALU.max,
                                                       row_max[:, s % 2, q:q + 1]).then_inc(masked, 1)
                            e.wait_ge(masked, (n_s + 1) * QT)
                            e.tensor_scalar(neg_max[:, s % 2, :], row_max[:, s % 2, :], -1.0, None,
                                            ALU.mult).then_inc(neg_done, 1)
                        elif k == "N":
                            s = item[1]
                            n_s = g * 8 + s
                            e.wait_ge(exp_done, (n_s + 1) * QT)
                            e.reciprocal(row_inv[:, s % 2, :], row_sum[:, s % 2, :]).then_inc(inv_done, 1)
                            e.wait_ge(inv_done, n_s + 1)
                            for q in range(QT):
                                c = slice(P_AT[q], P_AT[q] + (q + 1) * P)
                                m = e.tensor_scalar(probs[:, s % 2, c], probs[:, s % 2, c],
                                                    row_inv[:, s % 2, q:q + 1], None, ALU.mult)
                            m.then_inc(probs_ready, 1)
                        elif k == "T":
                            s, piece = item[1:]
                            G = g - 1 if s == 7 else g
                            at, blocks = PIECES[piece]
                            w = len(blocks) * P
                            e.wait_ge(t_hi, (G * 8 + s) * 3 + piece + 1)
                            e.tensor_tensor(pt_lo[:, at:at + w], banks[T_BANK + (3 * s + piece) % 2][:, 0:w],
                                            pt_hi[:, at:at + w].bitcast(F32), ALU.subtract).then_inc(t_out, 1)
                        elif k == "PV" and item[2] == 2:
                            s = item[1]
                            G = g - 1 if s == 7 else g
                            b, h = divmod(s, GROUP)
                            e.wait_ge(pv_hi, G * 8 + s + 1)
                            e.tensor_tensor(at_lo[:, b, h, :], banks[O_BANK][:], at_hi[:, b, h, :].bitcast(F32),
                                            ALU.subtract).then_inc(pv_out, 1)
                        elif k == "W":
                            prep(item[1], g if item[1] == "o" else g + 1, item[2])

                e.wait_ge(consts_ready, 1)
                for k in "kqv":
                    for part in range(W_PARTS[k]):
                        prep(k, 0, part)
                groups(e, run)
                run(KV_HEADS, False, False, True)

            engines["sync"].append(a_sync)
            engines["scalar"].append(a_scalar)
            engines["vector"].append(a_vector)
            engines["tensor"].append(a_tensor)
            a_units = cnt.base(KV_HEADS, "unit") + 4

            x1_ready, second_half1 = norm_stage(1, lambda e, i: None, lambda e, i: e.wait_ge(unit_out, a_units), True,
                                                "B" in phases, store=out if "B" not in phases else None)

        if "B" in phases:
            gathered = [sem(f"gathered{k}") for k in range(2)]
            written = [sem(f"written{k}") for k in range(2)]
            N_CODES = D // CODE
            paced = sem("paced")
            IN_FLIGHT = 8

            def gather_gpsimd(e):
                def write(k, t):
                    e.wait_ge(gathered[k], (t + 1) * 16 * N_CODES)
                    e.dma_start(wdram[bass.ts(t * 2 + k, 1), :, :].rearrange("a p c -> (a p) c"),
                                gathered_rows[:, k, :]).then_inc(written[k], 16)

                def body(t, first, last):
                    m = FLAST if last else P
                    for k in range(2):
                        if not first:
                            e.wait_ge(paced, t * 2 + k)
                        if first:
                            e.wait_ge(first_idx_loaded[k], 16)
                        else:
                            e.wait_ge(idx_loaded[k], t * 16)
                        if not first:
                            e.wait_ge(written[k], t * 16)
                        for c in range(N_CODES):
                            if c == 0:
                                e.tensor_tensor(pool_pace[:, k:k + 1], eps[0:1, :], eps[0:1, :],
                                                ALU.add).then_inc(paced, 1)
                            e.indirect_dma_start(gathered_rows[0:m, k, c * CODE:(c + 1) * CODE], None, codebook,
                                                 bass.IndirectOffsetOnAxis(ap=codes_at[0:m, k, c:c + 1], axis=0)
                                                 ).then_inc(gathered[k], 16)
                            if c == IN_FLIGHT:
                                if k:
                                    write(0, t)
                                    if not last:
                                        load_idx(e, 0, t + 1, idx_loaded)
                                elif not first:
                                    write(1, t - 1)
                                    load_idx(e, 1, t, idx_loaded)
                    if last:
                        write(1, t)
                body(0, True, False)
                with e.Fori(1, FT - 1) as t:
                    body(t, False, False)
                body(FT - 1, False, True)

            engines["gpsimd"].append(gather_gpsimd)

        def mlp(name, ready, second_half, arena_left, coded):
            if coded:
                cut_r, cut_f, (cut_b, cut_h), close = arenas(name, 10240, 9600, 6200)
            else:
                cut_r, cut_f, close = arenas(name, 10240, 5120)
            g_hi, g_lo = cut_r(2, KB, P), cut_r(2, KB, P)
            u_hi, u_lo = cut_r(2, KB, P), cut_r(2, KB, P)
            d_hi, d_lo = cut_r(2, D), cut_r(2, D)
            h_hi, h_lo = cut_r(2, TOK), cut_r(2, TOK)
            stage = [cut_f(3, D), cut_f(3, D)]
            gate = cut_f(2, SEQ)
            inner = cut_f(2, SEQ)
            if coded:
                ROUND = SEQ // P
                ROUNDS = KB * (P // CODE) // ROUND
                NIDX = ROUND * ROUNDS
                book = cut_f(HI_BLOCKS, LO * CODE)
                rest = cut_f(2, HI_BLOCKS * LO * CODE)
                parts = [cut_b(HI_BLOCKS, LO * CODE) for _ in range(3)]
                row_hot = cut_b(2, HI_BLOCKS, SEQ)
                spread = cut_h(2, SEQ)
                hi_half = cut_h(NIDX)
                identity_h = cut_h(P)
                codes_d, hi_int, lo_int = (cut_f(NIDX) for _ in range(3))
                entry_hot = cut_f(NIDX, LO)
                lo_f = cut_f(NIDX)
                masked_f = cut_f(2, SEQ)
                down_rows = cut_f(D)
                pick = {k: sem(f"pick_{k}") for k in
                        ("book_loaded", "book_part", "codes_loaded", "codes_split", "codes_ready",
                         "last_up", "spread_made", "spread_copied", "hot", "picked", "masked", "reduced")}
            close()
            G_BANK, U_BANK, D_BANK, T_BANK, D_RING = 0, 2, 4, 6, 4
            s = {k: sem(f"{name}_{k}") for k in
                 ("loaded", "g_made", "u_made", "silu_done", "inner_done", "h_hi_done", "h_ready",
                  "w_made", "w_hi_done", "w_ready", "down_made", "down_out", "scales_loaded")}

            def tiles(e, body):
                pairs = (FT - 5) // 2 if coded else (FT - 3) // 2
                body(0, 0, P)
                body(1, 1, P)
                with e.Fori(0, pairs) as i:
                    body(i * 2 + 2, 0, P)
                    body(i * 2 + 3, 1, P)
                for t in range(2 * pairs + 2, FT - 1):
                    body(t, t % 2, P)
                body(FT - 1, 0, FLAST)

            def is_int(t, v):
                return isinstance(t, int) and t == v

            def late(n, k):
                return not isinstance(n, int) or n >= k

            def sync(e):
                def load(t, par, m):
                    rows = t * P if isinstance(t, int) else e.snap(t * P)
                    tiles2 = t * 2 if isinstance(t, int) else e.snap(t * 2)
                    now = t if isinstance(t, int) else e.snap(t)
                    whole_tiles, left, so_far = (v if isinstance(t, int) else e.snap(v) for v in
                                                 ((t + 1) * 16, (t - 1) * 3, t * per_load))
                    if coded:
                        if not is_int(t, 0):
                            e.wait_ge(pick["codes_ready"], now)
                        arena_left(e)
                        e.sem_inc(may_load, 1)
                        e.dma_start(codes_d.bitcast(I32), idx[bass.ds(now, 1), 2, :, :].rearrange("a p c -> (a p) c")
                                    ).then_inc(pick["codes_loaded"], 16)
                        for k in range(1 if is_int(t, FT - 1) else 2):
                            e.wait_ge(written[k], whole_tiles)
                        e.sem_inc(may_load, 1)
                    if not (isinstance(t, int) and t < 2):
                        e.wait_ge(s["w_made"] if coded else s["w_ready"], left)
                        e.sem_inc(may_load, 1)
                    if not is_int(t, 0):
                        e.wait_ge(s["loaded"], so_far)
                    arena_left(e)
                    e.sem_inc(may_load, 1)
                    done = s["loaded"]
                    if coded:
                        n = 1 if is_int(t, FT - 1) else 2
                        e.dma_start(stage[par][:, 0:n, :], wdram[bass.ds(tiles2, n), :, :].rearrange("k p c -> p k c")
                                    ).then_inc(done, 16)
                        if is_int(t, FT - 1):
                            e.wait_ge(written[1], whole_tiles)
                            e.dma_start(stage[par][:, 1, :], wdram[tiles2 + 1, :, :]).then_inc(pick["last_up"], 16)
                        return
                    for k, w in enumerate((wf_gate, wf_up)):
                        e.dma_start(stage[par][:, k, :].rearrange("p (a b) -> p a b", a=KB)[:, :, 0:m].bitcast(I32),
                                    w.rearrange("(c p) n -> p c n", p=P)[:, :, bass.ds(rows, m)]).then_inc(done, 16)
                    e.dma_start(stage[par][0:m, 2, :].bitcast(I32), wf_down[bass.ds(rows, m), :]).then_inc(done, 16)
                if not coded:
                    e.dma_start(scale_sb[:], scales.to_broadcast([P, 3])).then_inc(s["scales_loaded"], 16)
                else:
                    arena_left(e)
                    e.dma_start(book, codebook.rearrange("(b p l) k -> p b (l k)", p=P, l=LO)
                                ).then_inc(pick["book_loaded"], 16)
                tiles(e, load)

            per_load = 16 if coded else 48

            def dest(k, par, lo):
                return {0: (g_hi, g_lo), 1: (u_hi, u_lo), 2: (d_hi, d_lo)}[k][lo][:, par]

            def width(k, m, ap):
                if k == 2:
                    return ap[0:m, :]
                return ap[:, :, 0:m]

            def source(k, par, m):
                b = banks[T_BANK + (par + k) % 2][:] if coded else stage[par][:, k, :].bitcast(I32)
                return width(k, m, b if k == 2 else b.rearrange("p (a b) -> p a b", a=KB))

            def scale_of(k, m):
                return scale_sb[0:(m if k == 2 else P), k:k + 1]

            def next_of(t, par, m):
                if is_int(t, FT - 1):
                    return None
                return t + 1, 1 - par, P

            def tensor(e):
                def turn(k, t, par, m):
                    if k == 0:
                        e.wait_ge(s["loaded"], (t + 1) * per_load)
                    if k == 1 and is_int(t, FT - 1):
                        e.wait_ge(pick["last_up"], 16)
                    if not (isinstance(t, int) and 3 * t + k < 2):
                        e.wait_ge(s["w_ready"], t * 3 + k - 1)
                    if k < 2 and late(t, 2):
                        e.wait_ge(s["down_out"], (t if is_int(t, FT - 1) else t - 1) * TILES)
                    if k == 2:
                        e.wait_ge(pick["reduced"], (t + 1) * ROUNDS)
                    for c in range(KB):
                        src = down_rows[:, c * P:(c + 1) * P] if k == 2 else stage[par][:, k, c * P:(c + 1) * P]
                        x_ = e.transpose(banks[T_BANK + (par + k) % 2][:, c * P:(c + 1) * P], src, identity[:])
                    x_.then_inc(s["w_made"], 1)

                def gather(t, par):
                    def spread_rows(q):
                        if late(t * ROUNDS + q, 2):
                            e.wait_ge(pick["spread_copied"], t * ROUNDS + q - 1)
                        for g in range(ROUND):
                            c = q * ROUND + g
                            x_ = e.matmul(banks[U_BANK + q % 2][:, g * P:(g + 1) * P],
                                          hi_half[:, c:c + 1].to_broadcast([P, P]), identity_h, start=True, stop=True)
                        x_.then_inc(pick["spread_made"], 1)

                    def pick_rows(q):
                        e.wait_ge(pick["hot"], t * ROUNDS + q + 1)
                        if late(t * ROUNDS + q, 2):
                            e.wait_ge(pick["masked"], t * ROUNDS + q - 1)
                        for g in range(ROUND):
                            for b in range(HI_BLOCKS):
                                for n, part in enumerate(parts):
                                    x_ = e.matmul(banks[G_BANK + q % 2][:, g * P:(g + 1) * P],
                                                  row_hot[:, q % 2, b, g * P:(g + 1) * P], part[:, b, :],
                                                  start=(b == 0 and n == 0), stop=(b == HI_BLOCKS - 1 and n == 2))
                        x_.then_inc(pick["picked"], 1)

                    e.wait_ge(pick["codes_ready"], t + 1)
                    for q in range(2):
                        if not is_int(t, 0):
                            e.wait_ge(s["inner_done"], t * 2 - 1 + q)
                        spread_rows(q)
                        if late(t, 2):
                            down_tile(t - 2, par, P, q)
                    if late(t, 2):
                        down_tile(t - 2, par, P, 2)
                        down_tile(t - 2, par, P, 3)
                    if not is_int(t, 0):
                        e.wait_ge(s["silu_done"], t * 2)
                    for q in range(ROUNDS):
                        pick_rows(q)
                        if q + 2 < ROUNDS:
                            spread_rows(q + 2)
                        if late(t, 2) and q + 4 < TILES:
                            down_tile(t - 2, par, P, q + 4)
                        if q >= ROUNDS - 2 and not is_int(t, FT - 1):
                            turn(q - (ROUNDS - 2), t, par, P)
                    if is_int(t, FT - 1):
                        down(t - 1, 1 - par, P)
                        turn(0, t, par, P)

                def up(t, par, m, half, matrices=(0, 1)):
                    r = slice(half * SEQ, (half + 1) * SEQ)
                    for k in matrices:
                        hi, lo, bank, made, out_ = ((g_hi, g_lo, G_BANK, "g_made", "silu_done"),
                                                    (u_hi, u_lo, U_BANK, "u_made", "inner_done"))[k]
                        if half == 0:
                            e.wait_ge(s["w_ready"], t * 3 + k + 1)
                        if coded and half == 0:
                            e.wait_ge(pick["spread_copied" if k else "masked"], (t + 1) * ROUNDS)
                        if not coded and not is_int(t, 0):
                            e.wait_ge(s[out_], t * 2 + half - 1)
                        for c in range(KB):
                            x_ = three(e, banks[bank + half][0:m, :], hi[:, par, c, 0:m], lo[:, par, c, 0:m],
                                       x_hi[:, c, r], x_lo[:, c, r], c == 0, c == KB - 1)
                        x_.then_inc(s[made], 1)

                def down_tile(t, par, m, i):
                    if i == 0:
                        e.wait_ge(s["w_ready"], t * 3 + 3)
                    if i == 0 or (is_int(t, FT - 1) and i == TILES // 2):
                        e.wait_ge(s["h_ready"], t * 2 + (1 if is_int(t, FT - 1) and i == 0 else 2))
                    if coded and i == T_BANK - D_BANK:
                        e.wait_ge(s["w_ready"], t * 3 + (3 if isinstance(t, int) and t >= FT - 2 else 6))
                    if not (is_int(t, 0) and i < D_RING):
                        e.wait_ge(s["down_out"], t * TILES + i + 1 - D_RING)
                    r = slice(i * P, (i + 1) * P)
                    three(e, banks[D_BANK + i % D_RING][:], h_hi[0:m, par, r], h_lo[0:m, par, r], d_hi[0:m, par, :],
                          d_lo[0:m, par, :], True, True).then_inc(s["down_made"], 1)

                def down(t, par, m):
                    for i in range(TILES):
                        down_tile(t, par, m, i)

                def body(t, par, m):
                    nxt = next_of(t, par, m)
                    if coded and not nxt:
                        up(t, par, m, 0, (0,))
                        up(t, par, m, 1, (0,))
                        turn(1, t, par, m)
                        turn(2, t, par, m)
                        up(t, par, m, 0, (1,))
                        up(t, par, m, 1, (1,))
                        return
                    up(t, par, m, 0)
                    if coded:
                        turn(2, t, par, m)
                    elif is_int(t, 0):
                        second_half(e, "tensor")
                    up(t, par, m, 1)
                    if coded and nxt:
                        gather(*nxt[0:2])
                    elif not is_int(t, 0):
                        down(t - 1, 1 - par, P)

                e.wait_ge(ready, TILES // 2)
                if coded:
                    second_half(e, "tensor")
                    gather(0, 0)
                tiles(e, body)
                down(FT - 1, 0, FLAST)

            def high_part(e, k, t, par, m):
                if coded:
                    e.wait_ge(s["w_made"], t * 3 + k + 1)
                elif k == 0:
                    e.wait_ge(s["loaded"], (t + 1) * per_load)
                if not (isinstance(t, int) and t < 2):
                    if k < 2:
                        e.wait_ge(s["u_made"], (t - 1) * 2)
                    else:
                        e.wait_ge(s["down_made"], (t - 1) * TILES)
                e.activation(width(k, m, dest(k, par, 0)), source(k, par, m), ACT.Copy,
                             scale=1.0 if coded else scale_of(k, m)).then_inc(s["w_hi_done"], 1)

            def first_parts(e):
                e.wait_ge(s["scales_loaded"], 16)
                for k in range(3):
                    high_part(e, k, 0, 0, P)
            if not coded:
                early[3] = first_parts

            def scalar(e):
                def part(k, t, par, m):
                    high_part(e, k, t, par, m)

                def silu(t, par, m, half):
                    e.wait_ge(s["g_made"], t * 2 + half + 1)
                    if not is_int(t, 0):
                        e.wait_ge(s["inner_done"], t * 2 + half - 1)
                    e.activation(gate[0:m, half, :], banks[G_BANK + half][0:m, :], ACT.Silu).then_inc(s["silu_done"], 1)

                def high(t, par, m, half):
                    e.wait_ge(s["inner_done"], t * 2 + half + 1)
                    if not (isinstance(t, int) and t < 2):
                        e.wait_ge(s["down_made"], (t - 1) * TILES)
                    r = slice(half * SEQ, (half + 1) * SEQ)
                    e.activation(h_hi[0:m, par, r], inner[0:m, half, :], ACT.Copy).then_inc(s["h_hi_done"], 1)

                def spread_copies(t, rounds):
                    for q in rounds:
                        e.wait_ge(pick["spread_made"], t * ROUNDS + q + 1)
                        if late(t * ROUNDS + q, 2):
                            e.wait_ge(pick["hot"], t * ROUNDS + q - 1)
                        e.activation(spread[:, q % 2, :], banks[U_BANK + q % 2][:], ACT.Copy
                                     ).then_inc(pick["spread_copied"], 1)

                def body(t, par, m):
                    nxt = next_of(t, par, m)
                    silu(t, par, m, 0)
                    if not nxt:
                        if coded:
                            silu(t, par, m, 1)
                            part(1, t, par, P)
                            part(2, t, par, P)
                        high(t, par, m, 0)
                        if not coded:
                            silu(t, par, m, 1)
                        high(t, par, m, 1)
                        return
                    if nxt and not coded:
                        part(0, *nxt)
                        part(1, *nxt)
                    elif coded:
                        part(2, t, par, P)
                    silu(t, par, m, 1)
                    high(t, par, m, 0)
                    if nxt and coded:
                        spread_copies(nxt[0], range(2))
                    high(t, par, m, 1)
                    if nxt and coded:
                        spread_copies(nxt[0], range(2, ROUNDS))
                        part(0, *nxt)
                        if not is_int(nxt[0], FT - 1):
                            part(1, *nxt)
                    elif nxt:
                        part(2, *nxt)

                e.wait_ge(ready, 1)
                if coded:
                    spread_copies(0, range(ROUNDS))
                    for k in range(2):
                        part(k, 0, 0, P)
                second_half(e, "scalar")
                tiles(e, body)

            def add_tile(e, t, i):
                e.wait_ge(s["down_made"], t * TILES + i + 1)
                e.tensor_tensor(acc[:, i, :], acc[:, i, :], banks[D_BANK + i % D_RING][:],
                                ALU.add).then_inc(s["down_out"], 1)

            def vector(e):
                def part(k, t, par, m):
                    e.wait_ge(s["w_hi_done"], t * 3 + k + 1)
                    e.scalar_tensor_tensor(out=width(k, m, dest(k, par, 1)), in0=source(k, par, m),
                                           scalar=1.0 if coded else scale_of(k, m),
                                           in1=width(k, m, dest(k, par, 0)).bitcast(F32), op0=ALU.mult,
                                           op1=ALU.subtract).then_inc(s["w_ready"], 1)

                def mult(t, par, m, half):
                    e.wait_ge(s["silu_done"], t * 2 + half + 1)
                    e.wait_ge(s["u_made"], t * 2 + half + 1)
                    if not is_int(t, 0):
                        e.wait_ge(s["h_ready"], t * 2 + half - 1)
                    e.tensor_tensor(inner[0:m, half, :], gate[0:m, half, :], banks[U_BANK + half][0:m, :],
                                    ALU.mult).then_inc(s["inner_done"], 1)

                def low(t, par, m, half):
                    r = slice(half * SEQ, (half + 1) * SEQ)
                    e.wait_ge(s["h_hi_done"], t * 2 + half + 1)
                    e.tensor_tensor(h_lo[0:m, par, r], inner[0:m, half, :], h_hi[0:m, par, r].bitcast(F32),
                                    ALU.subtract).then_inc(s["h_ready"], 1)

                def add(t):
                    for i in range(TILES):
                        add_tile(e, t, i)

                def split_book():
                    left = book.rearrange("p a b -> p (a b)")
                    e.wait_ge(pick["book_loaded"], 16)
                    for n in range(3):
                        flat = parts[n].rearrange("p a b -> p (a b)")
                        e.tensor_copy(flat, left).then_inc(pick["book_part"], 1)
                        e.wait_ge(pick["book_part"], 2 * n + 1)
                        if n < 2:
                            e.tensor_tensor(rest[:, n, :], left, flat, ALU.subtract).then_inc(pick["book_part"], 1)
                            e.wait_ge(pick["book_part"], 2 * n + 2)
                            left = rest[:, n, :]

                def split_codes(t):
                    e.wait_ge(pick["codes_loaded"], (t + 1) * 16)
                    if not is_int(t, 0):
                        e.wait_ge(pick["reduced"], t * ROUNDS)
                    e.tensor_scalar(hi_int.bitcast(I32), codes_d.bitcast(I32), LO.bit_length() - 1, None,
                                    ALU.logical_shift_right).then_inc(pick["codes_split"], 1)
                    e.tensor_scalar(lo_int.bitcast(I32), codes_d.bitcast(I32), LO - 1, None,
                                    ALU.bitwise_and).then_inc(pick["codes_split"], 1)
                    e.wait_ge(pick["codes_split"], t * 3 + 2)
                    e.tensor_copy(hi_half, hi_int.bitcast(I32))
                    e.tensor_copy(lo_f, lo_int.bitcast(I32)).then_inc(pick["codes_split"], 1)
                    e.wait_ge(pick["codes_split"], t * 3 + 3)
                    e.tensor_tensor(entry_hot, lo_f.unsqueeze(2).to_broadcast([P, NIDX, LO]),
                                    entry_number[:].unsqueeze(1).to_broadcast([P, NIDX, LO]), ALU.is_equal
                                    ).then_inc(pick["codes_ready"], 1)

                def gather(t, par, lows=None):
                    def hot(q):
                        e.wait_ge(pick["spread_copied"], t * ROUNDS + q + 1)
                        if late(t * ROUNDS + q, 2):
                            e.wait_ge(pick["picked"], t * ROUNDS + q - 1)
                        for b in range(HI_BLOCKS):
                            x_ = e.tensor_scalar(row_hot[:, q % 2, b, :], spread[:, q % 2, :],
                                                 row_number[:, b:b + 1], None, ALU.is_equal)
                        x_.then_inc(pick["hot"], 1)

                    def take(q):
                        e.wait_ge(pick["picked"], t * ROUNDS + q + 1)
                        if late(t * ROUNDS + q, 2):
                            e.wait_ge(pick["reduced"], t * ROUNDS + q - 1)
                        e.tensor_tensor(masked_f[:, q % 2, :].rearrange("p (a b) -> p a b", b=CODE),
                                        banks[G_BANK + q % 2][:].rearrange("p (a b) -> p a b", b=CODE),
                                        entry_hot.rearrange("p a b -> p (a b)")[:, q * ROUND * LO:(q + 1) * ROUND * LO]
                                        .unsqueeze(2).to_broadcast([P, ROUND * LO, CODE]), ALU.mult
                                        ).then_inc(pick["masked"], 1)
                        e.wait_ge(pick["masked"], t * ROUNDS + q + 1)
                        w = ROUND * CODE
                        e.tensor_reduce(down_rows[:, q * w:(q + 1) * w].rearrange("p (g k) -> p g k", g=ROUND),
                                        masked_f[:, q % 2, :].rearrange("p (g l k) -> p g k l", g=ROUND, l=LO),
                                        AX.X, ALU.add).then_inc(pick["reduced"], 1)

                    for q in range(2):
                        hot(q)
                        if lows is not None:
                            lows(q)
                    for q in range(ROUNDS):
                        if late(t, 2) and q < TILES:
                            add_tile(e, t - 2, q)
                        take(q)
                        if q + 2 < ROUNDS:
                            hot(q + 2)
                        if q >= ROUNDS - 2 and not is_int(t, FT - 1):
                            part(q - (ROUNDS - 2), t, par, P)
                    if is_int(t, FT - 1):
                        add(t - 1)
                        part(0, t, par, P)

                def body(t, par, m):
                    nxt = next_of(t, par, m)
                    if nxt and coded:
                        split_codes(nxt[0])
                    if not nxt:
                        if coded:
                            part(1, t, par, P)
                            part(2, t, par, P)
                        for half in range(2):
                            mult(t, par, m, half)
                            low(t, par, m, half)
                        if not coded:
                            add(t - 1)
                        return
                    mult(t, par, m, 0)
                    if nxt and not coded:
                        part(0, *nxt)
                        part(1, *nxt)
                    elif coded:
                        part(2, t, par, P)
                    mult(t, par, m, 1)
                    if nxt and coded:
                        gather(nxt[0], nxt[1], lambda half: low(t, par, m, half))
                        return
                    low(t, par, m, 0)
                    low(t, par, m, 1)
                    if not is_int(t, 0):
                        add(t - 1)
                    if nxt:
                        part(2, *nxt)

                if coded:
                    e.tensor_copy(identity_h, identity[:])
                    split_book()
                    split_codes(0)
                    gather(0, 0)
                else:
                    for k in range(3):
                        part(k, 0, 0, P)
                second_half(e, "vector")
                tiles(e, body)

            engines["sync"].append(sync)
            engines["scalar"].append(scalar)
            engines["vector"].append(vector)
            engines["tensor"].append(tensor)
            return (lambda e, i: add_tile(e, FT - 1, i),
                    lambda e, i: e.wait_ge(s["down_out"], (FT - 1) * TILES + i + 1), s["down_made"])

        if "B" in phases:
            finish, finished, code_down_made = mlp("code", x1_ready, second_half1,
                                   lambda e: e.wait_ge(unit_out, a_units), True)

            def arena_left(e):
                e.wait_ge(code_down_made, FT * TILES)

            x2_ready, second_half2 = norm_stage(2, finish, finished, True, "C" in phases, turn_bank=2, split_turns=True,
                                                store=out if "C" not in phases else None)

        if "C" in phases:
            STEPS = 2 * HEADS
            CHUNKS = SEQ // P
            cut_r, cut_f, close = arenas("c", 14848, 13600)
            LIN = "kqvgo"
            c_stage = {k: cut_f(KB, P) for k in "kqvg"} | {"o": cut_f(D)}
            c_hi = {k: cut_r(KB, P) for k in "kqvg"} | {"o": cut_r(D)}
            c_lo = {k: cut_r(KB, P) for k in "kqvg"} | {"o": cut_r(D)}
            gate_f = cut_f(2, SEQ)
            whole = {k: cut_f(SEQ) for k in "kqv"}
            k_h, k_l, q_h, q_l = (cut_r(2, SEQ) for _ in range(4))
            v_h, v_l = cut_r(CHUNKS, P), cut_r(CHUNKS, P)
            s_f, s_h, s_l = cut_f(P_COLS), cut_r(P_COLS), cut_r(P_COLS)
            y_f = cut_f(SEQ)
            y_h, y_l = cut_r(2, SEQ), cut_r(2, SEQ)
            square, sum_sq = cut_f(SEQ), cut_f(2, SEQ)
            proj = cut_f(TILES, D)
            dec_stage, dec = cut_f(SEQ + 2), cut_f(SEQ + 2)
            rms, rms_inv, ones = cut_f(TILES), cut_f(TILES), cut_f(2)
            close()
            weight = dec[:, SEQ:SEQ + 1]
            U, O_B, V_B, S_B, Y_B = 0, 2, 3, 4, 7
            LAST_O = (S_B, S_B + 1, O_B, V_B)
            c = {k: sem(f"c_{k}") for k in
                 ("unit_made", "unit_out", "part_hi", "part_ready", "v_turned", "v_hi", "v_ready", "s_made", "s_scaled",
                  "s_hi", "s_ready", "y_made", "y_done", "y_hi", "y_ready", "o_made", "o_added",
                  "squared", "sq_done", "dec_loaded", "dec_ready", "zeroed", "rms_made", "rms_sqrt", "rms_ready",
                  "rms_used")}
            c_loaded = {k: sem(f"c_w{k}_loaded") for k in LIN}
            c_hi_done = {k: sem(f"c_w{k}_hi_done") for k in LIN}
            c_ready = {k: sem(f"c_w{k}_ready") for k in LIN}
            S_PIECES = [(0, SEQ, [(0, 0)]), (512, 384, [(1, 0)]), (896, 384, [(2, 0), (3, 256)])]

            def late(n, k):
                return not isinstance(n, int) or n >= k

            def heads(e, body):
                body(0, True, False)
                with e.Fori(1, HEADS - 1) as h:
                    body(h, False, False)
                body(HEADS - 1, False, True)

            def c_sync(e):
                qkv = qkv_w.rearrange("(c p) (h n) -> p c h n", p=P, n=3 * P)
                src = {
                    "q": lambda h: qkv[:, :, bass.ds(h, 1), 0:P].rearrange("p c a n -> p (c a) n"),
                    "k": lambda h: qkv[:, :, bass.ds(h, 1), P:2 * P].rearrange("p c a n -> p (c a) n"),
                    "v": lambda h: qkv[:, :, bass.ds(h, 1), 2 * P:3 * P].rearrange("p c a n -> p (c a) n"),
                    "g": lambda h: gate_w.rearrange("(c p) (h n) -> p c h n", p=P, n=P)[:, :, bass.ds(h, 1), :]
                    .rearrange("p c a n -> p (c a) n"),
                    "o": lambda h: out_w.rearrange("(h p) n -> p h n", p=P)[:, bass.ds(h, 1), :]
                    .rearrange("p a n -> p (a n)"),
                }

                def load(h):
                    now = h if isinstance(h, int) else e.snap(h)
                    for k in "kqvgo":
                        if late(h, 1):
                            e.wait_ge(c_ready[k], now)
                        arena_left(e)
                        e.sem_inc(may_load, 1)
                        e.dma_start(c_stage[k], src[k](now)).then_inc(c_loaded[k], 16)
                    if late(h, 1):
                        e.wait_ge(c["dec_ready"], now)
                        e.sem_inc(may_load, 1)
                    e.dma_start(dec_stage[:, 0:SEQ], decay[bass.ds(now, 1), :, :].rearrange("a p n -> (a p) n")
                                ).then_inc(c["dec_loaded"], 16)
                    e.dma_start(dec_stage[:, SEQ:SEQ + 1], norm_w[bass.ds(now, 1), :, :].rearrange("a p n -> (a p) n")
                                ).then_inc(c["dec_loaded"], 16)

                load(0)
                with e.Fori(1, HEADS) as h:
                    load(h)

            def c_tensor(e):
                def chunk(j):
                    return slice(j * P, (j + 1) * P)

                def unit(k, n, b, h):
                    i = "kqvg".index(k)
                    if b == 0:
                        e.wait_ge(c_ready[k], h + 1)
                    if late(n * 4 + i, 2):
                        e.wait_ge(c["unit_out"], n * 4 + i - 1)
                    r = slice(b * SEQ, (b + 1) * SEQ)
                    for a in range(KB):
                        m = three(e, banks[U + i % 2][:], c_hi[k][:, a, :], c_lo[k][:, a, :], x_hi[:, a, r],
                                  x_lo[:, a, r], a == 0, a == KB - 1)
                    m.then_inc(c["unit_made"], 1)

                def turn_values(m):
                    e.wait_ge(c["unit_out"], m * 4 + 3)
                    if late(m, 1):
                        e.wait_ge(c["v_ready"], m)
                    for j in range(CHUNKS):
                        x_ = e.transpose(banks[V_B][:, chunk(j)], whole["v"][:, chunk(j)], identity[:])
                    x_.then_inc(c["v_turned"], 1)

                def scores(m, p):
                    e.wait_ge(c["part_ready"], m * 2 + 2)
                    for i, (at, w, blocks) in enumerate(S_PIECES):
                        if late(m, 1):
                            e.wait_ge(c["s_scaled"], m * 4 + (-3, -2, 0)[i])
                        for j, col in blocks:
                            x_ = three(e, banks[S_B + i][:, col:col + SEQ - j * P], k_h[:, p, chunk(j)],
                                       k_l[:, p, chunk(j)], q_h[:, p, j * P:SEQ], q_l[:, p, j * P:SEQ], True, True)
                        x_.then_inc(c["s_made"], 1)

                def values(m):
                    e.wait_ge(c["v_ready"], m + 1)
                    e.wait_ge(c["s_ready"], m * 3 + 3)
                    if late(m, 1):
                        e.wait_ge(c["y_done"], m)
                        e.wait_ge(c["squared"], m)
                    for j in range(CHUNKS):
                        cols = slice(PT_AT[j], PT_AT[j] + (QT - j) * P)
                        x_ = three(e, banks[Y_B][:, j * P:SEQ], v_h[:, j, :], v_l[:, j, :], s_h[:, cols],
                                   s_l[:, cols], j == 0, j == CHUNKS - 1)
                    x_.then_inc(c["y_made"], 1)

                def out_tile(o, head, p, i, bank=O_B):
                    if i == 0:
                        e.wait_ge(c["y_ready"], o + 1)
                        e.wait_ge(c_ready["o"], head + 1)
                    if is_int(o, STEPS - 1):
                        e.wait_ge(c["o_added"], o * 4)
                    elif late(o * 4 + i, 1):
                        e.wait_ge(c["o_added"], o * 4 + i)
                    three(e, banks[bank][:], y_h[:, p, chunk(i)], y_l[:, p, chunk(i)], c_hi["o"], c_lo["o"],
                          True, True).then_inc(c["o_made"], 1)

                def is_int(n, v):
                    return isinstance(n, int) and n == v

                def step(h, b, units, n, attend, project):
                    m, o = n - 1, n - 2
                    if attend:
                        turn_values(m)
                    for k, i in (("k", 0), ("q", 1), ("v", 2), ("g", 3)):
                        if units:
                            unit(k, n, b, h)
                        if is_int(n, 0) and k == "k":
                            second_half2(e, "tensor")
                        if project:
                            out_tile(o, h - 1, b, i)
                        if attend and k == "k":
                            scores(m, 1 - b)
                        if attend and k == "v":
                            values(m)

                def body(h, first, last):
                    step(h, 0, True, h * 2, not first, not first)
                    step(h, 1, True, h * 2 + 1, True, not first)

                e.wait_ge(x2_ready, TILES // 2)
                heads(e, body)
                step(HEADS, 0, False, STEPS, True, True)
                e.wait_ge(c["sq_done"], STEPS)
                for i in range(TILES):
                    x_ = e.matmul(banks[U][:, 2 * i:2 * i + 2], sum_sq[:, i // 4, chunk(i % 4)], ones,
                                  start=True, stop=True)
                x_.then_inc(c["rms_made"], 1)
                for i in range(CHUNKS):
                    out_tile(STEPS - 1, HEADS - 1, 1, i, LAST_O[i])

            def prepare(e, k, h):
                e.wait_ge(c_loaded[k], (h + 1) * 16)
                if late(h, 1):
                    if k == "o":
                        e.wait_ge(c["o_made"], h * 8)
                    else:
                        e.wait_ge(c["unit_made"], (h * 2 - 1) * 4 + "kqvg".index(k) + 1)
                e.activation(c_hi[k], c_stage[k], ACT.Copy).then_inc(c_hi_done[k], 1)

            def first_head(e):
                for k in "kqvg":
                    prepare(e, k, 0)
            early[2] = first_head

            def c_scalar(e):
                def prep(k, h):
                    prepare(e, k, h)

                def unit(k, n, b):
                    i = "kqvg".index(k)
                    e.wait_ge(c["unit_made"], n * 4 + i + 1)
                    dst = gate_f[:, b, :] if k == "g" else whole[k]
                    if k in "kq" and late(n, 1):
                        e.wait_ge(c["part_ready"], n * 2 - (1 if k == "k" else 0))
                    if k == "v" and late(n, 1):
                        e.wait_ge(c["v_turned"], n)
                    if k == "g" and late(n, 2):
                        e.wait_ge(c["y_done"], n - 1)
                    e.activation(dst, banks[U + i % 2][:], ACT.Sigmoid if k == "g" else ACT.Silu
                                 ).then_inc(c["unit_out"], 1)
                    if k in "kq":
                        hi = {"k": k_h, "q": q_h}[k][:, b, :]
                        e.wait_ge(c["unit_out"], n * 4 + i + 1)
                        if late(n, 2):
                            e.wait_ge(c["s_made"], (n - 1) * 3)
                        e.activation(hi, dst, ACT.Copy).then_inc(c["part_hi"], 1)

                def values_high(m):
                    e.wait_ge(c["v_turned"], m + 1)
                    if late(m, 1):
                        e.wait_ge(c["y_made"], m)
                    e.activation(v_h, banks[V_B][:].rearrange("p (a b) -> p a b", a=CHUNKS),
                                 ACT.Copy).then_inc(c["v_hi"], 1)

                def scores_high(m):
                    for i, (at, w, blocks) in enumerate(S_PIECES):
                        e.wait_ge(c["s_scaled"], m * 4 + (1, 2, 4)[i])
                        if i == 0 and late(m, 1):
                            e.wait_ge(c["y_made"], m)
                        e.activation(s_h[:, at:at + w], s_f[:, at:at + w], ACT.Copy).then_inc(c["s_hi"], 1)

                def squares(m):
                    e.wait_ge(c["y_made"], m + 1)
                    if late(m, 1):
                        e.wait_ge(c["sq_done"], m)
                    e.activation(square, banks[Y_B][:], ACT.Square).then_inc(c["squared"], 1)

                def out_high(m, p):
                    e.wait_ge(c["y_done"], m + 1)
                    if late(m, 2):
                        e.wait_ge(c["o_made"], (m - 1) * 4)
                    e.activation(y_h[:, p, :], y_f, ACT.Copy).then_inc(c["y_hi"], 1)

                def step(h, b, n, units, attend, first, last):
                    m = n - 1
                    if attend:
                        values_high(m)
                    if units:
                        unit("k", n, b)
                        if b == 0 and not first:
                            prep("g", h)
                    if attend:
                        scores_high(m)
                    if units:
                        unit("q", n, b)
                        if b == 1 and not last:
                            prep("k", h + 1)
                        unit("v", n, b)
                        if b == 1 and not last:
                            prep("q", h + 1)
                    if attend:
                        squares(m)
                        out_high(m, 1 - b)
                    if units:
                        if b == 1 and not last:
                            prep("v", h + 1)
                        unit("g", n, b)
                        if b == 1:
                            prep("o", h)

                def body(h, first, last):
                    step(h, 0, h * 2, True, not first, first, last)
                    step(h, 1, h * 2 + 1, True, True, first, last)

                second_half2(e, "scalar")
                heads(e, body)
                step(HEADS, 0, STEPS, False, True, False, True)
                e.wait_ge(c["rms_made"], 1)
                e.activation(rms, banks[U][:, 0:2 * TILES:2], ACT.Sqrt, bias=eps[:],
                             scale=1.0 / (HEADS * P)).then_inc(c["rms_sqrt"], 1)

            def add_output(e, o, p, i, bank):
                e.wait_ge(c["o_made"], o * 4 + i + 1)
                t = p * 4 + i
                e.tensor_tensor(proj[:, t, :], proj[:, t, :], banks[bank][:], ALU.add).then_inc(c["o_added"], 1)

            def c_vector(e):
                def low(k, n, b):
                    i = "kq".index(k)
                    hi = {"k": k_h, "q": q_h}[k][:, b, :]
                    lo = {"k": k_l, "q": q_l}[k][:, b, :]
                    e.wait_ge(c["part_hi"], n * 2 + i + 1)
                    e.tensor_tensor(lo, whole[k], hi.bitcast(F32), ALU.subtract).then_inc(c["part_ready"], 1)

                def values_low(m):
                    e.wait_ge(c["v_hi"], m + 1)
                    e.tensor_tensor(v_l, banks[V_B][:].rearrange("p (a b) -> p a b", a=CHUNKS), v_h.bitcast(F32),
                                    ALU.subtract).then_inc(c["v_ready"], 1)

                def scores_scaled(m):
                    for i, (at, w, blocks) in enumerate(S_PIECES):
                        e.wait_ge(c["s_made"], m * 3 + i + 1)
                        if i == 0 and late(m, 1):
                            e.wait_ge(c["s_ready"], m * 3)
                        for j, col in blocks:
                            n = SEQ - j * P
                            e.tensor_tensor(s_f[:, at + col:at + col + n], banks[S_B + i][:, col:col + n],
                                            dec[:, 0:n], ALU.mult).then_inc(c["s_scaled"], 1)

                def scores_low(m):
                    for i, (at, w, blocks) in enumerate(S_PIECES):
                        e.wait_ge(c["s_hi"], m * 3 + i + 1)
                        e.tensor_tensor(s_l[:, at:at + w], s_f[:, at:at + w], s_h[:, at:at + w].bitcast(F32),
                                        ALU.subtract).then_inc(c["s_ready"], 1)

                def outputs(m, p):
                    e.wait_ge(c["squared"], m + 1)
                    e.wait_ge(c["unit_out"], m * 4 + 4)
                    e.scalar_tensor_tensor(out=y_f, in0=banks[Y_B][:], scalar=weight, in1=gate_f[:, p, :],
                                           op0=ALU.mult, op1=ALU.mult).then_inc(c["y_done"], 1)
                    e.wait_ge(c["y_hi"], m + 1)
                    e.tensor_tensor(y_l[:, p, :], y_f, y_h[:, p, :].bitcast(F32),
                                    ALU.subtract).then_inc(c["y_ready"], 1)

                def add(o, p, i):
                    add_output(e, o, p, i, O_B)

                def step(h, b, n, units, attend, project):
                    m, o = n - 1, n - 2
                    if attend:
                        values_low(m)
                    if units:
                        low("k", n, b)
                    if project:
                        add(o, b, 0)
                    if attend:
                        e.wait_ge(c["dec_ready"], h + b)
                        scores_scaled(m)
                    if attend:
                        scores_low(m)
                    if project:
                        add(o, b, 1)
                    if units:
                        low("q", n, b)
                    if project:
                        add(o, b, 2)
                    if attend:
                        outputs(m, 1 - b)
                    if project:
                        add(o, b, 3)

                def body(h, first, last):
                    step(h, 0, h * 2, True, not first, not first)
                    step(h, 1, h * 2 + 1, True, True, not first)

                e.wait_ge(x2_ready, 1)
                e.wait_ge(c["zeroed"], 1)
                second_half2(e, "vector")
                heads(e, body)
                step(HEADS, 0, STEPS, False, True, True)
                e.wait_ge(c["rms_sqrt"], 1)
                e.reciprocal(rms_inv, rms).then_inc(c["rms_ready"], 1)
                e.wait_ge(c["rms_ready"], 1)

            def add_projection(e, t):
                if t >= CHUNKS:
                    add_output(e, STEPS - 1, 1, t - CHUNKS, LAST_O[t - CHUNKS])
                e.wait_ge(c["o_added"], (STEPS - 1) * 4 + max(t - CHUNKS + 1, 0))
                e.scalar_tensor_tensor(out=acc[:, t, :], in0=proj[:, t, :], scalar=rms_inv[:, t:t + 1],
                                       in1=acc[:, t, :], op0=ALU.mult, op1=ALU.add).then_inc(c["rms_used"], 1)

            def c_gpsimd(e):
                def low(k, h):
                    e.wait_ge(c_hi_done[k], h + 1)
                    e.tensor_tensor(c_lo[k], c_stage[k], c_hi[k].bitcast(F32), ALU.subtract).then_inc(c_ready[k], 1)

                def decays(h):
                    e.wait_ge(c["dec_loaded"], (h + 1) * 32)
                    if late(h, 1):
                        e.wait_ge(c["y_done"], h * 2)
                    e.tensor_tensor(dec[:, 0:SEQ + 1], dec_stage[:, 0:SEQ + 1], ones[:, 0:1].to_broadcast([P, SEQ + 1]),
                                    ALU.mult).then_inc(c["dec_ready"], 1)

                def square_sum(m, p):
                    e.wait_ge(c["squared"], m + 1)
                    e.tensor_tensor(sum_sq[:, p, :], sum_sq[:, p, :], square, ALU.add).then_inc(c["sq_done"], 1)

                def body(h, first, last):
                    if not first:
                        low("g", h)
                        square_sum(h * 2 - 1, 1)
                    decays(h)
                    if not last:
                        low("k", h + 1)
                        low("q", h + 1)
                    square_sum(h * 2, 0)
                    if not last:
                        low("v", h + 1)
                    low("o", h)

                arena_left(e)
                e.memset(proj, 0.0)
                e.memset(sum_sq, 0.0)
                e.memset(ones, 1.0).then_inc(c["zeroed"], 1)
                e.wait_ge(c["zeroed"], 1)
                for k in "kqvg":
                    low(k, 0)
                heads(e, body)
                square_sum(STEPS - 1, 1)

            engines["sync"].append(c_sync)
            engines["scalar"].append(c_scalar)
            engines["vector"].append(c_vector)
            engines["tensor"].append(c_tensor)
            engines["gpsimd"].append(c_gpsimd)
            x3_ready, second_half3 = norm_stage(3, add_projection, lambda e, i: e.wait_ge(c["rms_used"], i + 1), True,
                                                "D" in phases, turn_bank=4, split_turns=True,
                                                store=out if "D" not in phases else None)

        if "D" in phases:
            finish, finished, _ = mlp("int", x3_ready, second_half3,
                                   lambda e: e.wait_ge(c["o_made"], STEPS * 4), False)
            norm_stage(4, finish, finished, True, False, store=out)

        @block.sync
        def _(e):
            for f in engines["sync"]:
                f(e)

        @block.gpsimd
        def _(e):
            for f in engines["gpsimd"]:
                f(e)

        @block.scalar
        def _(e):
            for f in engines["scalar"]:
                f(e)

        @block.vector
        def _(e):
            for f in engines["vector"]:
                f(e)

        @block.tensor
        def _(e):
            for f in engines["tensor"]:
                f(e)


def host_arrays(inputs):
    import numpy as np
    a = {k.split("_", 2)[2] if "ffn" not in k else k.replace("_ffn_", "_"): np.asarray(v) for k, v in inputs.items()}
    pad = FT * P - FF

    def tiles_of_rows(i):
        return np.pad(i, ((0, pad), (0, 0))).reshape(FT, P, D // CODE)

    down = np.pad(a["L0_idx_down"], ((0, 0), (0, pad // CODE))).reshape(KB, P, FT, P // CODE)
    idx = np.stack([tiles_of_rows(a["L0_idx_gate"]), tiles_of_rows(a["L0_idx_up"]),
                    down.transpose(2, 1, 0, 3).reshape(FT, P, KB * P // CODE)], 1)
    slope = (np.float32(1.0 / 2.0 ** (8.0 / HEADS)) ** (np.arange(HEADS, dtype=np.float32) + 1)
             * np.float32(1.0 - 1 / (31 + 1e-05) + 1e-05)).astype(np.float64)
    gap = np.arange(SEQ, dtype=np.float64)[None, :] - np.arange(P, dtype=np.float64)[:, None]
    decay = np.where(gap >= 0, np.exp(-slope[:, None, None] * np.maximum(gap, 0)), 0).astype(np.float32)
    return {
        "x": a["hidden_states"].reshape(TOK, D), "w_q": a["w_q"], "w_k": a["w_k"], "w_v": a["w_v"],
        "w_o": a["w_o"], "codebook": a["L0_codebook"], "idx": np.ascontiguousarray(idx),
        "qkv_w": np.ascontiguousarray(a["qkv_w"].T), "out_w": np.ascontiguousarray(a["out_w"].T),
        "gate_w": np.ascontiguousarray(a["gate_w"].T), "norm_w": a["norm_w"].reshape(HEADS, P, 1),
        "decay": decay,
        "wf_gate": np.ascontiguousarray(a["L1_w_gate"].T), "wf_up": np.ascontiguousarray(a["L1_w_up"].T),
        "wf_down": np.ascontiguousarray(a["L1_w_down"].T),
        "scales": np.stack([a["L1_scale_gate"], a["L1_scale_up"], a["L1_scale_down"]]).reshape(1, 3),
    }


_INS = ["x", "w_q", "w_k", "w_v", "w_o", "codebook", "idx", "qkv_w", "out_w", "gate_w", "norm_w", "decay",
        "wf_gate", "wf_up", "wf_down", "scales"]


def kernel(**inputs):
    import numpy as _np
    import concourse.bacc as _bacc
    from concourse import mybir as _mybir
    from concourse.bass_utils import run_bass_kernel_spmd as _run

    nc = _bacc.Bacc("TRN2", target_bir_lowering=False, num_devices=1)
    laid = host_arrays(inputs)
    arrays, args = {}, []
    for name in _INS:
        a = _np.ascontiguousarray(laid[name])
        arrays[f"in_{name}_dram"] = a
        args.append(nc.dram_tensor(f"in_{name}_dram", a.shape, _mybir.dt.from_np(a.dtype), kind="ExternalInput").ap())
    out = nc.dram_tensor("out_0_dram", (TOK, D), F32, kind="ExternalOutput").ap()
    weights = nc.dram_tensor("coded_weights_dram", (2 * FT, P, D), F32, kind="Internal").ap()
    build(nc, *args, out, weights)
    r = _run(nc, [arrays], core_ids=[0])
    return r.results[0]["out_0_dram"].reshape(TOK // SEQ, SEQ, D)
```
